# Optimizing a Trainium2 kernel written in Bass

```python
import numpy as np
import jax
import jax.numpy as jnp

def _softmax(x, axis=-1):
    return jax.nn.softmax(x, axis=axis)

def _gelu(x):
    return jax.nn.gelu(x, approximate=True)

def _silu(x):
    return jax.nn.silu(x)

def _sigmoid(x):
    return jax.nn.sigmoid(x)

def _layernorm(x, axis=-1, eps=1e-05):
    m = jnp.mean(x, axis=axis, keepdims=True)
    v = jnp.var(x, axis=axis, keepdims=True)
    return (x - m) / jnp.sqrt(v + eps)

def _scatter_add(tgt, idx, src, axis=0):
    return tgt.at[idx].add(src)

def _segment_sum(src, seg, n):
    return jax.ops.segment_sum(src, seg, n)
kernel_name = 'mk_gnn_preln_d4_gnn_r16_9c8155'

def setup_inputs(seed: int=0):
    np.random.seed(seed)
    _w = jnp.asarray

    def _rec_inputs():
        import jax
        import jax.numpy as jnp
        _gk = jax.random.key(seed)
        x = -0.0005121 + 1.001 * jax.random.normal(jax.random.fold_in(_gk, 1), (3125, 64), jnp.float32)
        src = jax.random.randint(jax.random.fold_in(_gk, 2), (100000,), 0, 3125, jnp.int32)
        dst = jax.random.randint(jax.random.fold_in(_gk, 3), (100000,), 0, 3125, jnp.int32)
        _o = jnp.argsort(dst, stable=True)
        src = src[_o]
        dst = dst[_o]
        edge_attr_64 = -8.16379e-05 + 0.999858 * jax.random.normal(jax.random.fold_in(_gk, 12), (100000, 64), jnp.float32)
        return (x, src, dst, edge_attr_64)
    x, src, dst, edge_attr_64 = _rec_inputs()

    def _L0_gnn_setup():
        import jax, jax.numpy as jnp
        import numpy as np
        NEG_SLOPE = 0.2

        def _gat_forward(atom_features, edges, W, a, merge_kernel):
            N = atom_features.shape[0]
            U = W.shape[-1]
            src, dst = (edges[:, 0], edges[:, 1])
            h = jnp.einsum('nf,hfu->nhu', atom_features, W)
            a_src = a[:, :U, 0]
            a_dst = a[:, U:, 0]
            alpha_src = jnp.einsum('nhu,hu->nh', h, a_src)
            alpha_dst = jnp.einsum('nhu,hu->nh', h, a_dst)
            scores = jax.nn.leaky_relu(alpha_src[src] + alpha_dst[dst], NEG_SLOPE)
            att = jnp.exp(jnp.clip(scores, -2.0, 2.0))
            att_sum = jax.ops.segment_sum(att, src, num_segments=N)
            att_norm = att / att_sum[src]
            msgs = h[dst] * att_norm[:, :, None]
            out = jax.ops.segment_sum(msgs, src, num_segments=N)
            merged = out.reshape(N, -1)
            return jax.nn.leaky_relu(merged @ merge_kernel, NEG_SLOPE)
        key = jax.random.key(seed)
        ks = jax.random.split(key, 6)
        N, E, F, U, H = (3125, 50000, 64, 64, 8)
        atom_features = jax.random.normal(ks[0], (N, F), dtype=jnp.float32)
        src = jnp.sort(jax.random.randint(ks[1], (E,), 0, N, dtype=jnp.int32))
        dst = jax.random.randint(ks[2], (E,), 0, N, dtype=jnp.int32)
        edges = jnp.stack([src, dst], axis=1)
        W = jax.random.normal(ks[3], (H, F, U), dtype=jnp.float32) * 0.1
        a = jax.random.normal(ks[4], (H, 2 * U, 1), dtype=jnp.float32) * 0.1
        merge_kernel = jax.random.normal(ks[5], (H * U, U), dtype=jnp.float32) * 0.05
        return {'atom_features': atom_features, 'edges': edges, 'W': W, 'a': a, 'merge_kernel': merge_kernel}
    _L0_gnn_all = _L0_gnn_setup()
    _L0_gnn_in = {k: v for k, v in _L0_gnn_all.items() if k in ('W', 'a', 'merge_kernel')}
    del _L0_gnn_all

    def _L1_gnn_setup():
        import jax, jax.numpy as jnp
        import numpy as np
        N_NODES = 6250
        N_EDGES = 78125
        D_IN = 64
        D_HID = 64
        D_OUT = 64

        def sage_conv(x, edge_index, w_l, b_l, w_r):
            src, dst = (edge_index[0], edge_index[1])
            n = x.shape[0]
            msg_sum = jax.ops.segment_sum(x[src], dst, num_segments=n)
            deg = jax.ops.segment_sum(jnp.ones((src.shape[0],), x.dtype), dst, num_segments=n)
            mean = msg_sum / jnp.maximum(deg, 1.0)[:, None]
            return mean @ w_l + b_l + x @ w_r
        key = jax.random.key(seed)
        ks = jax.random.split(key, 8)
        x = jax.random.normal(ks[0], (N_NODES, D_IN), dtype=jnp.float32)
        edge_index = jax.random.randint(ks[1], (2, N_EDGES), 0, N_NODES, dtype=jnp.int64)
        s1 = 1.0 / np.sqrt(D_IN)
        s2 = 1.0 / np.sqrt(D_HID)
        w1_l = jax.random.uniform(ks[2], (D_IN, D_HID), jnp.float32, -s1, s1)
        w1_r = jax.random.uniform(ks[3], (D_IN, D_HID), jnp.float32, -s1, s1)
        b1 = jax.random.uniform(ks[4], (D_HID,), jnp.float32, -s1, s1)
        w2_l = jax.random.uniform(ks[5], (D_HID, D_OUT), jnp.float32, -s2, s2)
        w2_r = jax.random.uniform(ks[6], (D_HID, D_OUT), jnp.float32, -s2, s2)
        b2 = jax.random.uniform(ks[7], (D_OUT,), jnp.float32, -s2, s2)
        return {'x': x, 'edge_index': edge_index, 'w1_l': w1_l, 'b1': b1, 'w1_r': w1_r, 'w2_l': w2_l, 'b2': b2, 'w2_r': w2_r}
    _L1_gnn_all = _L1_gnn_setup()
    _L1_gnn_in = {k: v for k, v in _L1_gnn_all.items() if k in ('w1_l', 'b1', 'w1_r', 'w2_l', 'b2', 'w2_r')}
    del _L1_gnn_all

    def _L2_gnn_setup():
        import jax, jax.numpy as jnp
        import numpy as np
        N_NODES = 6250
        N_EDGES = 100000
        D_IN = 64
        D_OUT = 64
        key = jax.random.key(seed)
        k_h, k_e, k_src, k_dst, k_w = jax.random.split(key, 5)
        h = jax.random.normal(k_h, (N_NODES, D_IN), dtype=jnp.float32)
        e = jax.random.normal(k_e, (N_EDGES, D_IN), dtype=jnp.float32)
        src = jax.random.randint(k_src, (N_EDGES,), 0, N_NODES, dtype=jnp.int32)
        dst = jax.random.randint(k_dst, (N_EDGES,), 0, N_NODES, dtype=jnp.int32)
        W = jax.random.normal(k_w, (D_OUT, 2 * D_IN), dtype=jnp.float32) * (1.0 / np.sqrt(2 * D_IN))
        b = jnp.zeros((D_OUT,), dtype=jnp.float32)
        return {'h': h, 'e': e, 'src': src, 'dst': dst, 'W': W, 'b': b}
    _L2_gnn_all = _L2_gnn_setup()
    _L2_gnn_in = {k: v for k, v in _L2_gnn_all.items() if k in ('W', 'b')}
    del _L2_gnn_all

    def _L3_gnn_setup():
        import jax, jax.numpy as jnp
        import numpy as np
        N, E, D, H = (3125, 31250, 64, 8)
        LN_EPS = 1e-05
        SM_EPS = 1e-16
        SLOPE = 0.2

        def layer_norm(x, g, b):
            mu = jnp.mean(x, axis=-1, keepdims=True)
            var = jnp.mean((x - mu) ** 2, axis=-1, keepdims=True)
            return (x - mu) * jax.lax.rsqrt(var + LN_EPS) * g + b
        key = jax.random.key(seed)
        ks = jax.random.split(key, 12)
        glorot = lambda k, shape: jax.random.normal(k, shape, jnp.float32) * np.sqrt(2.0 / (shape[0] + shape[-1]))
        return {'x': jax.random.normal(ks[0], (N, D), jnp.float32), 'edge_index': jax.random.randint(ks[1], (2, E), 0, N, jnp.int64), 'W_att': glorot(ks[2], (D, H * D)), 'att_src': glorot(ks[3], (H, D)), 'att_dst': glorot(ks[4], (H, D)), 'bias_att': jnp.zeros((D,), jnp.float32), 'W1': glorot(ks[5], (D, 2 * D)), 'b1': jnp.zeros((2 * D,), jnp.float32), 'W2': glorot(ks[6], (2 * D, D)), 'b2': jnp.zeros((D,), jnp.float32), 'ln1_g': jnp.ones((D,), jnp.float32), 'ln1_b': jnp.zeros((D,), jnp.float32), 'ln2_g': jnp.ones((D,), jnp.float32), 'ln2_b': jnp.zeros((D,), jnp.float32)}
    _L3_gnn_all = _L3_gnn_setup()
    _L3_gnn_in = {k: v for k, v in _L3_gnn_all.items() if k in ('W_att', 'att_src', 'att_dst', 'bias_att', 'W1', 'b1', 'W2', 'b2', 'ln1_g', 'ln1_b', 'ln2_g', 'ln2_b')}
    del _L3_gnn_all
    return {'x': x, 'src': src, 'dst': dst, 'edge_attr_64': edge_attr_64, 'L0_gnn_W': _L0_gnn_in['W'], 'L0_gnn_a': _L0_gnn_in['a'], 'L0_gnn_merge_kernel': _L0_gnn_in['merge_kernel'], 'L1_gnn_w1_l': _L1_gnn_in['w1_l'], 'L1_gnn_b1': _L1_gnn_in['b1'], 'L1_gnn_w1_r': _L1_gnn_in['w1_r'], 'L1_gnn_w2_l': _L1_gnn_in['w2_l'], 'L1_gnn_b2': _L1_gnn_in['b2'], 'L1_gnn_w2_r': _L1_gnn_in['w2_r'], 'L2_gnn_W': _L2_gnn_in['W'], 'L2_gnn_b': _L2_gnn_in['b'], 'L3_gnn_W_att': _L3_gnn_in['W_att'], 'L3_gnn_att_src': _L3_gnn_in['att_src'], 'L3_gnn_att_dst': _L3_gnn_in['att_dst'], 'L3_gnn_bias_att': _L3_gnn_in['bias_att'], 'L3_gnn_W1': _L3_gnn_in['W1'], 'L3_gnn_b1': _L3_gnn_in['b1'], 'L3_gnn_W2': _L3_gnn_in['W2'], 'L3_gnn_b2': _L3_gnn_in['b2'], 'L3_gnn_ln1_g': _L3_gnn_in['ln1_g'], 'L3_gnn_ln1_b': _L3_gnn_in['ln1_b'], 'L3_gnn_ln2_g': _L3_gnn_in['ln2_g'], 'L3_gnn_ln2_b': _L3_gnn_in['ln2_b']}

def reference(x, src, dst, edge_attr_64, L0_gnn_W, L0_gnn_a, L0_gnn_merge_kernel, L1_gnn_w1_l, L1_gnn_b1, L1_gnn_w1_r, L1_gnn_w2_l, L1_gnn_b2, L1_gnn_w2_r, L2_gnn_W, L2_gnn_b, L3_gnn_W_att, L3_gnn_att_src, L3_gnn_att_dst, L3_gnn_bias_att, L3_gnn_W1, L3_gnn_b1, L3_gnn_W2, L3_gnn_b2, L3_gnn_ln1_g, L3_gnn_ln1_b, L3_gnn_ln2_g, L3_gnn_ln2_b):
    import jax
    import jax.numpy as jnp

    def _L0_gnn_ref(atom_features, edges, W, a, merge_kernel):
        import jax, jax.numpy as jnp
        import numpy as np
        NEG_SLOPE = 0.2

        def _gat_forward(atom_features, edges, W, a, merge_kernel):
            N = atom_features.shape[0]
            U = W.shape[-1]
            src, dst = (edges[:, 0], edges[:, 1])
            h = jnp.einsum('nf,hfu->nhu', atom_features, W)
            a_src = a[:, :U, 0]
            a_dst = a[:, U:, 0]
            alpha_src = jnp.einsum('nhu,hu->nh', h, a_src)
            alpha_dst = jnp.einsum('nhu,hu->nh', h, a_dst)
            scores = jax.nn.leaky_relu(alpha_src[src] + alpha_dst[dst], NEG_SLOPE)
            att = jnp.exp(jnp.clip(scores, -2.0, 2.0))
            att_sum = jax.ops.segment_sum(att, src, num_segments=N)
            att_norm = att / att_sum[src]
            msgs = h[dst] * att_norm[:, :, None]
            out = jax.ops.segment_sum(msgs, src, num_segments=N)
            merged = out.reshape(N, -1)
            return jax.nn.leaky_relu(merged @ merge_kernel, NEG_SLOPE)
        return _gat_forward(atom_features, edges, W, a, merge_kernel)

    def _L1_gnn_ref(x, edge_index, w1_l, b1, w1_r, w2_l, b2, w2_r):
        import jax, jax.numpy as jnp
        import numpy as np
        N_NODES = 6250
        N_EDGES = 78125
        D_IN = 64
        D_HID = 64
        D_OUT = 64

        def sage_conv(x, edge_index, w_l, b_l, w_r):
            src, dst = (edge_index[0], edge_index[1])
            n = x.shape[0]
            msg_sum = jax.ops.segment_sum(x[src], dst, num_segments=n)
            deg = jax.ops.segment_sum(jnp.ones((src.shape[0],), x.dtype), dst, num_segments=n)
            mean = msg_sum / jnp.maximum(deg, 1.0)[:, None]
            return mean @ w_l + b_l + x @ w_r
        h = jax.nn.relu(sage_conv(x, edge_index, w1_l, b1, w1_r))
        return sage_conv(h, edge_index, w2_l, b2, w2_r)

    def _L2_gnn_ref(h, e, src, dst, W, b):
        import jax, jax.numpy as jnp
        import numpy as np
        N_NODES = 6250
        N_EDGES = 100000
        D_IN = 64
        D_OUT = 64
        n_nodes = h.shape[0]
        msg = h[src] * e
        summed = jax.ops.segment_sum(msg, dst, num_segments=n_nodes)
        cnt = jax.ops.segment_sum(jnp.ones((msg.shape[0],), msg.dtype), dst, num_segments=n_nodes)
        h_N = summed / jnp.maximum(cnt, 1.0)[:, None]
        h_total = jnp.concatenate([h, h_N], axis=1)
        return h_total @ W.T + b

    def _L3_gnn_ref(x, edge_index, W_att, att_src, att_dst, bias_att, W1, b1, W2, b2, ln1_g, ln1_b, ln2_g, ln2_b):
        import jax, jax.numpy as jnp
        import numpy as np
        N, E, D, H = (3125, 31250, 64, 8)
        LN_EPS = 1e-05
        SM_EPS = 1e-16
        SLOPE = 0.2

        def layer_norm(x, g, b):
            mu = jnp.mean(x, axis=-1, keepdims=True)
            var = jnp.mean((x - mu) ** 2, axis=-1, keepdims=True)
            return (x - mu) * jax.lax.rsqrt(var + LN_EPS) * g + b
        n = x.shape[0]
        h = (x @ W_att).reshape(n, H, D)
        a_src = jnp.einsum('nhc,hc->nh', h, att_src)
        a_dst = jnp.einsum('nhc,hc->nh', h, att_dst)
        loops = jnp.arange(n, dtype=edge_index.dtype)
        src = jnp.concatenate([edge_index[0], loops])
        dst = jnp.concatenate([edge_index[1], loops])
        e = a_src[src] + a_dst[dst]
        e = jnp.where(e > 0, e, SLOPE * e)
        m = jax.ops.segment_max(e, dst, num_segments=n)
        e = jnp.exp(e - m[dst])
        s = jax.ops.segment_sum(e, dst, num_segments=n)
        alpha = e / (s[dst] + SM_EPS)
        msg = alpha[:, :, None] * h[src]
        out = jax.ops.segment_sum(msg, dst, num_segments=n)
        att_out = out.mean(axis=1) + bias_att
        x1 = layer_norm(att_out + x, ln1_g, ln1_b)
        ff = jax.nn.relu(x1 @ W1 + b1) @ W2 + b2
        return layer_norm(ff + x1, ln2_g, ln2_b)
    edge_index = jnp.stack([src, dst])
    edge_index_t = jnp.stack([src, dst], axis=1)
    h = jnp.maximum(_layernorm(x, axis=-1), 0.0)
    x = x + _L0_gnn_ref(h, edge_index_t, L0_gnn_W, L0_gnn_a, L0_gnn_merge_kernel)
    h = jnp.maximum(_layernorm(x, axis=-1), 0.0)
    x = x + _L1_gnn_ref(h, edge_index, L1_gnn_w1_l, L1_gnn_b1, L1_gnn_w1_r, L1_gnn_w2_l, L1_gnn_b2, L1_gnn_w2_r)
    h = jnp.maximum(_layernorm(x, axis=-1), 0.0)
    x = x + _L2_gnn_ref(h, edge_attr_64, src, dst, L2_gnn_W, L2_gnn_b)
    h = jnp.maximum(_layernorm(x, axis=-1), 0.0)
    x = x + _L3_gnn_ref(h, edge_index, L3_gnn_W_att, L3_gnn_att_src, L3_gnn_att_dst, L3_gnn_bias_att, L3_gnn_W1, L3_gnn_b1, L3_gnn_W2, L3_gnn_b2, L3_gnn_ln1_g, L3_gnn_ln1_b, L3_gnn_ln2_g, L3_gnn_ln2_b)
    return x

_drawn_inputs = setup_inputs


def setup_inputs(seed=0):
    import zlib

    import numpy as np

    out = dict(_drawn_inputs(seed))
    spreads = {'L2_gnn_b': (0.0, 0.1),
     'L3_gnn_bias_att': (0.0, 0.1),
     'L3_gnn_b1': (0.0, 0.1),
     'L3_gnn_b2': (0.0, 0.1),
     'L3_gnn_ln1_g': (1.0, 0.2),
     'L3_gnn_ln1_b': (0.0, 0.1),
     'L3_gnn_ln2_g': (1.0, 0.2),
     'L3_gnn_ln2_b': (0.0, 0.1)}
    factors = {'L3_gnn_att_src': 8.0, 'L3_gnn_att_dst': 8.0}
    for name, (base, spread) in spreads.items():
        noise = np.random.default_rng([zlib.crc32(name.encode()), seed]).standard_normal(out[name].shape)
        drawn = base * np.exp(spread * noise) if base else spread * noise
        out[name] = jnp.asarray(drawn.astype(out[name].dtype))
    for name, factor in factors.items():
        out[name] = (out[name] * factor).astype(out[name].dtype)
    return out
```

```python
from contextlib import ExitStack

import concourse.bass as bass
from concourse import mybir

F32 = mybir.dt.float32
BF16 = mybir.dt.bfloat16
I32 = mybir.dt.int32
ALU = mybir.AluOpType
ACT = mybir.ActivationFunctionType
AX = mybir.AxisListType

N, E, F, H = 3125, 100000, 64, 8
P = 125
W = N // P
T = 4
G = E // (P * T)
K = G + W - 1
Q = K // 4
HF = H * F
R = F + H
C = E // P
FAR = 1.0e30


class Own:

    def __init__(self, eng, sem):
        self.eng, self.sem, self.n = eng, sem, 0

    def __call__(self, instruction):
        self.n += 1
        instruction.then_inc(self.sem, 1)
        self.eng.wait_ge(self.sem, self.n)


def rounds(eng, step):
    for j in range(4):
        step(0, j)
    with eng.Fori(1, Q - 1, 1) as q:
        for j in range(4):
            step(q, j)
    for j in range(4):
        step(Q - 1, j)


def opening(q):
    return isinstance(q, int) and q == 0


def after(q, j):
    if isinstance(q, int) and q == Q - 1 and j == 3:
        return None
    return (q, j + 1) if j < 3 else (q + 1, 0)


def before(q, j):
    if opening(q) and j == 0:
        return None
    return (q, j - 1) if j else (q - 1, 3)


def over(ap, shape):
    return ap.to_broadcast(list(shape))


class Scope:

    def __init__(self, nc, stack, tag):
        self.nc, self.stack, self.tag = nc, stack, tag

    def sb(self, name, shape, dt=F32):
        return self.stack.enter_context(self.nc.sbuf_tensor(f"{self.tag}_{name}", shape, dt))

    def ps(self, name, shape=(128, 512)):
        return self.stack.enter_context(self.nc.psum_tensor(f"{self.tag}_{name}", list(shape), F32))

    def sem(self, name):
        return self.stack.enter_context(self.nc.semaphore(f"{self.tag}_{name}"))

    def sems(self, name, n):
        return [self.sem(f"{name}{i}") for i in range(n)]


class StepSems:

    NAMES = ("rel_ready", "hot_ready", "turned", "turned_copied", "near_ready", "z_ready", "leaky_ready", "less_max",
             "score_ready", "att_ready", "msg_ready", "sums_ready", "acc_ready", "zeroed", "gather_go", "load_go")

    def __init__(self, nc, stack):
        self.nc, self.base, self.used = nc, 0, False
        self.gathered = [stack.enter_context(nc.semaphore(f"step_gathered{i}")) for i in range(4)]
        self.keys_in = [stack.enter_context(nc.semaphore(f"step_keys_in{i}")) for i in range(4)]
        self.streamed = [stack.enter_context(nc.semaphore(f"step_streamed{i}")) for i in range(4)]
        self.by_name = {n: stack.enter_context(nc.semaphore(f"step_{n}")) for n in self.NAMES}

    def begin(self, gathers):
        if self.used:
            numbers = sorted(s.num for s in (*self.keys_in, *self.streamed, *self.by_name.values()))
            assert numbers == list(range(numbers[0], numbers[-1] + 1))
            self.nc.all_engine_barrier(sems_to_clear=range(numbers[0], numbers[-1] + 1))
        self.used = True
        base = self.base
        if gathers:
            self.base += 16 * T * Q
        return base



def norm_scratch(s):
    s.mean, s.var, s.root = s.sb("mean", [P, W]), s.sb("var", [P, W]), s.sb("root", [P, W])
    s.cen, s.sq = s.sb("cen", [P, W, F]), s.sb("sq", [P, W, F])
    s.var_ready, s.root_ready, s.norms = s.sem("var_ready"), s.sem("root_ready"), 0


def layer_norm(nc, own, s, x, y, relu=True):
    v = nc.vector
    own(v.tensor_reduce(s.mean[:, :], x, AX.X, ALU.add))
    own(v.tensor_scalar(s.mean[:, :], s.mean[:, :], 1.0 / F, None, ALU.mult))
    own(v.tensor_tensor(s.cen[:, :, :], x, over(s.mean[:, :].unsqueeze(2), (P, W, F)), ALU.subtract))
    own(v.tensor_tensor(s.sq[:, :, :], s.cen[:, :, :], s.cen[:, :, :], ALU.mult))
    own(v.tensor_reduce(s.var[:, :], s.sq[:, :, :], AX.X, ALU.add))
    v.tensor_scalar(s.var[:, :], s.var[:, :], 1.0 / F, 1e-5, ALU.mult, ALU.add).then_inc(s.var_ready, 1)
    s.norms += 1
    own.eng.wait_ge(s.root_ready, s.norms)
    own(v.reciprocal(s.root[:, :], s.root[:, :]))
    own(v.tensor_tensor(s.mean[:, :], s.root[:, :], s.root[:, :], ALU.mult))
    own(v.tensor_tensor(s.var[:, :], s.var[:, :], s.mean[:, :], ALU.mult))
    own(v.tensor_scalar(s.var[:, :], s.var[:, :], -0.5, 1.5, ALU.mult, ALU.add))
    own(v.tensor_tensor(s.var[:, :], s.var[:, :], s.root[:, :], ALU.mult))
    own(v.tensor_tensor(y, s.cen[:, :, :], over(s.var[:, :].unsqueeze(2), (P, W, F)), ALU.mult))
    if relu:
        own(v.tensor_scalar(y, y, 0.0, None, ALU.max))


def norm_root(nc, act, s, n):
    act.wait_ge(s.var_ready, n)
    nc.scalar.activation(s.root[:, :], s.var[:, :], ACT.Sqrt).then_inc(s.root_ready, 1)


def split3(nc, own, s, x, parts):
    v = nc.vector
    own(v.tensor_copy(parts[0], x))
    own(v.tensor_tensor(s.rest, x, parts[0], ALU.subtract))
    own(v.tensor_copy(parts[1], s.rest))
    own(v.tensor_tensor(s.rest, s.rest, parts[1], ALU.subtract))
    own(v.tensor_copy(parts[2], s.rest))



def set_up(nc, m, io):
    with ExitStack() as stack:
        s = Scope(nc, stack, "setup")
        loaded, made, iota_made = s.sem("loaded"), s.sem("made"), s.sem("iota_made")
        ints = s.sb("ints", [P, P], I32)
        step_ints = s.sb("step_ints", [128, K], I32)
        group_ints = s.sb("group_ints", [100, 2], I32)
        block = stack.enter_context(nc.Block())

        @block.sync
        def _(sp):
            loads = [
                (m.x[:, :, :], io["x"].rearrange("(w p) f -> p w f", p=P)),
                (m.src_run[:, :], io["src"].rearrange("(p c) -> p c", p=P)),
                (m.dst_run[:, :], io["dst"].rearrange("(p c) -> p c", p=P)),
                (m.last_key[:, :], io["dst"].rearrange("(j p e) -> p j e", p=100, e=P * T)[:, :, P * T - 1]),
                (m.wt0[:, :], io["wt0"]), (m.at0[:, :], io["at0"]), (m.merge[:, :, :], io["merge"]),
                (m.wt3[:, :], io["wt3"]), (m.at3[:, :], io["at3"]), (m.value3[:, :, :], io["value3"]),
                (m.sage1[:, :], io["sage1"]), (m.sage2[:, :], io["sage2"]), (m.edge_w[:, :], io["edge_w"]),
                (m.ff1[:, :], io["ff1"]), (m.ff1_b[:, :], io["ff1_b"]), (m.ff2[:, :], io["ff2"]),
                (m.rows[:, :], io["rows"].rearrange("a n -> (a n)").partition_broadcast(P)),
            ]
            for out, in_ in loads:
                sp.dma_start(out, in_, allow_slow_non_contiguous=in_.shape[0] == 100).then_inc(loaded, 16)
            sp.wait_ge(loaded, 16 * len(loads))

        @block.gpsimd
        def _(pool):
            own = Own(pool, made)
            g = nc.gpsimd
            own(g.memset(m.ident[:, :], 0.0))
            own(g.affine_select(out=m.ident[:, :], in_=m.ident[:, :], compare_op=ALU.not_equal, fill=1.0,
                                base=0, pattern=[[-1, 128]], channel_multiplier=1))
            own(g.memset(m.ones[:, :], 1.0))
            own(g.affine_select(out=m.upto[:, :], in_=m.ones[:, :], compare_op=ALU.is_ge, fill=0.0,
                                base=0, pattern=[[1, 128]], channel_multiplier=-1))
            own(g.iota(ints[:, :], pattern=[[1, P]], base=0, channel_multiplier=0))
            own(g.iota(step_ints[:, :], pattern=[[1, K]], base=0, channel_multiplier=0))
            g.iota(group_ints[:, :], pattern=[[100, 2]], base=0, channel_multiplier=1).then_inc(iota_made, 1)

        @block.vector
        def _(dve):
            dve.wait_ge(iota_made, 1)
            nc.vector.tensor_copy(m.node_iota[:, :], ints[:, :])
            nc.vector.tensor_copy(m.step_iota[:, :], step_ints[:, :])
            nc.vector.tensor_copy(m.group_iota[:, :], group_ints[:, :])
            nc.vector.tensor_scalar(m.edge_iota[:, :], group_ints[:, :], float(P * T), float(P * T - 1), ALU.mult, ALU.add)


def plan_steps(nc, own, s, m):
    v = nc.vector
    own(v.tensor_tensor(s.finish[:, :], s.last_window[:, :], m.group_iota[:, :], ALU.add))
    for j in range(2):
        own(v.tensor_scalar(s.done[:, j, :], m.step_iota[0:100, :], s.finish[:, j:j + 1], None, ALU.is_gt))


def order_edges(nc, m):
    with ExitStack() as stack:
        s = Scope(nc, stack, "order")
        s.finish = s.sb("finish", [100, 2])
        s.done = s.sb("done", [100, 2, K])
        s.last_window = s.sb("last_window", [100, 2])
        flags = s.sb("flags", [100, 2, W - 1])
        bounds = s.sb("bounds", [128, W - 1])
        key = s.sb("key", [P, C])
        win = s.sb("win", [P, C])
        mask = s.sb("mask", [P, C])
        one = s.sb("one", [P, C])
        count = s.sb("count", [P, W, C])
        place = s.sb("place", [P, C])
        totals = s.sb("totals", [P, W])
        base = s.sb("base", [128, W])
        cum = s.sb("cum", [128, W])
        own_sem, to_pe, from_pe = s.sem("dve_step"), s.sem("operands_ready"), s.sem("sums_ready")
        ps = s.ps("sums")
        ps2 = s.ps("before")
        block = stack.enter_context(nc.Block())

        def finish_steps(dve, own, table, n):
            v = nc.vector
            dve.wait_ge(from_pe, n)
            own(v.tensor_copy(table.group_f[:, :], ps[:, 0:K]))
            own(v.tensor_tensor(table.window_f[:, :], m.step_iota[:, :], table.group_f[:, :], ALU.subtract))
            own(v.tensor_scalar(table.first_node[:, :], table.window_f[:, :], float(P), None, ALU.mult))
            own(v.tensor_copy(table.group[:, :], table.group_f[0:1, :]))
            own(v.tensor_copy(table.window[:, :], table.window_f[0:1, :]))

        @block.vector
        def _(dve):
            own = Own(dve, own_sem)
            v = nc.vector
            own(v.tensor_scalar(bounds[:, :], m.step_iota[:, 1:W], float(P), None, ALU.mult))
            own(v.tensor_copy(s.finish[:, :], m.last_key[:, :]))
            own(v.tensor_tensor(flags[:, :, :], over(s.finish[:, :].unsqueeze(2), (100, 2, W - 1)),
                                over(bounds[0:100, :].unsqueeze(1), (100, 2, W - 1)), ALU.is_ge))
            own(v.tensor_reduce(s.last_window[:, :], flags[:, :, :], AX.X, ALU.add))
            plan_steps(nc, own, s, m)
            v.memset(one[:, :], 1.0).then_inc(to_pe, 1)
            finish_steps(dve, own, m.by_dst, 1)

            own(v.tensor_copy(key[:, :], m.src_run[:, :]))
            own(v.tensor_scalar(win[:, :], key[:, :], float(P), None, ALU.is_ge))
            for w in range(2, W):
                own(v.scalar_tensor_tensor(win[:, :], key[:, :], float(w * P), win[:, :], ALU.is_ge, ALU.add))
            for w in range(W):
                own(v.tensor_scalar(mask[:, :], win[:, :], float(w), None, ALU.is_equal))
                own(v.tensor_tensor_scan(count[:, w, :], one[:, :], mask[:, :], 0.0, ALU.mult, ALU.add))
            v.tensor_copy(totals[:, :], count[:, :, C - 1]).then_inc(to_pe, 1)
            dve.wait_ge(from_pe, 2)
            own(v.tensor_tensor_scan(cum[0:P, :], one[:, 0:W], ps[0:P, 0:W], 0.0, ALU.mult, ALU.add))
            own(v.tensor_tensor(base[0:P, :], cum[0:P, :], ps[0:P, 0:W], ALU.subtract))
            own(v.tensor_tensor(base[0:P, :], base[0:P, :], ps2[0:P, 0:W], ALU.add))
            own(v.tensor_tensor(base[0:P, :], base[0:P, :], totals[:, :], ALU.subtract))
            own(v.memset(place[:, :], -1.0))
            for w in range(W):
                own(v.tensor_scalar(count[:, w, :], count[:, w, :], base[0:P, w:w + 1], None, ALU.add))
                own(v.scalar_tensor_tensor(mask[:, :], win[:, :], float(w), count[:, w, :],
                                           ALU.is_equal, ALU.mult))
                own(v.tensor_tensor(place[:, :], place[:, :], mask[:, :], ALU.add))
            own(v.tensor_copy(m.place[:, :], place[:, :]))
            own(v.tensor_copy(m.record[:, :, 0], m.src_run[:, :]))
            own(v.tensor_copy(m.record[:, :, 1], m.dst_run[:, :]))
            own(v.tensor_tensor(flags[:, :, :], over(m.edge_iota[:, :].unsqueeze(2), (100, 2, W - 1)),
                                over(cum[0:100, 0:W - 1].unsqueeze(1), (100, 2, W - 1)), ALU.is_ge))
            own(v.tensor_reduce(s.last_window[:, :], flags[:, :, :], AX.X, ALU.add))
            plan_steps(nc, own, s, m)
            v.memset(one[:, :], 1.0).then_inc(to_pe, 1)
            finish_steps(dve, own, m.by_src, 3)

        @block.tensor
        def _(pe):
            def add_up(n):
                pe.wait_ge(to_pe, n)
                nc.tensor.matmul(ps[:, 0:K], m.ones[0:100, :], s.done[:, 0, :], start=True, stop=False)
                nc.tensor.matmul(ps[:, 0:K], m.ones[0:100, :], s.done[:, 1, :], start=False,
                                 stop=True).then_inc(from_pe, 1)
            add_up(1)
            pe.wait_ge(to_pe, 2)
            nc.tensor.matmul(ps[0:P, 0:W], m.ones[0:P, 0:P], totals[:, :], start=True, stop=True)
            nc.tensor.matmul(ps2[0:P, 0:W], m.upto[0:P, 0:P], totals[:, :], start=True,
                             stop=True).then_inc(from_pe, 1)
            add_up(3)


def scatter_and_tables(nc, m):
    with ExitStack() as stack:
        s = Scope(nc, stack, "l0tab")
        slot_place = [s.sb(f"place{i}", [P, 8], I32) for i in range(2)]
        slot_record = [s.sb(f"record{i}", [P, 8, 2], I32) for i in range(2)]
        staged, sent, go = s.sem("staged"), s.sems("sent", 2), s.sem("go")
        tables = Tables(nc, s, m)
        block = stack.enter_context(nc.Block())

        @block.gpsimd
        def _(pool):
            def half(i, b):
                if not (isinstance(i, int) and i == 0):
                    pool.wait_ge(sent[b], 128 * i)
                nc.gpsimd.tensor_copy(slot_place[b][:, :], m.place[:, bass.ds(16 * i + 8 * b, 8)])
                nc.gpsimd.tensor_copy(slot_record[b][:, :, :],
                                      m.record[:, bass.ds(16 * i + 8 * b, 8), :]).then_inc(staged, 1)
                pool.wait_ge(staged, 2 * i + b + 1)
                pool.sem_inc(go, 1)
                for t in range(8):
                    pool.indirect_dma_start(
                        m.records[:, :], bass.IndirectOffsetOnAxis(ap=slot_place[b][:, t:t + 1], axis=0),
                        slot_record[b][:, t, :], None).then_inc(sent[b], 16)
            half(0, 0)
            half(0, 1)
            with pool.Fori(1, C // 16, 1) as i:
                half(i, 0)
                half(i, 1)
            for b in range(2):
                pool.wait_ge(sent[b], 128 * (C // 16))

        tables.write(block, m.x, m.wt0, m.at0, table_score=1)


class Tables:

    def __init__(self, nc, s, m):
        self.nc, self.s, self.m = nc, s, m
        norm_scratch(s)
        self.vec = s.sb("vec", [F, 2 * H])
        self.rest = s.sb("rest", [P, W, H])
        s.rest = self.rest[:, :, :]
        self.ps_t = [s.ps(f"turned{i}") for i in range(2)]
        self.ps_v, self.ps_s = s.ps("vec_ps"), s.ps("score_ps")
        self.own_sem = s.sem("dve_step")
        self.h_ready, self.turned, self.copied = s.sem("h_ready"), s.sem("turned"), s.sem("copied")
        self.vec_ready, self.vec_copied = s.sem("vec_ready"), s.sem("vec_copied")
        self.scores_ready, self.rows_ready = s.sem("scores_ready"), s.sem("rows_ready")
        self.written = s.sem("written")
        self.graph_rows = s.sb("graph_rows", [P, W, R])

    def write(self, block, x, wt, at, table_score):
        nc, m, s = self.nc, self.m, self.s
        near = 1 - table_score

        @block.vector
        def _(dve):
            own = Own(dve, self.own_sem)
            v = nc.vector
            layer_norm(nc, own, s, x[:, :, :], m.h[:, :, :])
            v.tensor_copy(self.graph_rows[:, :, 0:F], m.h[:, :, :]).then_inc(self.h_ready, 1)
            dve.wait_ge(self.vec_ready, 1)
            v.tensor_copy(self.vec[:, :], self.ps_v[0:F, 0:2 * H]).then_inc(self.vec_copied, 1)
            dve.wait_ge(self.scores_ready, 1)
            both = self.ps_s[0:P, 0:W * 2 * H].rearrange("p (w a h) -> p w a h", a=2, h=H)
            own(v.tensor_copy(m.near[:, :, :], both[:, :, near, :]))
            own(v.tensor_copy(m.far[:, :, :], both[:, :, table_score, :]))
            v.tensor_copy(self.graph_rows[:, :, F:R], m.far[:, :, :]).then_inc(self.rows_ready, 1)
            split3(nc, own, s, m.near[:, :, :], [m.near_parts[:, :, i, 0:H] for i in range(3)])

        @block.tensor
        def _(pe):
            for a in range(2):
                for h in range(H):
                    c = a * H + h
                    last = nc.tensor.matmul(self.ps_v[0:F, c:c + 1], wt[:, h * F:(h + 1) * F],
                                            at[:, c:c + 1], start=True, stop=True)
            last.then_inc(self.vec_ready, 1)
            pe.wait_ge(self.h_ready, 1)
            for c in range((W + 3) // 4):
                if c >= 2:
                    pe.wait_ge(self.copied, c - 1)
                for w in range(4 * c, min(4 * c + 4, W)):
                    o = (w % 4) * P
                    last = nc.tensor.transpose(self.ps_t[c % 2][0:F, o:o + P], m.h[:, w, :], m.ident[0:P, 0:P])
                last.then_inc(self.turned, 1)
            pe.wait_ge(self.vec_copied, 1)
            pe.wait_ge(self.copied, (W + 3) // 4)
            for w in range(W):
                last = nc.tensor.matmul(self.ps_s[0:P, w * 2 * H:(w + 1) * 2 * H], m.h_turned[:, w * P:(w + 1) * P],
                                        self.vec[:, :], start=True, stop=True)
            last.then_inc(self.scores_ready, 1)

        @block.scalar
        def _(act):
            norm_root(nc, act, s, 1)
            for c in range((W + 3) // 4):
                act.wait_ge(self.turned, c + 1)
                n = P * (min(4 * c + 4, W) - 4 * c)
                nc.scalar.activation(m.h_turned[:, 4 * c * P:4 * c * P + n], self.ps_t[c % 2][0:F, 0:n],
                                     ACT.Copy).then_inc(self.copied, 1)

        @block.sync
        def _(sp):
            sp.wait_ge(self.rows_ready, 1)
            sp.dma_start(m.table[:, :].rearrange("(w p) c -> p w c", p=P),
                         self.graph_rows[:, :, :]).then_inc(self.written, 16)
            sp.wait_ge(self.written, 16)


def attend(nc, m, tag, steps, from_spill):
    near_cols = 2 * H if from_spill else H
    with ExitStack() as stack:
        s = Scope(nc, stack, tag)
        pairs = [s.sb(f"pairs{i}", [P, 2 * T], I32) for i in range(4)]
        rows = [s.sb(f"rows{i}", [P, T, R]) for i in range(4)]
        rel = [s.sb(f"rel{i}", [P, T]) for i in range(4)]
        hot = [s.sb(f"hot{i}", [P, T, P]) for i in range(4)]
        hot_turned = [s.sb(f"hot_turned{i}", [P, T * P], BF16) for i in range(2)]
        z = [s.sb(f"z{i}", [P, T, H]) for i in range(2)]
        score = [s.sb(f"score{i}", [P, T, H]) for i in range(2)]
        att = [s.sb(f"att{i}", [P, T, H]) for i in range(2)]
        msg = [s.sb(f"msg{i}", [P, T, H, F]) for i in range(2)]
        turn_ps = [s.ps(f"turn_ps{i}") for i in range(2)]
        near_ps = [s.ps(f"near_ps{i}") for i in range(2)]
        sum_ps = [s.ps(f"sum_ps{i}") for i in range(2)]
        base = m.sems.begin(gathers=not from_spill)
        keys_in, rows_in = m.sems.keys_in, m.sems.streamed if from_spill else m.sems.gathered
        (rel_ready, hot_ready, turned, turned_copied, near_ready, z_ready, leaky_ready, less_max, score_ready,
         att_ready, msg_ready, sums_ready, acc_ready, zeroed, gather_go, load_go) = (m.sems.by_name[n] for n in m.sems.NAMES)
        if from_spill:
            base = 0
        block = stack.enter_context(nc.Block())

        key_of = [(x[:, 0:T] if from_spill else x[:, 0:2 * T:2]) for x in pairs]
        rows_count = 16 if from_spill else 16 * T

        @block.sync
        def _(sp):
            def load(q, j):
                k = 4 * q + j
                g = sp.value_load(steps.group[0:1, bass.ds(k, 1)], min_val=0, max_val=G - 1)
                if not opening(q):
                    sp.wait_ge(hot_ready, k - 3)
                    sp.sem_inc(load_go, 1)
                    if from_spill:
                        sp.wait_ge(msg_ready, k - 3)
                    else:
                        sp.wait_ge(rows_in[j], base + 16 * T * q)
                    sp.sem_inc(load_go, 1)
                if from_spill:
                    sp.dma_start(pairs[j][:, 0:T],
                                 m.dst[bass.ds(g * (P * T), P * T)].rearrange("(p t) -> p t", t=T)).then_inc(keys_in[j], 16)
                    sp.dma_start(rows[j][:, :, :],
                                 m.spill[bass.ds(g * (P * T), P * T), :].rearrange("(p t) c -> p t c", t=T)
                                 ).then_inc(rows_in[j], 16)
                else:
                    sp.dma_start(pairs[j][:, :],
                                 m.records[bass.ds(g * (P * T), P * T), :].rearrange("(p t) c -> p (t c)", t=T)
                                 ).then_inc(keys_in[j], 16)
            rounds(sp, load)

        @block.gpsimd
        def _(pool):
            nc.gpsimd.memset(m.acc[:, :, :], 0.0).then_inc(zeroed, 1)
            if from_spill:
                return

            def gather(q, j):
                k = 4 * q + j
                pool.wait_ge(keys_in[j], 16 * (q + 1))
                if not opening(q):
                    pool.wait_ge(msg_ready, k - 3)
                pool.sem_inc(gather_go, 1)
                for t in range(T):
                    pool.indirect_dma_start(
                        rows[j][:, t, :], None, m.table[:, :],
                        bass.IndirectOffsetOnAxis(ap=pairs[j][:, 2 * t + 1:2 * t + 2], axis=0)).then_inc(rows_in[j], 16)
            rounds(pool, gather)

        @block.vector
        def _(dve):
            v = nc.vector

            def one_hot(q, j):
                k = 4 * q + j
                dve.wait_ge(keys_in[j], 16 * (q + 1))
                if not opening(q):
                    dve.wait_ge(sums_ready, k - 3)
                v.tensor_scalar(rel[j][:, :], key_of[j], steps.first_node[0:P, bass.ds(k, 1)], None,
                                ALU.subtract).then_inc(rel_ready, 1)
                dve.wait_ge(rel_ready, k + 1)
                v.tensor_tensor(hot[j][:, :, :], over(rel[j][:, :].unsqueeze(2), (P, T, P)),
                                over(m.node_iota[:, :].unsqueeze(1), (P, T, P)), ALU.is_equal).then_inc(hot_ready, 1)

            def scores(q, j):
                k, b = 4 * q + j, j % 2
                dve.wait_ge(near_ready, k + 1)
                dve.wait_ge(rows_in[j], base + rows_count * (q + 1))
                near = near_ps[b][0:P, 0:T * near_cols].rearrange("p (t c) -> p t c", t=T)
                v.tensor_tensor(z[b][:, :, :], near[:, :, 0:H], rows[j][:, :, F:R], ALU.add).then_inc(z_ready, 1)
                dve.wait_ge(z_ready, k + 1)
                v.scalar_tensor_tensor(z[b][:, :, :], z[b][:, :, :], 0.2, z[b][:, :, :], ALU.mult,
                                       ALU.max).then_inc(leaky_ready, 1)
                dve.wait_ge(leaky_ready, k + 1)
                if not (opening(q) and j < 2):
                    dve.wait_ge(att_ready, k - 1)
                if from_spill:
                    v.tensor_tensor(z[b][:, :, :], z[b][:, :, :], near[:, :, H:2 * H], ALU.subtract).then_inc(less_max, 1)
                    dve.wait_ge(less_max, k + 1)
                    v.tensor_scalar(score[b][:, :, :], z[b][:, :, :], 0.0, None, ALU.min).then_inc(score_ready, 1)
                else:
                    v.tensor_scalar(score[b][:, :, :], z[b][:, :, :], -2.0, 2.0, ALU.max, ALU.min).then_inc(score_ready, 1)

            def messages(q, j):
                k, b = 4 * q + j, j % 2
                dve.wait_ge(att_ready, k + 1)
                if not (opening(q) and j < 2):
                    dve.wait_ge(sums_ready, k - 1)
                v.tensor_tensor(msg[b][:, :, :, :], over(rows[j][:, :, 0:F].unsqueeze(2), (P, T, H, F)),
                                over(att[b][:, :, :].unsqueeze(3), (P, T, H, F)), ALU.mult).then_inc(msg_ready, 1)

            def accumulate(q, j):
                k, b = 4 * q + j, j % 2
                dve.wait_ge(sums_ready, k + 1)
                if not (opening(q) and j == 0):
                    dve.wait_ge(acc_ready, k)
                w = dve.value_load(steps.window[0:1, bass.ds(k, 1)], min_val=0, max_val=W - 1)
                v.tensor_tensor(m.acc[:, bass.ds(w, 1), HF:HF + H], m.acc[:, bass.ds(w, 1), HF:HF + H],
                                near_ps[b][0:P, 256:256 + H].unsqueeze(1), ALU.add)
                v.tensor_tensor(m.acc[:, bass.ds(w, 1), 0:HF], m.acc[:, bass.ds(w, 1), 0:HF],
                                sum_ps[b][0:P, 0:HF].unsqueeze(1), ALU.add).then_inc(acc_ready, 1)

            def step(q, j):
                if after(q, j):
                    one_hot(*after(q, j))
                messages(q, j)
                if after(q, j):
                    scores(*after(q, j))
                if before(q, j):
                    accumulate(*before(q, j))
            dve.wait_ge(zeroed, 1)
            one_hot(0, 0)
            scores(0, 0)
            rounds(dve, step)
            accumulate(Q - 1, 3)

        @block.tensor
        def _(pe):
            def turn(q, j):
                k, b = 4 * q + j, j % 2
                pe.wait_ge(hot_ready, k + 1)
                if not (opening(q) and j < 2):
                    pe.wait_ge(turned_copied, k - 1)
                for t in range(T):
                    last = nc.tensor.transpose(turn_ps[b][0:P, t * P:(t + 1) * P], hot[j][:, t, :], m.ident[0:P, 0:P])
                last.then_inc(turned, 1)

            def near(q, j):
                k, b = 4 * q + j, j % 2
                pe.wait_ge(turned_copied, k + 1)
                if not (opening(q) and j < 2):
                    pe.wait_ge(score_ready, k - 1)
                w = pe.value_load(steps.window[0:1, bass.ds(k, 1)], min_val=0, max_val=W - 1)
                for t in range(T):
                    for i in range(3):
                        last = nc.tensor.matmul(near_ps[b][0:P, t * near_cols:(t + 1) * near_cols],
                                                hot_turned[b][:, t * P:(t + 1) * P],
                                                m.near_parts[:, bass.ds(w, 1), i, 0:near_cols].rearrange("p a c -> p (a c)"),
                                                start=(i == 0), stop=(i == 2))
                last.then_inc(near_ready, 1)

            def sums(q, j):
                k, b = 4 * q + j, j % 2
                pe.wait_ge(msg_ready, k + 1)
                if not (opening(q) and j < 2):
                    pe.wait_ge(acc_ready, k - 1)
                for t in range(T):
                    nc.tensor.matmul(sum_ps[b][0:P, 0:HF], hot[j][:, t, :],
                                     msg[b][:, t, :, :].rearrange("p h f -> p (h f)"), start=(t == 0), stop=(t == T - 1))
                for t in range(T):
                    last = nc.tensor.matmul(near_ps[b][0:P, 256:256 + H], hot[j][:, t, :], att[b][:, t, :],
                                            start=(t == 0), stop=(t == T - 1))
                last.then_inc(sums_ready, 1)

            def step(q, j):
                if after(q, j):
                    turn(*after(q, j))
                    near(*after(q, j))
                sums(q, j)
            turn(0, 0)
            near(0, 0)
            rounds(pe, step)

        @block.scalar
        def _(act):
            def step(q, j):
                k, b = 4 * q + j, j % 2
                act.wait_ge(turned, k + 1)
                if not (opening(q) and j < 2):
                    act.wait_ge(near_ready, k - 1)
                nc.scalar.activation(hot_turned[b][:, :], turn_ps[b][0:P, 0:T * P], ACT.Copy).then_inc(turned_copied, 1)
                act.wait_ge(score_ready, k + 1)
                if not (opening(q) and j < 2):
                    act.wait_ge(sums_ready, k - 1)
                nc.scalar.activation(att[b][:, :, :], score[b][:, :, :], ACT.Exp).then_inc(att_ready, 1)
            rounds(act, step)


def gather_sum(nc, m, tag, cols, edge_attr=None):
    with ExitStack() as stack:
        s = Scope(nc, stack, tag)
        keys = [s.sb(f"keys{i}", [P, T], I32) for i in range(4)]
        sources = [s.sb(f"sources{i}", [P, T], I32) for i in range(4)]
        rows = [s.sb(f"rows{i}", [P, T, R]) for i in range(4)]
        rel = [s.sb(f"rel{i}", [P, T]) for i in range(4)]
        hot = [s.sb(f"hot{i}", [P, T, P]) for i in range(4)]
        attr = [s.sb(f"attr{i}", [P, T, F]) for i in range(4)] if edge_attr is not None else None
        msg = [s.sb(f"msg{i}", [P, T, F]) for i in range(4)] if edge_attr is not None else rows
        sum_ps = [s.ps(f"sum_ps{i}") for i in range(2)]
        base = m.sems.begin(gathers=True)
        keys_in, rows_in = m.sems.keys_in, m.sems.gathered
        rel_ready, hot_ready, msg_ready, sums_ready, acc_ready, zeroed, gather_go, load_go = (
            m.sems.by_name[n] for n in ("rel_ready", "hot_ready", "msg_ready", "sums_ready", "acc_ready", "zeroed",
                                        "gather_go", "load_go"))
        steps = m.by_dst
        loads = 48 if edge_attr is not None else 32
        block = stack.enter_context(nc.Block())

        @block.sync
        def _(sp):
            def load(q, j):
                k = 4 * q + j
                g = sp.value_load(steps.group[0:1, bass.ds(k, 1)], min_val=0, max_val=G - 1)
                if not opening(q):
                    sp.wait_ge(hot_ready, k - 3)
                    sp.sem_inc(load_go, 1)
                    sp.wait_ge(rows_in[j], base + 16 * T * q)
                    if edge_attr is not None:
                        sp.sem_inc(load_go, 1)
                        sp.wait_ge(msg_ready, k - 3)
                    sp.sem_inc(load_go, 1)
                here = bass.ds(g * (P * T), P * T)
                sp.dma_start(sources[j][:, :], m.src[here].rearrange("(p t) -> p t", t=T)).then_inc(keys_in[j], 16)
                sp.dma_start(keys[j][:, :], m.dst[here].rearrange("(p t) -> p t", t=T)).then_inc(keys_in[j], 16)
                if edge_attr is not None:
                    sp.dma_start(attr[j][:, :, :], edge_attr[here, :].rearrange("(p t) f -> p t f", t=T)
                                 ).then_inc(keys_in[j], 16)
            rounds(sp, load)

        @block.gpsimd
        def _(pool):
            nc.gpsimd.memset(m.acc[:, :, 0:cols], 0.0).then_inc(zeroed, 1)

            def gather(q, j):
                k = 4 * q + j
                pool.wait_ge(keys_in[j], loads * (q + 1))
                if not opening(q):
                    pool.wait_ge(sums_ready if edge_attr is None else msg_ready, k - 3)
                pool.sem_inc(gather_go, 1)
                for t in range(T):
                    pool.indirect_dma_start(rows[j][:, t, :], None, m.table[:, :],
                                            bass.IndirectOffsetOnAxis(ap=sources[j][:, t:t + 1], axis=0)
                                            ).then_inc(rows_in[j], 16)
            rounds(pool, gather)

        @block.vector
        def _(dve):
            v = nc.vector

            def accumulate(q, j):
                k, b = 4 * q + j, j % 2
                dve.wait_ge(sums_ready, k + 1)
                if not (opening(q) and j == 0):
                    dve.wait_ge(acc_ready, k)
                w = dve.value_load(steps.window[0:1, bass.ds(k, 1)], min_val=0, max_val=W - 1)
                v.tensor_tensor(m.acc[:, bass.ds(w, 1), 0:cols], m.acc[:, bass.ds(w, 1), 0:cols],
                                sum_ps[b][0:P, 0:cols].unsqueeze(1), ALU.add).then_inc(acc_ready, 1)

            def step(q, j):
                k = 4 * q + j
                dve.wait_ge(keys_in[j], loads * (q + 1))
                if not opening(q):
                    dve.wait_ge(sums_ready, k - 3)
                v.tensor_scalar(rel[j][:, :], keys[j][:, :], steps.first_node[0:P, bass.ds(k, 1)], None,
                                ALU.subtract).then_inc(rel_ready, 1)
                dve.wait_ge(rel_ready, k + 1)
                v.tensor_tensor(hot[j][:, :, :], over(rel[j][:, :].unsqueeze(2), (P, T, P)),
                                over(m.node_iota[:, :].unsqueeze(1), (P, T, P)), ALU.is_equal).then_inc(hot_ready, 1)
                if edge_attr is not None:
                    dve.wait_ge(rows_in[j], base + 16 * T * (q + 1))
                    v.tensor_tensor(msg[j][:, :, :], rows[j][:, :, 0:F], attr[j][:, :, :], ALU.mult).then_inc(msg_ready, 1)
                if before(q, j):
                    accumulate(*before(q, j))
            dve.wait_ge(zeroed, 1)
            rounds(dve, step)
            accumulate(Q - 1, 3)

        @block.tensor
        def _(pe):
            def step(q, j):
                k, b = 4 * q + j, j % 2
                pe.wait_ge(hot_ready, k + 1)
                if edge_attr is not None:
                    pe.wait_ge(msg_ready, k + 1)
                else:
                    pe.wait_ge(rows_in[j], base + 16 * T * (q + 1))
                if not (opening(q) and j < 2):
                    pe.wait_ge(acc_ready, k - 1)
                for t in range(T):
                    last = nc.tensor.matmul(sum_ps[b][0:P, 0:cols], hot[j][:, t, :], msg[j][:, t, 0:cols],
                                            start=(t == 0), stop=(t == T - 1))
                last.then_inc(sums_ready, 1)
            rounds(pe, step)


class Heads:

    def __init__(self, nc, s, m):
        self.nc, self.s, self.m = nc, s, m
        self.ps_t = [s.ps(f"heads_t{i}") for i in range(2)]
        self.ps_o = [s.ps(f"heads_o{i}") for i in range(4)]
        self.turned_sb = [s.sb(f"heads_sb{i}", [128, 4 * P]) for i in range(2)]
        self.acc_ready, self.turned = s.sem("heads_acc_ready"), s.sem("heads_turned")
        self.copied, self.out_ready = s.sem("heads_copied"), s.sem("heads_out")

    def pe(self, pe, value):
        nc, m = self.nc, self.m
        pe.wait_ge(self.acc_ready, 1)

        def turn(w):
            if w >= 2:
                pe.wait_ge(self.copied, w - 1)
            for c in range(4):
                last = nc.tensor.transpose(self.ps_t[w % 2][:, c * P:(c + 1) * P], m.acc[:, w, c * 128:(c + 1) * 128],
                                           m.ident[0:P, 0:P])
            last.then_inc(self.turned, 1)
        turn(0)
        for w in range(W):
            if w + 1 < W:
                turn(w + 1)
            pe.wait_ge(self.copied, w + 1)
            for c in range(4):
                last = nc.tensor.matmul(self.ps_o[w // 8][0:P, (w % 8) * F:(w % 8 + 1) * F],
                                        self.turned_sb[w % 2][:, c * P:(c + 1) * P], value[:, c, :],
                                        start=(c == 0), stop=(c == 3))
            last.then_inc(self.out_ready, 1)

    def act(self, act):
        for w in range(W):
            act.wait_ge(self.turned, w + 1)
            if w >= 2:
                act.wait_ge(self.out_ready, w - 1)
            self.nc.scalar.activation(self.turned_sb[w % 2][:, :], self.ps_t[w % 2][:, 0:4 * P],
                                      ACT.Copy).then_inc(self.copied, 1)

    def banks(self):
        for b in range(4):
            n = min(8, W - 8 * b)
            yield 8 * b, n, self.ps_o[b][0:P, 0:n * F].rearrange("p (w f) -> p w f", f=F)


class Dense:

    def __init__(self, nc, s, m, ps_t, ps_o, tag):
        self.nc, self.m, self.ps_t, self.ps_o = nc, m, ps_t, ps_o
        self.turned_sb = s.sb(f"{tag}_sb", [128, W * P])
        self.ready, self.turned = s.sem(f"{tag}_in_ready"), s.sem(f"{tag}_turned")
        self.copied, self.out_ready = s.sem(f"{tag}_copied"), s.sem(f"{tag}_out")
        self.chunks = (W + 3) // 4

    def pe_turn(self, pe, cat, width):
        pe.wait_ge(self.ready, 1)
        for c in range(self.chunks):
            if c >= 2:
                pe.wait_ge(self.copied, c - 1)
            for w in range(4 * c, min(4 * c + 4, W)):
                o = (w % 4) * P
                last = self.nc.tensor.transpose(self.ps_t[c % 2][0:width, o:o + P], cat[:, w, 0:width], self.m.ident[0:P, 0:P])
            last.then_inc(self.turned, 1)

    def pe_out(self, pe, width, weight):
        pe.wait_ge(self.copied, self.chunks)
        for w in range(W):
            last = self.nc.tensor.matmul(self.ps_o[w // 8][0:P, (w % 8) * F:(w % 8 + 1) * F],
                                         self.turned_sb[0:width, w * P:(w + 1) * P], weight, start=True, stop=True)
        last.then_inc(self.out_ready, 1)

    def act(self, act, width):
        for c in range(self.chunks):
            act.wait_ge(self.turned, c + 1)
            n = P * (min(4 * c + 4, W) - 4 * c)
            self.nc.scalar.activation(self.turned_sb[0:width, 4 * c * P:4 * c * P + n], self.ps_t[c % 2][0:width, 0:n],
                                      ACT.Copy).then_inc(self.copied, 1)

    def banks(self):
        for b in range(4):
            n = min(8, W - 8 * b)
            yield 8 * b, n, self.ps_o[b][0:P, 0:n * F].rearrange("p (w f) -> p w f", f=F)


def finish_layer0(nc, m):
    with ExitStack() as stack:
        s = Scope(nc, stack, "l0end")
        norm_scratch(s)
        heads = Heads(nc, s, m)
        value = s.sb("value", [128, 4, F])
        inv = s.sb("inv", [P, W, H])
        y = s.sb("y", [P, W, F])
        graph_rows = s.sb("graph_rows", [P, W, F + 1])
        value_ps = s.ps("value_ps")
        own_sem, value_ready, value_copied = s.sem("dve_step"), s.sem("value_ready"), s.sem("value_copied")
        rows_ready, written = s.sem("rows_ready"), s.sem("written")
        block = stack.enter_context(nc.Block())

        @block.vector
        def _(dve):
            own, v = Own(dve, own_sem), nc.vector
            own(v.tensor_scalar(inv[:, :, :], m.acc[:, :, HF:HF + H], 1e-30, None, ALU.max))
            own(v.reciprocal(inv[:, :, :], inv[:, :, :]))
            for h in range(H):
                cols = m.acc[:, :, h * F:(h + 1) * F]
                last = v.tensor_tensor(cols, cols, over(inv[:, :, h].unsqueeze(2), (P, W, F)), ALU.mult)
                if h < H - 1:
                    own(last)
            last.then_inc(heads.acc_ready, 1)
            dve.wait_ge(heads.out_ready, W)
            for w0, n, out in heads.banks():
                yb = y[:, w0:w0 + n, :]
                own(v.tensor_copy(yb, out))
                own(v.scalar_tensor_tensor(yb, yb, 0.2, yb, ALU.mult, ALU.max))
                own(v.tensor_tensor(m.x[:, w0:w0 + n, :], m.x[:, w0:w0 + n, :], yb, ALU.add))
            layer_norm(nc, own, s, m.x[:, :, :], m.h[:, :, :])
            own(v.tensor_copy(graph_rows[:, :, 0:F], m.h[:, :, :]))
            v.memset(graph_rows[:, :, F:F + 1], 1.0).then_inc(rows_ready, 1)

        @block.tensor
        def _(pe):
            for h in range(H):
                o, c = (h % 2) * F, h // 2
                last = nc.tensor.matmul(value_ps[o:o + F, c * F:(c + 1) * F], m.wt0[:, h * F:(h + 1) * F],
                                        m.merge[:, h, :], start=True, stop=True)
            last.then_inc(value_ready, 1)
            pe.wait_ge(value_copied, 1)
            heads.pe(pe, value)

        @block.scalar
        def _(act):
            act.wait_ge(value_ready, 1)
            nc.scalar.activation(value[:, :, :], value_ps[:, 0:4 * F].rearrange("p (c f) -> p c f", f=F),
                                 ACT.Copy).then_inc(value_copied, 1)
            heads.act(act)
            norm_root(nc, act, s, 1)

        @block.sync
        def _(sp):
            sp.wait_ge(rows_ready, 1)
            sp.dma_start(m.table[:, 0:F + 1].rearrange("(w p) c -> p w c", p=P), graph_rows[:, :, :]).then_inc(written, 16)
            sp.wait_ge(written, 16)


def finish_mean(nc, m, tag, weight, bias, kind):
    with ExitStack() as stack:
        s = Scope(nc, stack, tag)
        norm_scratch(s)
        cat = s.sb("cat", [P, W, 2 * F])
        inv = s.sb("inv", [P, W])
        ps_t = [s.ps(f"ps_t{i}") for i in range(2)]
        ps_o = [s.ps(f"ps_o{i}") for i in range(4)]
        dense = Dense(nc, s, m, ps_t, ps_o, "dense")
        own_sem, rows_ready, written = s.sem("dve_step"), s.sem("rows_ready"), s.sem("written")
        block = stack.enter_context(nc.Block())

        @block.vector
        def _(dve):
            own, v = Own(dve, own_sem), nc.vector
            if kind == "hidden":
                own(v.tensor_copy(m.degree[:, :], m.acc[:, :, F]))
            own(v.tensor_scalar(inv[:, :], m.degree[:, :], 1.0, None, ALU.max))
            own(v.reciprocal(inv[:, :], inv[:, :]))
            own(v.tensor_tensor(cat[:, :, 0:F], m.acc[:, :, 0:F], over(inv[:, :].unsqueeze(2), (P, W, F)), ALU.mult))
            v.tensor_copy(cat[:, :, F:2 * F], m.h[:, :, :]).then_inc(dense.ready, 1)
            dve.wait_ge(dense.out_ready, 1)
            for w0, n, out in dense.banks():
                b = over(bias.unsqueeze(1), (P, n, F))
                if kind == "hidden":
                    own(v.tensor_tensor(m.h[:, w0:w0 + n, :], out, b, ALU.add))
                else:
                    own(v.tensor_tensor(cat[:, w0:w0 + n, 0:F], out, b, ALU.add))
                    own(v.tensor_tensor(m.x[:, w0:w0 + n, :], m.x[:, w0:w0 + n, :], cat[:, w0:w0 + n, 0:F], ALU.add))
            if kind == "hidden":
                own(v.tensor_scalar(m.h[:, :, :], m.h[:, :, :], 0.0, None, ALU.max))
            if kind == "last":
                layer_norm(nc, own, s, m.x[:, :, :], m.h[:, :, :])
            v.memset(inv[:, :], 0.0).then_inc(rows_ready, 1)

        @block.tensor
        def _(pe):
            dense.pe_turn(pe, cat, 2 * F)
            dense.pe_out(pe, 2 * F, weight)

        @block.scalar
        def _(act):
            dense.act(act, 2 * F)
            if kind == "last":
                norm_root(nc, act, s, 1)

        if kind != "edges":
            @block.sync
            def _(sp):
                sp.wait_ge(rows_ready, 1)
                sp.dma_start(m.table[:, 0:F].rearrange("(w p) c -> p w c", p=P), m.h[:, :, :]).then_inc(written, 16)
                sp.wait_ge(written, 16)


def tables3(nc, m):
    with ExitStack() as stack:
        s = Scope(nc, stack, "l3tab")
        tables = Tables(nc, s, m)
        block = stack.enter_context(nc.Block())
        tables.write(block, m.x, m.wt3, m.at3, table_score=0)


def gather_rows3(nc, m):
    with ExitStack() as stack:
        s = Scope(nc, stack, "l3rows")
        index = [s.sb(f"index{i}", [P, 8], I32) for i in range(2)]
        rows = [s.sb(f"rows{i}", [P, 8, R]) for i in range(2)]
        staged, kept, go = s.sem("staged"), s.sem("kept"), s.sem("go")
        gathered, spilled = s.sems("gathered", 2), s.sems("spilled", 2)
        block = stack.enter_context(nc.Block())
        spill = m.spill[:, :].rearrange("(p c) r -> p c r", p=P)

        @block.gpsimd
        def _(pool):
            def half(i, b):
                if not (isinstance(i, int) and i == 0):
                    pool.wait_ge(gathered[b], 128 * i)
                    pool.wait_ge(spilled[b], 16 * i)
                    pool.wait_ge(kept, 2 * i + b - 1)
                nc.gpsimd.tensor_copy(index[b][:, :], m.src_run[:, bass.ds(16 * i + 8 * b, 8)]).then_inc(staged, 1)
                pool.wait_ge(staged, 2 * i + b + 1)
                pool.sem_inc(go, 1)
                for t in range(8):
                    pool.indirect_dma_start(rows[b][:, t, :], None, m.table[:, :],
                                            bass.IndirectOffsetOnAxis(ap=index[b][:, t:t + 1], axis=0)
                                            ).then_inc(gathered[b], 16)
            half(0, 0)
            half(0, 1)
            with pool.Fori(1, C // 16, 1) as i:
                half(i, 0)
                half(i, 1)

        @block.sync
        def _(sp):
            with sp.Fori(0, C // 16, 1) as i:
                for b in range(2):
                    sp.wait_ge(gathered[b], 128 * (i + 1))
                    sp.dma_start(spill[:, bass.ds(16 * i + 8 * b, 8), :], rows[b][:, :, :]).then_inc(spilled[b], 16)
            for b in range(2):
                sp.wait_ge(spilled[b], 16 * (C // 16))

        @block.vector
        def _(dve):
            with dve.Fori(0, C // 16, 1) as i:
                for b in range(2):
                    dve.wait_ge(gathered[b], 128 * (i + 1))
                    nc.vector.tensor_copy(m.edge_score[:, bass.ds(16 * i + 8 * b, 8), :],
                                          rows[b][:, :, F:R]).then_inc(kept, 1)


def maxima3(nc, m):
    with ExitStack() as stack:
        s = Scope(nc, stack, "l3max")
        key, neq, same0 = s.sb("key", [P, C]), s.sb("neq", [P, C]), s.sb("same0", [P, C])
        run = s.sb("run", [P, C, H])
        ends = s.sb("ends", [P, 4])
        edge_turn = s.sb("edge_turn", [4, 128])
        prev_last = s.sb("prev_last", [P, 1])
        cont, whole = s.sb("cont", [P, 1]), s.sb("whole", [P, 1])
        pack = s.sb("pack", [P, 4, H])
        turned = s.sb("turned", [H, 4, 128])
        carry = s.sb("carry", [H, 128])
        carry_in = s.sb("carry_in", [H, 128])
        carry_p = s.sb("carry_p", [P, H])
        last_f = s.sb("last_f", [P, W])
        cum = s.sb("cum", [P, W])
        last_i = s.sb("last_i", [P, W], I32)
        found = s.sb("found", [P, W, H])
        hole = s.sb("hole", [P, W])
        rest = s.sb("rest", [P, W, H])
        s.rest = rest[:, :, :]
        ps = s.ps("sums")
        ps2 = s.ps("before")
        ps3 = [s.ps(f"turn{i}") for i in range(4)]
        own_sem = s.sem("dve_step")
        to_pe, from_pe = s.sem("operands_ready"), s.sem("products_ready")
        run_ready, run_written, found_in, index_ready = s.sem("run_ready"), s.sem("run_written"), s.sem("found_in"), s.sem("index_ready")
        block = stack.enter_context(nc.Block())

        @block.vector
        def _(dve):
            own, v = Own(dve, own_sem), nc.vector
            v.tensor_copy(key[:, :], m.dst_run[:, :]).then_inc(to_pe, 1)
            dve.wait_ge(from_pe, 1)
            own(v.tensor_tensor_scan(cum[:, :], m.ones[0:P, 0:W], ps[0:P, 0:W], 0.0, ALU.mult, ALU.add))
            own(v.tensor_tensor(cum[:, :], cum[:, :], ps[0:P, 0:W], ALU.subtract))
            own(v.tensor_tensor(last_f[:, :], cum[:, :], ps2[0:P, 0:W], ALU.add))
            own(v.tensor_scalar(last_f[:, :], last_f[:, :], -1.0, 0.0, ALU.add, ALU.max))
            v.tensor_copy(last_i[:, :], last_f[:, :]).then_inc(index_ready, 1)
            own(v.memset(neq[:, 0:1], -FAR))
            own(v.tensor_tensor(neq[:, 1:C], key[:, 1:C], key[:, 0:C - 1], ALU.not_equal))
            own(v.tensor_scalar(neq[:, 1:C], neq[:, 1:C], -FAR, None, ALU.mult))
            for h in range(H):
                own(v.tensor_tensor_scan(run[:, :, h], neq[:, :], m.edge_score[:, :, h], -FAR, ALU.add, ALU.max))
            own(v.tensor_copy(pack[:, 0, :], run[:, C - 1, :]))
            own(v.tensor_copy(pack[:, 1, :], over(key[:, 0:1], (P, H))))
            v.tensor_copy(pack[:, 2, :], over(key[:, C - 1:C], (P, H))).then_inc(to_pe, 1)
            dve.wait_ge(from_pe, 2)
            for i in range(3):
                own(v.tensor_copy(turned[:, i, 0:P], ps3[i][0:H, 0:P]))
            last, first, final = turned[:, 0, 0:P], turned[:, 1, 0:P], turned[:, 2, 0:P]
            gate = turned[:, 3, 0:P]
            own(v.memset(carry_in[:, :], -FAR))
            own(v.memset(gate, -FAR))
            own(v.tensor_tensor(turned[:, 3, 1:P], turned[:, 1, 1:P], turned[:, 2, 0:P - 1], ALU.not_equal))
            own(v.tensor_scalar(turned[:, 3, 1:P], turned[:, 3, 1:P], -FAR, None, ALU.mult))
            own(v.tensor_tensor(final, first, final, ALU.not_equal))
            own(v.scalar_tensor_tensor(final, final, -FAR, gate, ALU.mult, ALU.min))
            own(v.tensor_tensor_scan(carry[:, 0:P], final, last, -FAR, ALU.add, ALU.max))
            own(v.tensor_tensor(carry_in[:, 1:P], carry[:, 0:P - 1], turned[:, 3, 1:P], ALU.add))
            v.tensor_scalar(carry_in[:, 0:P], carry_in[:, 0:P], -FAR, None, ALU.max).then_inc(to_pe, 1)
            own(v.tensor_scalar(same0[:, :], key[:, :], key[:, 0:1], -FAR, ALU.not_equal, ALU.mult))
            dve.wait_ge(from_pe, 3)
            own(v.tensor_copy(carry_p[:, :], ps3[3][0:P, 0:H]))
            for h in range(H):
                last_op = v.scalar_tensor_tensor(run[:, :, h], same0[:, :], carry_p[:, h:h + 1], run[:, :, h],
                                                 ALU.add, ALU.max)
                if h < H - 1:
                    own(last_op)
            last_op.then_inc(run_ready, 1)
            own(v.tensor_scalar(hole[:, :], m.degree[:, :], 0.0, None, ALU.is_equal))
            dve.wait_ge(found_in, 16 * W)
            own(v.tensor_scalar(hole[:, :], hole[:, :], -FAR, None, ALU.mult))
            own(v.tensor_tensor(found[:, :, :], found[:, :, :], over(hole[:, :].unsqueeze(2), (P, W, H)), ALU.add))
            own(v.tensor_tensor(found[:, :, :], found[:, :, :], m.far[:, :, :], ALU.max))
            own(v.tensor_tensor(found[:, :, :], found[:, :, :], m.near[:, :, :], ALU.add))
            own(v.scalar_tensor_tensor(found[:, :, :], found[:, :, :], 0.2, found[:, :, :], ALU.mult, ALU.max))
            split3(nc, own, s, found[:, :, :], [m.near_parts[:, :, i, H:2 * H] for i in range(3)])
            own(v.tensor_tensor(rest[:, :, :], m.near[:, :, :], m.far[:, :, :], ALU.add))
            own(v.scalar_tensor_tensor(rest[:, :, :], rest[:, :, :], 0.2, rest[:, :, :], ALU.mult, ALU.max))
            own(v.tensor_tensor(m.loop_att[:, :, :], rest[:, :, :], found[:, :, :], ALU.subtract))

        @block.tensor
        def _(pe):
            pe.wait_ge(to_pe, 1)
            nc.tensor.matmul(ps[0:P, 0:W], m.ones[0:P, 0:P], m.degree[:, :], start=True, stop=True)
            nc.tensor.matmul(ps2[0:P, 0:W], m.upto[0:P, 0:P], m.degree[:, :], start=True, stop=True).then_inc(from_pe, 1)
            pe.wait_ge(to_pe, 2)
            for i in range(3):
                last = nc.tensor.transpose(ps3[i][0:H, 0:P], pack[:, i, :], m.ident[0:P, 0:P])
            last.then_inc(from_pe, 1)
            pe.wait_ge(to_pe, 3)
            nc.tensor.transpose(ps3[3][0:P, 0:H], carry_in[:, 0:P], m.ident[0:H, 0:H]).then_inc(from_pe, 1)

        @block.sync
        def _(sp):
            sp.wait_ge(run_ready, 1)
            sp.dma_start(m.running[:, :].rearrange("(p c) h -> p c h", p=P), run[:, :, :]).then_inc(run_written, 16)

        @block.gpsimd
        def _(pool):
            pool.wait_ge(index_ready, 1)
            pool.wait_ge(run_written, 16)
            for w in range(W):
                pool.indirect_dma_start(found[:, w, :], None, m.running[:, :],
                                        bass.IndirectOffsetOnAxis(ap=last_i[:, w:w + 1], axis=0)).then_inc(found_in, 16)
            pool.wait_ge(found_in, 16 * W)


def finish_layer3(nc, m, io, out):
    with ExitStack() as stack:
        s = Scope(nc, stack, "l3end")
        norm_scratch(s)
        heads = Heads(nc, s, m)
        loop = s.sb("loop", [P, W, H])
        inv = s.sb("inv", [P, W, H])
        y = s.sb("y", [P, W, F])
        x1 = s.sb("x1", [P, W, F])
        hidden = s.sb("hidden", [2 * F, W * P])
        dense1 = Dense(nc, s, m, heads.ps_t, heads.ps_o, "ffn")
        own_sem, exp_ready, ff_ready, ff_psum = s.sem("dve_step"), s.sem("exp_ready"), s.sem("ff_ready"), s.sem("ff_psum")
        ff_out, result_ready, written = s.sem("ff_out"), s.sem("result_ready"), s.sem("written")
        block = stack.enter_context(nc.Block())
        bias_att, b2, g1, c1, g2, c2 = (m.rows[:, i * F:(i + 1) * F] for i in range(3, 9))
        chunks = (W + 3) // 4

        def rowwise(ap, n=W):
            return over(ap.unsqueeze(1), (P, n, F))

        @block.vector
        def _(dve):
            own, v = Own(dve, own_sem), nc.vector
            dve.wait_ge(exp_ready, 1)
            own(v.tensor_tensor(inv[:, :, :], m.acc[:, :, HF:HF + H], loop[:, :, :], ALU.add))
            own(v.tensor_scalar(inv[:, :, :], inv[:, :, :], 1e-16, None, ALU.add))
            own(v.reciprocal(inv[:, :, :], inv[:, :, :]))
            own(v.tensor_scalar(inv[:, :, :], inv[:, :, :], 1.0 / H, None, ALU.mult))
            for h in range(H):
                cols = m.acc[:, :, h * F:(h + 1) * F]
                own(v.tensor_tensor(y[:, :, :], m.h[:, :, :], over(loop[:, :, h].unsqueeze(2), (P, W, F)), ALU.mult))
                own(v.tensor_tensor(cols, cols, y[:, :, :], ALU.add))
                last = v.tensor_tensor(cols, cols, over(inv[:, :, h].unsqueeze(2), (P, W, F)), ALU.mult)
                if h < H - 1:
                    own(last)
            last.then_inc(heads.acc_ready, 1)
            dve.wait_ge(heads.out_ready, W)
            own(v.tensor_tensor(y[:, :, :], m.h[:, :, :], rowwise(bias_att), ALU.add))
            for w0, n, o in heads.banks():
                own(v.tensor_tensor(y[:, w0:w0 + n, :], y[:, w0:w0 + n, :], o, ALU.add))
            layer_norm(nc, own, s, y[:, :, :], x1[:, :, :], relu=False)
            own(v.tensor_tensor(x1[:, :, :], x1[:, :, :], rowwise(g1), ALU.mult))
            v.tensor_tensor(x1[:, :, :], x1[:, :, :], rowwise(c1), ALU.add).then_inc(dense1.ready, 1)
            dve.wait_ge(dense1.ready, 1)
            dve.wait_ge(ff_out, 1)
            own(v.tensor_tensor(y[:, :, :], x1[:, :, :], rowwise(b2), ALU.add))
            for w0, n, o in heads.banks():
                own(v.tensor_tensor(y[:, w0:w0 + n, :], y[:, w0:w0 + n, :], o, ALU.add))
            layer_norm(nc, own, s, y[:, :, :], x1[:, :, :], relu=False)
            own(v.tensor_tensor(x1[:, :, :], x1[:, :, :], rowwise(g2), ALU.mult))
            own(v.tensor_tensor(x1[:, :, :], x1[:, :, :], rowwise(c2), ALU.add))
            v.tensor_tensor(x1[:, :, :], x1[:, :, :], m.x[:, :, :], ALU.add).then_inc(result_ready, 1)

        @block.tensor
        def _(pe):
            heads.pe(pe, m.value3)
            dense1.pe_turn(pe, x1, F)
            pe.wait_ge(dense1.copied, chunks)
            for c in range(chunks):
                if c >= 2:
                    pe.wait_ge(ff_ready, c - 1)
                n = P * (min(4 * c + 4, W) - 4 * c)
                nc.tensor.matmul(heads.ps_t[c % 2][:, 0:n], m.ff1[:, :], dense1.turned_sb[0:F, 4 * c * P:4 * c * P + n],
                                 start=True, stop=True).then_inc(ff_psum, 1)
            pe.wait_ge(ff_ready, chunks)
            for w in range(W):
                last = nc.tensor.matmul(heads.ps_o[w // 8][0:P, (w % 8) * F:(w % 8 + 1) * F],
                                        hidden[:, w * P:(w + 1) * P], m.ff2[:, :], start=True, stop=True)
            last.then_inc(ff_out, 1)

        @block.scalar
        def _(act):
            nc.scalar.activation(loop[:, :, :], m.loop_att[:, :, :], ACT.Exp).then_inc(exp_ready, 1)
            heads.act(act)
            norm_root(nc, act, s, 1)
            dense1.act(act, F)
            for c in range(chunks):
                act.wait_ge(ff_psum, c + 1)
                n = P * (min(4 * c + 4, W) - 4 * c)
                nc.scalar.activation(hidden[:, 4 * c * P:4 * c * P + n], heads.ps_t[c % 2][:, 0:n], ACT.Relu,
                                     bias=m.ff1_b[:, 0:1]).then_inc(ff_ready, 1)
            norm_root(nc, act, s, 2)

        @block.sync
        def _(sp):
            sp.wait_ge(result_ready, 1)
            sp.dma_start(out.rearrange("(w p) f -> p w f", p=P), x1[:, :, :]).then_inc(written, 16)
            sp.wait_ge(written, 16)


class Memory:
    pass


LAYERS = 4


def program(nc, io, out):
    m = Memory()
    with ExitStack() as stack:
        def sb(name, shape, dt=F32):
            return stack.enter_context(nc.sbuf_tensor(name, shape, dt))

        m.x, m.h = sb("x", [P, W, F]), sb("h", [P, W, F])
        m.h_turned = sb("h_turned", [F, N])
        m.src_run, m.dst_run = sb("src_run", [P, C], I32), sb("dst_run", [P, C], I32)
        m.last_key = sb("last_key", [100, 2], I32)
        m.wt0, m.at0, m.merge = sb("wt0", [F, HF]), sb("at0", [F, 2 * H]), sb("merge", [F, H, F])
        m.wt3, m.at3, m.value3 = sb("wt3", [F, HF]), sb("at3", [F, 2 * H]), sb("value3", [2 * F, 4, F])
        m.sage1, m.sage2, m.edge_w = (sb(n, [2 * F, F]) for n in ("sage1", "sage2", "edge_w"))
        m.ff1, m.ff1_b, m.ff2 = sb("ff1", [F, 2 * F]), sb("ff1_b", [2 * F, 1]), sb("ff2", [2 * F, F])
        m.rows = sb("rows", [P, 9 * F])
        m.ident, m.ones, m.upto = (sb(n, [128, 128]) for n in ("ident", "ones", "upto"))
        m.node_iota, m.step_iota = sb("node_iota", [P, P]), sb("step_iota", [128, K])
        m.group_iota, m.edge_iota = sb("group_iota", [100, 2]), sb("edge_iota", [100, 2])
        for name in ("by_dst", "by_src"):
            t = Memory()
            t.group_f, t.window_f, t.first_node = (sb(f"{name}_{n}", [128, K]) for n in ("group_f", "window_f", "first"))
            t.group, t.window = sb(f"{name}_group", [1, K], I32), sb(f"{name}_window", [1, K], I32)
            if name == "by_dst":
                m.by_dst = t
            else:
                m.by_src = t
        m.near, m.far = sb("near", [P, W, H]), sb("far", [P, W, H])
        m.near_parts = sb("near_parts", [P, W, 3, 2 * H], BF16)
        m.degree, m.loop_att = sb("degree", [P, W]), sb("loop_att", [P, W, H])
        m.src, m.dst = io["src"], io["dst"]
        m.records = nc.dram_tensor("records", (E, 2), I32, kind="Internal").ap()
        m.table = nc.dram_tensor("table", (N, R), F32, kind="Internal").ap()
        m.spill = nc.dram_tensor("spill", (E, R), F32, kind="Internal").ap()
        m.running = nc.dram_tensor("running", (E, H), F32, kind="Internal").ap()

        m.sems = StepSems(nc, stack)
        set_up(nc, m, io)
        with ExitStack() as early:
            m.place = early.enter_context(nc.sbuf_tensor("place", [P, C], I32))
            m.record = early.enter_context(nc.sbuf_tensor("record", [P, C, 2], I32))
            order_edges(nc, m)
            scatter_and_tables(nc, m)
        with ExitStack() as rest:
            m.acc = rest.enter_context(nc.sbuf_tensor("acc", [P, W, HF + H], F32))
            attend(nc, m, "l0", m.by_src, from_spill=False)
            finish_layer0(nc, m)
            if LAYERS >= 2:
                gather_sum(nc, m, "l1a", F + 1)
                finish_mean(nc, m, "l1a_end", m.sage1[:, :], m.rows[:, 0:F], "hidden")
                gather_sum(nc, m, "l1b", F)
                finish_mean(nc, m, "l1b_end", m.sage2[:, :], m.rows[:, F:2 * F], "last")
            if LAYERS >= 3:
                gather_sum(nc, m, "l2", F, io["edge_attr"])
                finish_mean(nc, m, "l2_end", m.edge_w[:, :], m.rows[:, 2 * F:3 * F], "edges")
            if LAYERS >= 4:
                tables3(nc, m)
                with ExitStack() as scores:
                    m.edge_score = scores.enter_context(nc.sbuf_tensor("edge_score", [P, C, H], F32))
                    gather_rows3(nc, m)
                    maxima3(nc, m)
                attend(nc, m, "l3", m.by_dst, from_spill=True)
                finish_layer3(nc, m, io, out)
            else:
                with ExitStack() as st:
                    w = st.enter_context(nc.semaphore("dbg"))
                    block = st.enter_context(nc.Block())

                    @block.sync
                    def _(sp):
                        sp.dma_start(out.rearrange("(w p) f -> p w f", p=P), m.x[:, :, :]).then_inc(w, 16)
                        sp.wait_ge(w, 16)


def kernel(**inputs):
    import numpy as np
    import concourse.bacc as bacc
    from concourse.bass_utils import run_bass_kernel_spmd

    a = {k: np.asarray(v) for k, v in inputs.items()}
    a0, w0 = a["L0_gnn_a"], a["L0_gnn_W"]
    w3 = a["L3_gnn_W_att"]
    arrays = {
        "x": a["x"], "src": a["src"], "dst": a["dst"], "edge_attr": a["edge_attr_64"],
        "wt0": w0.transpose(2, 0, 1).reshape(F, HF),
        "at0": np.concatenate([a0[:, :F, 0].T, a0[:, F:, 0].T], axis=1),
        "merge": a["L0_gnn_merge_kernel"].reshape(H, F, F).transpose(1, 0, 2),
        "wt3": w3.reshape(F, H, F).transpose(2, 1, 0).reshape(F, HF),
        "at3": np.concatenate([a["L3_gnn_att_src"].T, a["L3_gnn_att_dst"].T], axis=1),
        "value3": w3.reshape(F, 4, 2, F).transpose(2, 0, 1, 3).reshape(2 * F, 4, F),
        "sage1": np.concatenate([a["L1_gnn_w1_l"], a["L1_gnn_w1_r"]]),
        "sage2": np.concatenate([a["L1_gnn_w2_l"], a["L1_gnn_w2_r"]]),
        "edge_w": np.concatenate([a["L2_gnn_W"].T[F:], a["L2_gnn_W"].T[:F]]),
        "ff1": a["L3_gnn_W1"], "ff1_b": a["L3_gnn_b1"].reshape(2 * F, 1), "ff2": a["L3_gnn_W2"],
        "rows": np.stack([a[n] for n in (
            "L1_gnn_b1", "L1_gnn_b2", "L2_gnn_b", "L3_gnn_bias_att", "L3_gnn_b2",
            "L3_gnn_ln1_g", "L3_gnn_ln1_b", "L3_gnn_ln2_g", "L3_gnn_ln2_b")]),
    }
    nc = bacc.Bacc("TRN2", target_bir_lowering=False, num_devices=1)
    io = {}
    for name, value in arrays.items():
        arrays[name] = np.ascontiguousarray(value)
        io[name] = nc.dram_tensor(name + "_in", value.shape, mybir.dt.from_np(value.dtype), kind="ExternalInput").ap()
    out = nc.dram_tensor("out", (N, F), F32, kind="ExternalOutput").ap()
    program(nc, io, out)
    r = run_bass_kernel_spmd(nc, [{k + "_in": v for k, v in arrays.items()}], core_ids=[0])
    return r.results[0]["out"]
```

```python
from contextlib import ExitStack

import concourse.bass as bass
from concourse import mybir
from concourse.bass import OrderedEngineSet

F32 = mybir.dt.float32
BF16 = mybir.dt.bfloat16
F16 = mybir.dt.float16
I32 = mybir.dt.int32
ALU = mybir.AluOpType
ACT = mybir.ActivationFunctionType
AX = mybir.AxisListType

N, E, F, H = 3125, 100000, 64, 8
P = 125
W = N // P
T = 4
SLOTS = 4
U = 8
G = E // (P * T)
K = G + W - 1
Q = K // U
HF = H * F
D = 25
V = N // D
KV = G + V - 1
UV = 12
CW = 26 * D
HALF = (HF + H) // 2
R = F + H
C = E // P
FAR = 1.0e30
OUT = 1000.0
PAD = U


def load_group(nc, steps, k):
    _, values = nc.values_load_multi_w_load_instructions(
        steps.group[0:1, bass.ds(k, 1)], engines=[mybir.EngineType.SP], min_val=0, max_val=G - 1,
        skip_runtime_bounds_check_because="order_edges counts the groups, from 0 to G - 1")
    return values[0]


class Own:

    def __init__(self, eng, sem):
        self.eng, self.sem, self.n = eng, sem, 0

    def __call__(self, instruction):
        self.n += 1
        instruction.then_inc(self.sem, 1)
        self.eng.wait_ge(self.sem, self.n)


def rounds(nc, eng, step, load=None, steps=K, u=U):
    last = steps // u - 1
    def one_round(q):
        if load:
            values = load(q)
            for j in range(u):
                step(q, j, values[j])
        else:
            for j in range(u):
                step(q, j)
    one_round(0)
    with nc.Fori(1, last, 1, engines=OrderedEngineSet([eng.engine]), hint_back_edge=True) as q:
        one_round(q)
    one_round(last)


def load_windows(nc, engine, steps, first):
    _, values = nc.values_load_multi_w_load_instructions(
        steps.window[0:1, bass.ds(first + PAD, U)], engines=[engine], min_val=0, max_val=W - 1,
        skip_runtime_bounds_check_because="order_edges counts the windows, from 0 to W - 1")
    return values


def early(q, j, n=SLOTS):
    return isinstance(q, int) and q == 0 and j < n


def uses(q, j):
    return q * (U // SLOTS) + j // SLOTS


def after(q, j, n=1):
    if isinstance(q, int) and q == Q - 1 and j + n >= U:
        return None
    return (q, j + n) if j + n < U else (q + 1, j + n - U)


def before(q, j):
    if early(q, j, 1):
        return None
    return (q, j - 1) if j else (q - 1, U - 1)


def over(ap, shape):
    return ap.to_broadcast(list(shape))


class SharedSems:

    def __init__(self, nc, stack, n):
        self.nc, self.used = nc, 0
        self.all = [stack.enter_context(nc.semaphore(f"shared{i}")) for i in range(n)]
        assert [x.num for x in self.all] == list(range(self.all[0].num, self.all[0].num + n))

    def reset(self):
        if self.used:
            first = self.all[0].num
            self.nc.all_engine_barrier(sems_to_clear=range(first, first + self.used))
        self.used = 0

    def take(self):
        self.used += 1
        return self.all[self.used - 1]


class Scope:

    def __init__(self, nc, stack, tag, shared=None):
        self.nc, self.stack, self.tag, self.shared = nc, stack, tag, shared
        if shared:
            shared.reset()

    def sb(self, name, shape, dt=F32):
        return self.stack.enter_context(self.nc.sbuf_tensor(f"{self.tag}_{name}", shape, dt))

    def ps(self, name, shape=(128, 512)):
        return self.stack.enter_context(self.nc.psum_tensor(f"{self.tag}_{name}", list(shape), F32))

    def sem(self, name):
        return self.shared.take()

    def sems(self, name, n):
        return [self.sem(f"{name}{i}") for i in range(n)]

    def pool_dma_sems(self, name, n):
        return [self.stack.enter_context(self.nc.semaphore(f"{self.tag}_{name}{i}")) for i in range(n)]


class StepSems:

    NAMES = ("rel_ready", "hot_ready", "turned", "turned_copied", "near_ready", "z_ready", "leaky_ready", "less_max",
             "score_ready", "att_ready", "msg_ready", "sums_ready", "acc_ready", "zeroed", "gather_go", "load_go")

    def __init__(self, nc, stack):
        self.nc, self.base, self.used = nc, 0, False
        self.gathered = [stack.enter_context(nc.semaphore(f"step_gathered{i}")) for i in range(4)]
        self.keys_in = [stack.enter_context(nc.semaphore(f"step_keys_in{i}")) for i in range(4)]
        self.streamed = [stack.enter_context(nc.semaphore(f"step_streamed{i}")) for i in range(4)]
        self.by_name = {n: stack.enter_context(nc.semaphore(f"step_{n}")) for n in self.NAMES}

    def begin(self, gathers):
        if self.used:
            numbers = sorted(s.num for s in (*self.keys_in, *self.streamed, *self.by_name.values()))
            assert numbers == list(range(numbers[0], numbers[-1] + 1))
            self.nc.all_engine_barrier(sems_to_clear=range(numbers[0], numbers[-1] + 1))
        self.used = True
        base = self.base
        if gathers:
            self.base += 16 * T * K // SLOTS
        return base



def norm_scratch(s):
    s.mean, s.var, s.root = s.sb("mean", [P, W]), s.sb("var", [P, W]), s.sb("root", [P, W])
    s.cen, s.sq = s.sb("cen", [P, W, F]), s.sb("sq", [P, W, F])
    s.var_ready, s.root_ready, s.norms = s.sem("var_ready"), s.sem("root_ready"), 0


def layer_norm(nc, own, s, x, y, relu=True):
    v = nc.vector
    own(v.tensor_reduce(s.mean[:, :], x, AX.X, ALU.add))
    own(v.tensor_scalar(s.mean[:, :], s.mean[:, :], 1.0 / F, None, ALU.mult))
    own(v.tensor_tensor(s.cen[:, :, :], x, over(s.mean[:, :].unsqueeze(2), (P, W, F)), ALU.subtract))
    own(v.tensor_tensor(s.sq[:, :, :], s.cen[:, :, :], s.cen[:, :, :], ALU.mult))
    own(v.tensor_reduce(s.var[:, :], s.sq[:, :, :], AX.X, ALU.add))
    v.tensor_scalar(s.var[:, :], s.var[:, :], 1.0 / F, 1e-5, ALU.mult, ALU.add).then_inc(s.var_ready, 1)
    s.norms += 1
    own.eng.wait_ge(s.root_ready, s.norms)
    own(v.reciprocal(s.root[:, :], s.root[:, :]))
    own(v.tensor_tensor(s.mean[:, :], s.root[:, :], s.root[:, :], ALU.mult))
    own(v.tensor_tensor(s.var[:, :], s.var[:, :], s.mean[:, :], ALU.mult))
    own(v.tensor_scalar(s.var[:, :], s.var[:, :], -0.5, 1.5, ALU.mult, ALU.add))
    own(v.tensor_tensor(s.var[:, :], s.var[:, :], s.root[:, :], ALU.mult))
    own(v.tensor_tensor(y, s.cen[:, :, :], over(s.var[:, :].unsqueeze(2), (P, W, F)), ALU.mult))
    if relu:
        own(v.tensor_scalar(y, y, 0.0, None, ALU.max))


def norm_root(nc, act, s, n):
    act.wait_ge(s.var_ready, n)
    nc.scalar.activation(s.root[:, :], s.var[:, :], ACT.Sqrt).then_inc(s.root_ready, 1)


def split3(nc, own, s, x, parts):
    v = nc.vector
    own(v.tensor_copy(parts[0], x))
    own(v.tensor_tensor(s.rest, x, parts[0], ALU.subtract))
    own(v.tensor_copy(parts[1], s.rest))
    own(v.tensor_tensor(s.rest, s.rest, parts[1], ALU.subtract))
    own(v.tensor_copy(parts[2], s.rest))



def set_up(nc, m, io):
    with ExitStack() as stack:
        s = Scope(nc, stack, "setup", m.shared)
        loaded, made, iota_made = s.sem("loaded"), s.sem("made"), s.sem("iota_made")
        ints = s.sb("ints", [P, P], I32)
        step_ints = s.sb("step_ints", [128, CW], I32)
        group_ints = s.sb("group_ints", [100, 2], I32)
        block = stack.enter_context(nc.Block())

        @block.sync
        def _(sp):
            loads = [
                (m.x[:, :, :], io["x"].rearrange("(w p) f -> p w f", p=P)),
                (m.src_run[:, :], io["src"].rearrange("(p c) -> p c", p=P)),
                (m.dst_run[:, :], io["dst"].rearrange("(p c) -> p c", p=P)),
                (m.last_key[:, :], io["dst"].rearrange("(j p e) -> p j e", p=100, e=P * T)[:, :, P * T - 1]),
                (m.wt0[:, :], io["wt0"]), (m.at0[:, :], io["at0"]), (m.merge[:, :, :], io["merge"]),
                (m.wt3[:, :], io["wt3"]), (m.at3[:, :], io["at3"]), (m.value3[:, :, :], io["value3"]),
                (m.sage1[:, :], io["sage1"]), (m.sage2[:, :], io["sage2"]), (m.edge_w[:, :], io["edge_w"]),
                (m.ff1[:, :], io["ff1"]), (m.ff1_b[:, :], io["ff1_b"]), (m.ff2[:, :], io["ff2"]),
                (m.rows[:, :], io["rows"].rearrange("a n -> (a n)").partition_broadcast(P)),
            ]
            for out, in_ in loads:
                sp.dma_start(out, in_, allow_slow_non_contiguous=in_.shape[0] == 100).then_inc(loaded, 16)
            sp.wait_ge(loaded, 16 * len(loads))

        @block.gpsimd
        def _(pool):
            own = Own(pool, made)
            g = nc.gpsimd
            own(g.memset(m.ident[:, :], 0.0))
            own(g.affine_select(out=m.ident[:, :], in_=m.ident[:, :], compare_op=ALU.not_equal, fill=1.0,
                                base=0, pattern=[[-1, 128]], channel_multiplier=1))
            own(g.memset(m.ones[:, :], 1.0))
            own(g.affine_select(out=m.upto[:, :], in_=m.ones[:, :], compare_op=ALU.is_ge, fill=0.0,
                                base=0, pattern=[[1, 128]], channel_multiplier=-1))
            own(g.iota(ints[:, :], pattern=[[1, P]], base=0, channel_multiplier=0))
            own(g.iota(step_ints[:, :], pattern=[[1, CW]], base=0, channel_multiplier=0))
            g.iota(group_ints[:, :], pattern=[[100, 2]], base=0, channel_multiplier=1).then_inc(iota_made, 1)

        @block.vector
        def _(dve):
            dve.wait_ge(iota_made, 1)
            nc.vector.tensor_copy(m.node_iota[:, :], ints[:, :])
            nc.vector.tensor_copy(m.step_iota[:, :], step_ints[:, 0:KV])
            nc.vector.tensor_copy(m.code_iota[:, :], step_ints[0:P, :])
            nc.vector.tensor_copy(m.group_iota[:, :], group_ints[:, :])
            nc.vector.tensor_scalar(m.edge_iota[:, :], group_ints[:, :], float(P * T), float(P * T - 1), ALU.mult, ALU.add)


def plan_steps(nc, own, s, m, steps=K):
    v = nc.vector
    own(v.tensor_tensor(s.finish[:, :], s.last_window[:, :], m.group_iota[:, :], ALU.add))
    for j in range(2):
        own(v.tensor_scalar(s.done[:, j, 0:steps], m.step_iota[0:100, 0:steps], s.finish[:, j:j + 1], None, ALU.is_gt))


def order_edges(nc, m):
    with ExitStack() as stack:
        s = Scope(nc, stack, "order", m.shared)
        s.finish = s.sb("finish", [100, 2])
        s.done = s.sb("done", [100, 2, KV])
        s.last_window = s.sb("last_window", [100, 2])
        flags = s.sb("flags", [100, 2, W - 1])
        bounds = s.sb("bounds", [128, W - 1])
        fine_flags = s.sb("fine_flags", [100, 2, V - 1])
        fine_bounds = s.sb("fine_bounds", [128, V - 1])
        last_key = s.sb("last_key", [100, 2])
        key = s.sb("key", [P, C])
        win = s.sb("win", [P, C])
        mask = s.sb("mask", [P, C])
        one = s.sb("one", [P, C])
        count = s.sb("count", [P, W, C])
        place = s.sb("place", [P, C])
        totals = s.sb("totals", [P, W])
        base = s.sb("base", [128, W])
        cum = s.sb("cum", [128, W])
        code = s.sb("code", [P, C, 3])
        coded, codes_written = s.sem("coded"), s.sem("codes_written")
        own_sem, to_pe, from_pe = s.sem("dve_step"), s.sem("operands_ready"), s.sem("sums_ready")
        ps = s.ps("sums")
        ps2 = s.ps("before")
        block = stack.enter_context(nc.Block())

        def finish_steps(dve, own, table, n):
            v = nc.vector
            dve.wait_ge(from_pe, n)
            own(v.tensor_scalar(table.group_f[:, :], ps[:, 0:K], float(G - 1), None, ALU.min))
            own(v.tensor_tensor(table.window_f[:, :], m.step_iota[:, 0:K], table.group_f[:, :], ALU.subtract))
            own(v.tensor_scalar(table.first_node[:, :], table.window_f[:, :], float(P), None, ALU.mult))
            own(v.tensor_copy(table.group[:, :], table.group_f[0:1, :]))
            own(v.memset(table.window[:, :], 0))
            own(v.tensor_copy(table.window[:, PAD:PAD + K], table.window_f[0:1, :]))

        def finish_fine(dve, own, n):
            v, t = nc.vector, m.fine
            dve.wait_ge(from_pe, n)
            own(v.tensor_scalar(t.group_f[:, :], ps[:, 0:KV], float(G - 1), None, ALU.min))
            own(v.tensor_tensor(t.window_f[:, :], m.step_iota[:, 0:KV], t.group_f[:, :], ALU.subtract))
            own(v.tensor_copy(t.group[:, :], t.group_f[0:1, :]))
            own(v.tensor_copy(t.window[:, :], t.window_f[0:1, :]))
            own(v.tensor_scalar(t.first[:, :], t.window_f[:, :], float(D), None, ALU.mult))
            own(v.tensor_scalar(t.last[:, :], t.window_f[:, :], float(D), float(D - 1), ALU.mult, ALU.add))
            own(v.memset(t.same[:, 0:1], 0.0))
            own(v.tensor_tensor(t.same[:, 1:KV], t.window_f[:, 1:KV], t.window_f[:, 0:KV - 1], ALU.is_equal))

        @block.vector
        def _(dve):
            own = Own(dve, own_sem)
            v = nc.vector
            own(v.tensor_scalar(bounds[:, :], m.step_iota[:, 1:W], float(P), None, ALU.mult))
            own(v.tensor_copy(last_key[:, :], m.last_key[:, :]))
            own(v.tensor_tensor(flags[:, :, :], over(last_key[:, :].unsqueeze(2), (100, 2, W - 1)),
                                over(bounds[0:100, :].unsqueeze(1), (100, 2, W - 1)), ALU.is_ge))
            own(v.tensor_reduce(s.last_window[:, :], flags[:, :, :], AX.X, ALU.add))
            plan_steps(nc, own, s, m)
            v.memset(one[:, :], 1.0).then_inc(to_pe, 1)
            finish_steps(dve, own, m.by_dst, 1)
            own(v.tensor_scalar(fine_bounds[:, :], m.step_iota[:, 1:V], float(D), None, ALU.mult))
            own(v.tensor_tensor(fine_flags[:, :, :], over(last_key[:, :].unsqueeze(2), (100, 2, V - 1)),
                                over(fine_bounds[0:100, :].unsqueeze(1), (100, 2, V - 1)), ALU.is_ge))
            own(v.tensor_reduce(s.last_window[:, :], fine_flags[:, :, :], AX.X, ALU.add))
            plan_steps(nc, own, s, m, KV)
            v.memset(one[:, :], 1.0).then_inc(to_pe, 1)
            finish_fine(dve, own, 2)

            own(v.tensor_copy(key[:, :], m.src_run[:, :]))
            own(v.tensor_scalar(win[:, :], key[:, :], float(P), None, ALU.is_ge))
            for w in range(2, W):
                own(v.scalar_tensor_tensor(win[:, :], key[:, :], float(w * P), win[:, :], ALU.is_ge, ALU.add))
            own(v.tensor_copy(code[:, :, 2], m.dst_run[:, :]))
            own(v.scalar_tensor_tensor(code[:, :, 0], win[:, :], float(P), key[:, :], ALU.mult, ALU.subtract))
            own(v.tensor_scalar(mask[:, :], code[:, :, 2], 1.0 - OUT, None, ALU.mult))
            v.scalar_tensor_tensor(code[:, :, 1], win[:, :], float(D), mask[:, :], ALU.mult, ALU.add).then_inc(coded, 1)
            dve.wait_ge(coded, 1)
            for w in range(W):
                own(v.tensor_scalar(mask[:, :], win[:, :], float(w), None, ALU.is_equal))
                own(v.tensor_tensor_scan(count[:, w, :], one[:, :], mask[:, :], 0.0, ALU.mult, ALU.add))
            v.tensor_copy(totals[:, :], count[:, :, C - 1]).then_inc(to_pe, 1)
            dve.wait_ge(from_pe, 3)
            own(v.tensor_tensor_scan(cum[0:P, :], one[:, 0:W], ps[0:P, 0:W], 0.0, ALU.mult, ALU.add))
            own(v.tensor_tensor(base[0:P, :], cum[0:P, :], ps[0:P, 0:W], ALU.subtract))
            own(v.tensor_tensor(base[0:P, :], base[0:P, :], ps2[0:P, 0:W], ALU.add))
            own(v.tensor_tensor(base[0:P, :], base[0:P, :], totals[:, :], ALU.subtract))
            own(v.memset(place[:, :], -1.0))
            for w in range(W):
                own(v.tensor_scalar(count[:, w, :], count[:, w, :], base[0:P, w:w + 1], None, ALU.add))
                own(v.scalar_tensor_tensor(mask[:, :], win[:, :], float(w), count[:, w, :],
                                           ALU.is_equal, ALU.mult))
                own(v.tensor_tensor(place[:, :], place[:, :], mask[:, :], ALU.add))
            own(v.tensor_copy(m.place[:, :], place[:, :]))
            own(v.tensor_copy(m.record[:, :, 0], m.src_run[:, :]))
            own(v.tensor_copy(m.record[:, :, 1], m.dst_run[:, :]))
            own(v.tensor_tensor(flags[:, :, :], over(m.edge_iota[:, :].unsqueeze(2), (100, 2, W - 1)),
                                over(cum[0:100, 0:W - 1].unsqueeze(1), (100, 2, W - 1)), ALU.is_ge))
            own(v.tensor_reduce(s.last_window[:, :], flags[:, :, :], AX.X, ALU.add))
            plan_steps(nc, own, s, m)
            v.memset(one[:, :], 1.0).then_inc(to_pe, 1)
            finish_steps(dve, own, m.by_src, 4)

        @block.tensor
        def _(pe):
            def add_up(n, steps=K):
                pe.wait_ge(to_pe, n)
                nc.tensor.matmul(ps[:, 0:steps], m.ones[0:100, :], s.done[:, 0, 0:steps], start=True, stop=False)
                nc.tensor.matmul(ps[:, 0:steps], m.ones[0:100, :], s.done[:, 1, 0:steps], start=False,
                                 stop=True).then_inc(from_pe, 1)
            add_up(1)
            add_up(2, KV)
            pe.wait_ge(to_pe, 3)
            nc.tensor.matmul(ps[0:P, 0:W], m.ones[0:P, 0:P], totals[:, :], start=True, stop=True)
            nc.tensor.matmul(ps2[0:P, 0:W], m.upto[0:P, 0:P], totals[:, :], start=True,
                             stop=True).then_inc(from_pe, 1)
            add_up(4)

        @block.sync
        def _(sp):
            sp.wait_ge(coded, 1)
            sp.dma_start(m.codes[:, :].rearrange("(p c) a -> p c a", p=P), code[:, :, :]).then_inc(codes_written, 16)
            sp.wait_ge(codes_written, 16)


def scatter_and_tables(nc, m):
    with ExitStack() as stack:
        s = Scope(nc, stack, "l0tab", m.shared)
        slot_place = [s.sb(f"place{i}", [P, 8], I32) for i in range(2)]
        slot_record = [s.sb(f"record{i}", [P, 8, 2], I32) for i in range(2)]
        staged, sent, go = s.sem("staged"), s.pool_dma_sems("sent", 2), s.sem("go")
        tables = Tables(nc, s, m)
        count = Count(nc, s, m)
        block = stack.enter_context(nc.Block())

        @block.gpsimd
        def _(pool):
            def half(i, b):
                if not (isinstance(i, int) and i == 0):
                    pool.wait_ge(sent[b], 128 * i)
                nc.gpsimd.tensor_copy(slot_place[b][:, :], m.place[:, bass.ds(16 * i + 8 * b, 8)])
                nc.gpsimd.tensor_copy(slot_record[b][:, :, :],
                                      m.record[:, bass.ds(16 * i + 8 * b, 8), :]).then_inc(staged, 1)
                pool.wait_ge(staged, 2 * i + b + 1)
                pool.sem_inc(go, 1)
                for t in range(8):
                    pool.indirect_dma_start(
                        m.records[:, :], bass.IndirectOffsetOnAxis(ap=slot_place[b][:, t:t + 1], axis=0),
                        slot_record[b][:, t, :], None).then_inc(sent[b], 16)
            half(0, 0)
            half(0, 1)
            with pool.Fori(1, C // 16, 1) as i:
                half(i, 0)
                half(i, 1)
            for b in range(2):
                pool.wait_ge(sent[b], 128 * (C // 16))

        tables.write(block, m.x, m.wt0, m.at0, table_score=1, count=count)


class Count:

    def __init__(self, nc, s, m):
        self.nc, self.m = nc, m
        self.codes = [s.sb(f"codes{i}", [P, T, 3]) for i in range(SLOTS)]
        self.held = [s.sb(f"held{i}", [P, T]) for i in range(2)]
        self.key = [s.sb(f"key{i}", [P, T]) for i in range(2)]
        self.pair_hot = [s.sb(f"pair_hot{i}", [P, T, CW], BF16) for i in range(2)]
        self.src_hot = [s.sb(f"src_hot{i}", [P, T, P], BF16) for i in range(2)]
        self.off = [s.sb(f"off{i}", [P, T, P]) for i in range(2)]
        self.off_ready, self.src_hot_ready = s.sem("off_ready"), s.sem("src_hot_ready")
        self.sum = [s.sb(f"sum{i}", [P, 2, CW // 2]) for i in range(SLOTS)]
        self.ps = [s.ps(f"count_ps{i}", (128, 2, 512)) for i in range(2)]
        self.codes_in, self.sum_out = s.sems("codes_in", SLOTS), s.sems("sum_out", SLOTS)
        self.held_ready, self.key_ready, self.hot_ready = s.sem("held_ready"), s.sem("key_ready"), s.sem("hot_ready")
        self.count_ready, self.sum_ready, self.go = s.sem("count_ready"), s.sem("sum_ready"), s.sem("count_go")

    @staticmethod
    def uses(q, j):
        return q * (UV // SLOTS) + j // SLOTS

    def sp(self, sp):
        nc, m = self.nc, self.m

        def store(q, j, v):
            k = UV * q + j
            sp.wait_ge(self.sum_ready, k + 1)
            sp.sem_inc(self.go, 1)
            if not early(q, j, 1):
                pq, pj = (q, j - 1) if j else (q - 1, UV - 1)
                sp.wait_ge(self.sum_out[pj % SLOTS], 16 * (self.uses(pq, pj) + 1))
                sp.sem_inc(self.go, 1)
            sp.dma_start(m.counts[bass.ds(v, 1), :, :].rearrange("v i c -> i (v c)"),
                         self.sum[j % SLOTS][:, :, :].rearrange("p a c -> p (a c)")).then_inc(self.sum_out[j % SLOTS], 16)

        def step(q, j, values):
            k = UV * q + j
            g, v_before = values
            if not early(q, j):
                sp.wait_ge(self.hot_ready, k - 3)
                sp.sem_inc(self.go, 1)
                sp.wait_ge(self.off_ready, k - 3)
                sp.sem_inc(self.go, 1)
            sp.dma_start(self.codes[j % SLOTS][:, :, :],
                         m.codes[bass.ds(g * (P * T), P * T), :].rearrange("(p t) a -> p t a", t=T)
                         ).then_inc(self.codes_in[j % SLOTS], 16)
            if not early(q, j, 2):
                pq, pj = (q, j - 2) if j >= 2 else (q - 1, UV + j - 2)
                store(pq, pj, v_before)

        def load(q):
            out = []
            for j in range(UV):
                k = UV * q + j
                out.append([self.value(m.fine.group, k, G), None if early(q, j, 2) else self.value(m.fine.window, k - 2, V)])
            return out
        rounds(nc, sp, step, load, steps=KV, u=UV)
        for j in (UV - 2, UV - 1):
            store(KV // UV - 1, j, self.value(m.fine.window, KV - UV + j, V))
        for j in range(SLOTS):
            sp.wait_ge(self.sum_out[j], 16 * (KV // SLOTS))

    def value(self, table, k, n):
        _, values = self.nc.values_load_multi_w_load_instructions(
            table[0:1, bass.ds(k, 1)], engines=[mybir.EngineType.SP], min_val=0, max_val=n - 1,
            skip_runtime_bounds_check_because="order_edges counts groups and windows within their bounds")
        return values[0]

    def dve(self, dve):
        nc, m, v = self.nc, self.m, self.nc.vector

        def add(q, j):
            k, b = UV * q + j, j % 2
            dve.wait_ge(self.count_ready, k + 1)
            if early(q, j, 1):
                v.tensor_copy(self.sum[0][:, :, :], self.ps[0][0:P, :, 0:CW // 2]).then_inc(self.sum_ready, 1)
                return
            dve.wait_ge(self.sum_ready, k)
            if not early(q, j):
                dve.wait_ge(self.sum_out[j % SLOTS], 16 * self.uses(q, j))
            v.scalar_tensor_tensor(self.sum[j % SLOTS][:, :, :], self.sum[(j - 1) % SLOTS][:, :, :],
                                   m.fine.same[0:P, bass.ds(k, 1)], self.ps[b][0:P, :, 0:CW // 2],
                                   ALU.mult, ALU.add).then_inc(self.sum_ready, 1)

        def step(q, j):
            k, b = UV * q + j, j % 2
            codes = self.codes[j % SLOTS]
            dve.wait_ge(self.codes_in[j % SLOTS], 16 * (self.uses(q, j) + 1))
            v.tensor_scalar(self.held[b][:, :], codes[:, :, 2], m.fine.first[0:P, bass.ds(k, 1)],
                            m.fine.last[0:P, bass.ds(k, 1)], ALU.max, ALU.min).then_inc(self.held_ready, 1)
            if not early(q, j, 2):
                dve.wait_ge(self.count_ready, k - 1)
            dve.wait_ge(self.held_ready, k + 1)
            v.scalar_tensor_tensor(self.key[b][:, :], self.held[b][:, :], OUT, codes[:, :, 1],
                                   ALU.mult, ALU.add).then_inc(self.key_ready, 1)
            dve.wait_ge(self.key_ready, k + 1)
            for t in range(T):
                last = v.tensor_scalar(self.pair_hot[b][:, t, :], m.code_iota[:, :], m.fine.first[0:P, bass.ds(k, 1)],
                                       self.key[b][:, t:t + 1], ALU.add, ALU.is_equal)
            last.then_inc(self.hot_ready, 1)
            if not early(q, j, 1):
                add(*((q, j - 1) if j else (q - 1, UV - 1)))
        rounds(nc, dve, step, steps=KV, u=UV)
        add(KV // UV - 1, UV - 1)

    def act(self, act):
        nc, m = self.nc, self.m

        def step(q, j):
            k, b = UV * q + j, j % 2
            act.wait_ge(self.codes_in[j % SLOTS], 16 * (self.uses(q, j) + 1))
            for t in range(T):
                last = nc.scalar.activation(self.off[b][:, t, :], m.code_iota[:, 0:P], ACT.Abs,
                                            bias=self.codes[j % SLOTS][:, t, 0:1])
            last.then_inc(self.off_ready, 1)
            if not early(q, j, 2):
                act.wait_ge(self.count_ready, k - 1)
            act.wait_ge(self.off_ready, k + 1)
            nc.scalar.activation(self.src_hot[b][:, :, :], self.off[b][:, :, :], ACT.Relu, scale=-1.0,
                                 bias=m.ones[0:P, 0:1]).then_inc(self.src_hot_ready, 1)
        rounds(nc, act, step, steps=KV, u=UV)

    def pe(self, pe):
        nc = self.nc

        def step(q, j):
            k, b = UV * q + j, j % 2
            pe.wait_ge(self.src_hot_ready, k + 1)
            pe.wait_ge(self.hot_ready, k + 1)
            if not early(q, j, 2):
                pe.wait_ge(self.sum_ready, k - 1)
            for t in range(T):
                for c in range(2):
                    last = nc.tensor.matmul(self.ps[b][0:P, c, 0:CW // 2], self.src_hot[b][:, t, :],
                                            self.pair_hot[b][:, t, c * (CW // 2):(c + 1) * (CW // 2)],
                                            start=(t == 0), stop=(t == T - 1))
            last.then_inc(self.count_ready, 1)
        rounds(nc, pe, step, steps=KV, u=UV)


class Tables:

    def __init__(self, nc, s, m):
        self.nc, self.s, self.m = nc, s, m
        norm_scratch(s)
        self.vec = s.sb("vec", [F, 2 * H])
        self.rest = s.sb("rest", [P, W, H])
        s.rest = self.rest[:, :, :]
        self.ps_t = [s.ps(f"turned{i}") for i in range(2)]
        self.ps_v, self.ps_s = s.ps("vec_ps"), s.ps("score_ps")
        self.own_sem = s.sem("dve_step")
        self.h_ready, self.turned, self.copied = s.sem("h_ready"), s.sem("turned"), s.sem("copied")
        self.vec_ready, self.vec_copied = s.sem("vec_ready"), s.sem("vec_copied")
        self.scores_ready, self.rows_ready = s.sem("scores_ready"), s.sem("rows_ready")
        self.written = s.sem("written")
        self.graph_rows = s.sb("graph_rows", [P, W, R])

    def write(self, block, x, wt, at, table_score, count=None):
        nc, m, s = self.nc, self.m, self.s
        near = 1 - table_score

        @block.vector
        def _(dve):
            own = Own(dve, self.own_sem)
            v = nc.vector
            layer_norm(nc, own, s, x[:, :, :], m.h[:, :, :])
            v.tensor_copy(self.graph_rows[:, :, 0:F], m.h[:, :, :]).then_inc(self.h_ready, 1)
            dve.wait_ge(self.vec_ready, 1)
            v.tensor_copy(self.vec[:, :], self.ps_v[0:F, 0:2 * H]).then_inc(self.vec_copied, 1)
            dve.wait_ge(self.scores_ready, 1)
            both = self.ps_s[0:P, 0:W * 2 * H].rearrange("p (w a h) -> p w a h", a=2, h=H)
            own(v.tensor_copy(m.near[:, :, :], both[:, :, near, :]))
            own(v.tensor_copy(m.far[:, :, :], both[:, :, table_score, :]))
            v.tensor_copy(self.graph_rows[:, :, F:R], m.far[:, :, :]).then_inc(self.rows_ready, 1)
            split3(nc, own, s, m.near[:, :, :], [m.near_parts[:, :, i, 0:H] for i in range(3)])
            if count:
                count.dve(dve)

        @block.tensor
        def _(pe):
            for a in range(2):
                for h in range(H):
                    c = a * H + h
                    last = nc.tensor.matmul(self.ps_v[0:F, c:c + 1], wt[:, h * F:(h + 1) * F],
                                            at[:, c:c + 1], start=True, stop=True)
            last.then_inc(self.vec_ready, 1)
            pe.wait_ge(self.h_ready, 1)
            for c in range((W + 3) // 4):
                if c >= 2:
                    pe.wait_ge(self.copied, c - 1)
                for w in range(4 * c, min(4 * c + 4, W)):
                    o = (w % 4) * P
                    last = nc.tensor.transpose(self.ps_t[c % 2][0:F, o:o + P], m.h[:, w, :], m.ident[0:P, 0:P])
                last.then_inc(self.turned, 1)
            pe.wait_ge(self.vec_copied, 1)
            pe.wait_ge(self.copied, (W + 3) // 4)
            for w in range(W):
                last = nc.tensor.matmul(self.ps_s[0:P, w * 2 * H:(w + 1) * 2 * H], m.h_turned[:, w * P:(w + 1) * P],
                                        self.vec[:, :], start=True, stop=True)
            last.then_inc(self.scores_ready, 1)
            if count:
                count.pe(pe)

        @block.scalar
        def _(act):
            norm_root(nc, act, s, 1)
            for c in range((W + 3) // 4):
                act.wait_ge(self.turned, c + 1)
                n = P * (min(4 * c + 4, W) - 4 * c)
                nc.scalar.activation(m.h_turned[:, 4 * c * P:4 * c * P + n], self.ps_t[c % 2][0:F, 0:n],
                                     ACT.Copy).then_inc(self.copied, 1)
            if count:
                count.act(act)

        @block.sync
        def _(sp):
            sp.wait_ge(self.rows_ready, 1)
            sp.dma_start(m.table[:, :].rearrange("(w p) c -> p w c", p=P),
                         self.graph_rows[:, :, :]).then_inc(self.written, 16)
            sp.wait_ge(self.written, 16)
            if count:
                count.sp(sp)


def attend(nc, m, tag, steps, from_spill):
    near_cols = 2 * H if from_spill else H
    with ExitStack() as stack:
        s = Scope(nc, stack, tag, m.shared)
        pairs = [s.sb(f"pairs{i}", [P, 2 * T], I32) for i in range(4)]
        rows = [s.sb(f"rows{i}", [P, T, R]) for i in range(4)]
        rel = [s.sb(f"rel{i}", [P, T]) for i in range(4)]
        hot = [s.sb(f"hot{i}", [P, T, P]) for i in range(4)]
        hot_turned = [s.sb(f"hot_turned{i}", [P, T * P], BF16) for i in range(2)]
        z = [s.sb(f"z{i}", [P, T, H]) for i in range(2)]
        score = [s.sb(f"score{i}", [P, T, H]) for i in range(2)]
        msg = [s.sb(f"msg{i}", [P, T, HF + H]) for i in range(2)]
        att = [x[:, :, HF:HF + H] for x in msg]
        turn_ps = [s.ps(f"turn_ps{i}") for i in range(2)]
        near_ps = [s.ps(f"near_ps{i}") for i in range(2)]
        sum_ps = [s.ps(f"sum_ps{i}", (128, 2, 512)) for i in range(2)]
        base = m.sems.begin(gathers=not from_spill)
        keys_in, rows_in = m.sems.keys_in, m.sems.streamed if from_spill else m.sems.gathered
        (rel_ready, hot_ready, turned, turned_copied, near_ready, z_ready, leaky_ready, less_max, score_ready,
         att_ready, msg_ready, sums_ready, acc_ready, zeroed, gather_go, load_go) = (m.sems.by_name[n] for n in m.sems.NAMES)
        if from_spill:
            base = 0
        block = stack.enter_context(nc.Block())

        key_of = [(x[:, 0:T] if from_spill else x[:, 0:2 * T:2]) for x in pairs]
        rows_count = 16 if from_spill else 16 * T

        @block.sync
        def _(sp):
            def load(q, j):
                k = U * q + j
                g = load_group(nc, steps, k)
                if not early(q, j):
                    sp.wait_ge(hot_ready, k - 3)
                    sp.sem_inc(load_go, 1)
                    if from_spill:
                        sp.wait_ge(msg_ready, k - 3)
                    else:
                        sp.wait_ge(rows_in[j % SLOTS], base + 16 * T * uses(q, j))
                    sp.sem_inc(load_go, 1)
                if from_spill:
                    sp.dma_start(pairs[j % SLOTS][:, 0:T],
                                 m.dst[bass.ds(g * (P * T), P * T)].rearrange("(p t) -> p t", t=T)).then_inc(keys_in[j % SLOTS], 16)
                    sp.dma_start(rows[j % SLOTS][:, :, :],
                                 m.spill[bass.ds(g * (P * T), P * T), :].rearrange("(p t) c -> p t c", t=T)
                                 ).then_inc(rows_in[j % SLOTS], 16)
                else:
                    sp.dma_start(pairs[j % SLOTS][:, :],
                                 m.records[bass.ds(g * (P * T), P * T), :].rearrange("(p t) c -> p (t c)", t=T)
                                 ).then_inc(keys_in[j % SLOTS], 16)
            rounds(nc, sp, load)

        @block.gpsimd
        def _(pool):
            nc.gpsimd.memset(m.acc[:, :, :], 0.0).then_inc(zeroed, 1)
            if from_spill:
                return

            def gather(q, j):
                k = U * q + j
                pool.wait_ge(keys_in[j % SLOTS], 16 * (uses(q, j) + 1))
                if not early(q, j):
                    pool.wait_ge(msg_ready, k - 3)
                pool.sem_inc(gather_go, 1)
                for t in range(T):
                    pool.indirect_dma_start(
                        rows[j % SLOTS][:, t, :], None, m.table[:, :],
                        bass.IndirectOffsetOnAxis(ap=pairs[j % SLOTS][:, 2 * t + 1:2 * t + 2], axis=0)).then_inc(rows_in[j % SLOTS], 16)
            rounds(nc, pool, gather)

        @block.vector
        def _(dve):
            v = nc.vector

            def one_hot(q, j):
                k = U * q + j
                dve.wait_ge(keys_in[j % SLOTS], 16 * (uses(q, j) + 1))
                if not early(q, j):
                    dve.wait_ge(sums_ready, k - 3)
                v.tensor_scalar(rel[j % SLOTS][:, :], key_of[j % SLOTS], steps.first_node[0:P, bass.ds(k, 1)], None,
                                ALU.subtract).then_inc(rel_ready, 1)
                dve.wait_ge(rel_ready, k + 1)
                v.tensor_tensor(hot[j % SLOTS][:, :, :], over(rel[j % SLOTS][:, :].unsqueeze(2), (P, T, P)),
                                over(m.node_iota[:, :].unsqueeze(1), (P, T, P)), ALU.is_equal).then_inc(hot_ready, 1)

            def scores(q, j):
                k, b = U * q + j, j % 2
                dve.wait_ge(near_ready, k + 1)
                dve.wait_ge(rows_in[j % SLOTS], base + rows_count * (uses(q, j) + 1))
                near = near_ps[b][0:P, 0:T * near_cols].rearrange("p (t c) -> p t c", t=T)
                v.tensor_tensor(z[b][:, :, :], near[:, :, 0:H], rows[j % SLOTS][:, :, F:R], ALU.add).then_inc(z_ready, 1)
                dve.wait_ge(z_ready, k + 1)
                v.scalar_tensor_tensor(z[b][:, :, :], z[b][:, :, :], 0.2, z[b][:, :, :], ALU.mult,
                                       ALU.max).then_inc(leaky_ready, 1)
                dve.wait_ge(leaky_ready, k + 1)
                if not early(q, j, 2):
                    dve.wait_ge(att_ready, k - 1)
                if from_spill:
                    v.tensor_tensor(z[b][:, :, :], z[b][:, :, :], near[:, :, H:2 * H], ALU.subtract).then_inc(less_max, 1)
                    dve.wait_ge(less_max, k + 1)
                    v.tensor_scalar(score[b][:, :, :], z[b][:, :, :], 0.0, None, ALU.min).then_inc(score_ready, 1)
                else:
                    v.tensor_scalar(score[b][:, :, :], z[b][:, :, :], -2.0, 2.0, ALU.max, ALU.min).then_inc(score_ready, 1)

            def messages(q, j):
                k, b = U * q + j, j % 2
                dve.wait_ge(att_ready, k + 1)
                if not early(q, j, 2):
                    dve.wait_ge(sums_ready, k - 1)
                v.tensor_tensor(msg[b][:, :, 0:HF].rearrange("p t (h f) -> p t h f", h=H), over(rows[j % SLOTS][:, :, 0:F].unsqueeze(2), (P, T, H, F)),
                                over(att[b].unsqueeze(3), (P, T, H, F)), ALU.mult).then_inc(msg_ready, 1)

            def accumulate(q, j, w):
                k, b = U * q + j, j % 2
                dve.wait_ge(sums_ready, k + 1)
                if not early(q, j, 1):
                    dve.wait_ge(acc_ready, k)
                here = m.acc[:, bass.ds(w, 1), :].rearrange("p a (c f) -> p (a c) f", c=2)
                v.tensor_tensor(here, here, sum_ps[b][0:P, :, 0:HALF], ALU.add).then_inc(acc_ready, 1)

            def step(q, j, window_before):
                if after(q, j, 2):
                    one_hot(*after(q, j, 2))
                messages(q, j)
                if after(q, j):
                    scores(*after(q, j))
                if before(q, j):
                    accumulate(*before(q, j), window_before)
            dve.wait_ge(zeroed, 1)
            one_hot(0, 0)
            one_hot(0, 1)
            scores(0, 0)
            rounds(nc, dve, step, lambda q: load_windows(nc, mybir.EngineType.DVE, steps, U * q - 1))
            accumulate(Q - 1, U - 1, load_windows(nc, mybir.EngineType.DVE, steps, K - 1)[0])

        @block.tensor
        def _(pe):
            def turn(q, j):
                k, b = U * q + j, j % 2
                pe.wait_ge(hot_ready, k + 1)
                if not early(q, j, 2):
                    pe.wait_ge(turned_copied, k - 1)
                for t in range(T):
                    last = nc.tensor.transpose(turn_ps[b][0:P, t * P:(t + 1) * P], hot[j % SLOTS][:, t, :], m.ident[0:P, 0:P])
                last.then_inc(turned, 1)

            def near(q, j, w):
                k, b = U * q + j, j % 2
                pe.wait_ge(turned_copied, k + 1)
                if not early(q, j, 2):
                    pe.wait_ge(score_ready, k - 1)
                for t in range(T):
                    for i in range(3):
                        last = nc.tensor.matmul(near_ps[b][0:P, t * near_cols:(t + 1) * near_cols],
                                                hot_turned[b][:, t * P:(t + 1) * P],
                                                m.near_parts[:, bass.ds(w, 1), i, 0:near_cols].rearrange("p a c -> p (a c)"),
                                                start=(i == 0), stop=(i == 2))
                last.then_inc(near_ready, 1)

            def sums(q, j):
                k, b = U * q + j, j % 2
                pe.wait_ge(msg_ready, k + 1)
                if not early(q, j, 2):
                    pe.wait_ge(acc_ready, k - 1)
                for c in range(2):
                    for t in range(T):
                        last = nc.tensor.matmul(sum_ps[b][0:P, c, 0:HALF], hot[j % SLOTS][:, t, :],
                                                msg[b][:, t, c * HALF:(c + 1) * HALF], start=(t == 0), stop=(t == T - 1))
                last.then_inc(sums_ready, 1)

            def step(q, j, window_behind):
                if after(q, j):
                    near(*after(q, j), window_behind)
                if after(q, j, 2):
                    turn(*after(q, j, 2))
                sums(q, j)
            turn(0, 0)
            near(0, 0, load_windows(nc, mybir.EngineType.PE, steps, 0)[0])
            turn(0, 1)
            rounds(nc, pe, step, lambda q: load_windows(nc, mybir.EngineType.PE, steps, U * q + 1))

        @block.scalar
        def _(act):
            def copy(q, j):
                k, b = U * q + j, j % 2
                act.wait_ge(turned, k + 1)
                if not early(q, j, 2):
                    act.wait_ge(near_ready, k - 1)
                nc.scalar.activation(hot_turned[b][:, :], turn_ps[b][0:P, 0:T * P], ACT.Copy).then_inc(turned_copied, 1)

            def exponential(q, j):
                k, b = U * q + j, j % 2
                act.wait_ge(score_ready, k + 1)
                if not early(q, j, 2):
                    act.wait_ge(sums_ready, k - 1)
                nc.scalar.activation(att[b], score[b][:, :, :], ACT.Exp).then_inc(att_ready, 1)

            def step(q, j):
                if after(q, j):
                    copy(*after(q, j))
                exponential(q, j)
            copy(0, 0)
            rounds(nc, act, step)


def gather_sum(nc, m, tag, cols, edge_attr=None):
    with ExitStack() as stack:
        s = Scope(nc, stack, tag, m.shared)
        keys = [s.sb(f"keys{i}", [P, T], I32) for i in range(4)]
        sources = [s.sb(f"sources{i}", [P, T], I32) for i in range(4)]
        rows = [s.sb(f"rows{i}", [P, T, R]) for i in range(4)]
        rel = [s.sb(f"rel{i}", [P, T]) for i in range(4)]
        hot = [s.sb(f"hot{i}", [P, T, P]) for i in range(4)]
        attr = [s.sb(f"attr{i}", [P, T, F]) for i in range(4)] if edge_attr is not None else None
        msg = [s.sb(f"msg{i}", [P, T, F]) for i in range(4)] if edge_attr is not None else rows
        sum_ps = [s.ps(f"sum_ps{i}") for i in range(2)]
        base = m.sems.begin(gathers=True)
        keys_in, rows_in = m.sems.keys_in, m.sems.gathered
        rel_ready, hot_ready, msg_ready, sums_ready, acc_ready, zeroed, gather_go, load_go = (
            m.sems.by_name[n] for n in ("rel_ready", "hot_ready", "msg_ready", "sums_ready", "acc_ready", "zeroed",
                                        "gather_go", "load_go"))
        steps = m.by_dst
        loads = 48 if edge_attr is not None else 32
        block = stack.enter_context(nc.Block())

        @block.sync
        def _(sp):
            def load(q, j):
                k = U * q + j
                g = load_group(nc, steps, k)
                if not early(q, j):
                    sp.wait_ge(hot_ready, k - 3)
                    sp.sem_inc(load_go, 1)
                    sp.wait_ge(rows_in[j % SLOTS], base + 16 * T * uses(q, j))
                    if edge_attr is not None:
                        sp.sem_inc(load_go, 1)
                        sp.wait_ge(msg_ready, k - 3)
                    sp.sem_inc(load_go, 1)
                here = bass.ds(g * (P * T), P * T)
                sp.dma_start(sources[j % SLOTS][:, :], m.src[here].rearrange("(p t) -> p t", t=T)).then_inc(keys_in[j % SLOTS], 16)
                sp.dma_start(keys[j % SLOTS][:, :], m.dst[here].rearrange("(p t) -> p t", t=T)).then_inc(keys_in[j % SLOTS], 16)
                if edge_attr is not None:
                    sp.dma_start(attr[j % SLOTS][:, :, :], edge_attr[here, :].rearrange("(p t) f -> p t f", t=T)
                                 ).then_inc(keys_in[j % SLOTS], 16)
            rounds(nc, sp, load)

        @block.gpsimd
        def _(pool):
            nc.gpsimd.memset(m.acc[:, :, 0:cols], 0.0).then_inc(zeroed, 1)

            def gather(q, j):
                k = U * q + j
                pool.wait_ge(keys_in[j % SLOTS], loads * (uses(q, j) + 1))
                if not early(q, j):
                    pool.wait_ge(sums_ready if edge_attr is None else msg_ready, k - 3)
                pool.sem_inc(gather_go, 1)
                for t in range(T):
                    pool.indirect_dma_start(rows[j % SLOTS][:, t, :], None, m.table[:, :],
                                            bass.IndirectOffsetOnAxis(ap=sources[j % SLOTS][:, t:t + 1], axis=0)
                                            ).then_inc(rows_in[j % SLOTS], 16)
            rounds(nc, pool, gather)

        @block.vector
        def _(dve):
            v = nc.vector

            def accumulate(q, j, w):
                k, b = U * q + j, j % 2
                dve.wait_ge(sums_ready, k + 1)
                if not early(q, j, 1):
                    dve.wait_ge(acc_ready, k)
                v.tensor_tensor(m.acc[:, bass.ds(w, 1), 0:cols], m.acc[:, bass.ds(w, 1), 0:cols],
                                sum_ps[b][0:P, 0:cols].unsqueeze(1), ALU.add).then_inc(acc_ready, 1)

            def step(q, j, window_before):
                k = U * q + j
                dve.wait_ge(keys_in[j % SLOTS], loads * (uses(q, j) + 1))
                if not early(q, j):
                    dve.wait_ge(sums_ready, k - 3)
                v.tensor_scalar(rel[j % SLOTS][:, :], keys[j % SLOTS][:, :], steps.first_node[0:P, bass.ds(k, 1)], None,
                                ALU.subtract).then_inc(rel_ready, 1)
                dve.wait_ge(rel_ready, k + 1)
                v.tensor_tensor(hot[j % SLOTS][:, :, :], over(rel[j % SLOTS][:, :].unsqueeze(2), (P, T, P)),
                                over(m.node_iota[:, :].unsqueeze(1), (P, T, P)), ALU.is_equal).then_inc(hot_ready, 1)
                if edge_attr is not None:
                    dve.wait_ge(rows_in[j % SLOTS], base + 16 * T * (uses(q, j) + 1))
                    v.tensor_tensor(msg[j % SLOTS][:, :, :], rows[j % SLOTS][:, :, 0:F], attr[j % SLOTS][:, :, :], ALU.mult).then_inc(msg_ready, 1)
                if before(q, j):
                    accumulate(*before(q, j), window_before)
            dve.wait_ge(zeroed, 1)
            rounds(nc, dve, step, lambda q: load_windows(nc, mybir.EngineType.DVE, steps, U * q - 1))
            accumulate(Q - 1, U - 1, load_windows(nc, mybir.EngineType.DVE, steps, K - 1)[0])

        @block.tensor
        def _(pe):
            def step(q, j):
                k, b = U * q + j, j % 2
                pe.wait_ge(hot_ready, k + 1)
                if edge_attr is not None:
                    pe.wait_ge(msg_ready, k + 1)
                else:
                    pe.wait_ge(rows_in[j % SLOTS], base + 16 * T * (uses(q, j) + 1))
                if not early(q, j, 2):
                    pe.wait_ge(acc_ready, k - 1)
                for t in range(T):
                    last = nc.tensor.matmul(sum_ps[b][0:P, 0:cols], hot[j % SLOTS][:, t, :], msg[j % SLOTS][:, t, 0:cols],
                                            start=(t == 0), stop=(t == T - 1))
                last.then_inc(sums_ready, 1)
            rounds(nc, pe, step)


AT_ONCE = 3

def count_sum(nc, m, tag):
    chunks = [(w, min(AT_ONCE, W - w)) for w in range(0, W, AT_ONCE)]
    with ExitStack() as stack:
        s = Scope(nc, stack, tag, m.shared)
        h_one = s.sb("h_one", [P, W, F + 1])
        counts = [s.sb(f"counts{i}", [P, AT_ONCE * V // W, CW]) for i in range(2)]
        sums = [s.sb(f"sums{i}", [F + 1, AT_ONCE * P]) for i in range(2)]
        ps = [s.ps(f"ps{i}") for i in range(2)]
        turned_ps = [s.ps(f"turned_ps{i}") for i in range(2)]
        counts_in = s.sems("counts_in", 2)
        h_ready, sums_ready, sums_copied, turned, done = (
            s.sem(n) for n in ("h_ready", "sums_ready", "sums_copied", "turned", "done"))
        block = stack.enter_context(nc.Block())

        @block.sync
        def _(sp):
            for c, (w, n) in enumerate(chunks):
                if c >= 2:
                    sp.wait_ge(sums_ready, c - 1)
                sp.dma_start(counts[c % 2][:, 0:n * V // W, :], m.counts[w * (V // W):(w + n) * (V // W), :, :].rearrange(
                    "v i c -> i v c")).then_inc(counts_in[c % 2], 16)

        @block.vector
        def _(dve):
            nc.vector.memset(h_one[:, :, F:F + 1], 1.0)
            nc.vector.tensor_copy(h_one[:, :, 0:F], m.h[:, :, :]).then_inc(h_ready, 1)
            for c, (w, n) in enumerate(chunks):
                dve.wait_ge(turned, c + 1)
                nc.vector.tensor_copy(m.acc[:, w:w + n, 0:F + 1], turned_ps[c % 2][0:P, 0:n * (F + 1)].rearrange(
                    "p (w f) -> p w f", f=F + 1)).then_inc(done, 1)

        @block.scalar
        def _(act):
            for c, (w, n) in enumerate(chunks):
                act.wait_ge(sums_ready, c + 1)
                if c >= 2:
                    act.wait_ge(turned, c - 1)
                nc.scalar.activation(sums[c % 2][:, 0:n * P], ps[c % 2][0:F + 1, 0:n * P], ACT.Copy).then_inc(sums_copied, 1)

        @block.tensor
        def _(pe):
            def turn(c):
                w, n = chunks[c]
                pe.wait_ge(sums_copied, c + 1)
                if c >= 2:
                    pe.wait_ge(done, c - 1)
                for i in range(n):
                    last = nc.tensor.transpose(turned_ps[c % 2][0:P, i * (F + 1):(i + 1) * (F + 1)],
                                               sums[c % 2][:, i * P:(i + 1) * P], m.ident[0:F + 1, 0:F + 1])
                last.then_inc(turned, 1)
            pe.wait_ge(h_ready, 1)
            for c, (w, n) in enumerate(chunks):
                pe.wait_ge(counts_in[c % 2], 16 * (c // 2 + 1))
                if c >= 2:
                    pe.wait_ge(sums_copied, c - 1)
                for b in range(W):
                    last = nc.tensor.matmul(ps[c % 2][0:F + 1, 0:n * P], h_one[:, b, :],
                                            counts[c % 2][:, 0:n * V // W, b * D:(b + 1) * D],
                                            start=(b == 0), stop=(b == W - 1))
                last.then_inc(sums_ready, 1)
                if c:
                    turn(c - 1)
            turn(len(chunks) - 1)


class Heads:

    def __init__(self, nc, s, m):
        self.nc, self.s, self.m = nc, s, m
        self.ps_t = [s.ps(f"heads_t{i}") for i in range(2)]
        self.ps_o = [s.ps(f"heads_o{i}") for i in range(4)]
        self.turned_sb = [s.sb(f"heads_sb{i}", [128, 4 * P]) for i in range(2)]
        self.acc_ready, self.turned = s.sem("heads_acc_ready"), s.sem("heads_turned")
        self.copied, self.out_ready = s.sem("heads_copied"), s.sem("heads_out")

    def pe(self, pe, value):
        nc, m = self.nc, self.m
        pe.wait_ge(self.acc_ready, 1)

        def turn(w):
            if w >= 2:
                pe.wait_ge(self.copied, w - 1)
            for c in range(4):
                last = nc.tensor.transpose(self.ps_t[w % 2][:, c * P:(c + 1) * P], m.acc[:, w, c * 128:(c + 1) * 128],
                                           m.ident[0:P, 0:P])
            last.then_inc(self.turned, 1)
        turn(0)
        for w in range(W):
            if w + 1 < W:
                turn(w + 1)
            pe.wait_ge(self.copied, w + 1)
            for c in range(4):
                last = nc.tensor.matmul(self.ps_o[w // 8][0:P, (w % 8) * F:(w % 8 + 1) * F],
                                        self.turned_sb[w % 2][:, c * P:(c + 1) * P], value[:, c, :],
                                        start=(c == 0), stop=(c == 3))
            last.then_inc(self.out_ready, 1)

    def act(self, act):
        for w in range(W):
            act.wait_ge(self.turned, w + 1)
            if w >= 2:
                act.wait_ge(self.out_ready, w - 1)
            self.nc.scalar.activation(self.turned_sb[w % 2][:, :], self.ps_t[w % 2][:, 0:4 * P],
                                      ACT.Copy).then_inc(self.copied, 1)

    def banks(self):
        for b in range(4):
            n = min(8, W - 8 * b)
            yield 8 * b, n, self.ps_o[b][0:P, 0:n * F].rearrange("p (w f) -> p w f", f=F)


class Dense:

    def __init__(self, nc, s, m, ps_t, ps_o, tag):
        self.nc, self.m, self.ps_t, self.ps_o = nc, m, ps_t, ps_o
        self.turned_sb = s.sb(f"{tag}_sb", [128, W * P])
        self.ready, self.turned = s.sem(f"{tag}_in_ready"), s.sem(f"{tag}_turned")
        self.copied, self.out_ready = s.sem(f"{tag}_copied"), s.sem(f"{tag}_out")
        self.chunks = (W + 3) // 4

    def pe_turn(self, pe, cat, width):
        pe.wait_ge(self.ready, 1)
        for c in range(self.chunks):
            if c >= 2:
                pe.wait_ge(self.copied, c - 1)
            for w in range(4 * c, min(4 * c + 4, W)):
                o = (w % 4) * P
                last = self.nc.tensor.transpose(self.ps_t[c % 2][0:width, o:o + P], cat[:, w, 0:width], self.m.ident[0:P, 0:P])
            last.then_inc(self.turned, 1)

    def pe_out(self, pe, width, weight):
        pe.wait_ge(self.copied, self.chunks)
        for w in range(W):
            last = self.nc.tensor.matmul(self.ps_o[w // 8][0:P, (w % 8) * F:(w % 8 + 1) * F],
                                         self.turned_sb[0:width, w * P:(w + 1) * P], weight, start=True, stop=True)
        last.then_inc(self.out_ready, 1)

    def act(self, act, width):
        for c in range(self.chunks):
            act.wait_ge(self.turned, c + 1)
            n = P * (min(4 * c + 4, W) - 4 * c)
            self.nc.scalar.activation(self.turned_sb[0:width, 4 * c * P:4 * c * P + n], self.ps_t[c % 2][0:width, 0:n],
                                      ACT.Copy).then_inc(self.copied, 1)

    def banks(self):
        for b in range(4):
            n = min(8, W - 8 * b)
            yield 8 * b, n, self.ps_o[b][0:P, 0:n * F].rearrange("p (w f) -> p w f", f=F)


def finish_layer0(nc, m):
    with ExitStack() as stack:
        s = Scope(nc, stack, "l0end", m.shared)
        norm_scratch(s)
        heads = Heads(nc, s, m)
        value = s.sb("value", [128, 4, F])
        inv = s.sb("inv", [P, W, H])
        y = s.sb("y", [P, W, F])
        graph_rows = s.sb("graph_rows", [P, W, F + 1])
        value_ps = s.ps("value_ps")
        own_sem, value_ready, value_copied = s.sem("dve_step"), s.sem("value_ready"), s.sem("value_copied")
        rows_ready, written = s.sem("rows_ready"), s.sem("written")
        block = stack.enter_context(nc.Block())

        @block.vector
        def _(dve):
            own, v = Own(dve, own_sem), nc.vector
            own(v.tensor_scalar(inv[:, :, :], m.acc[:, :, HF:HF + H], 1e-30, None, ALU.max))
            own(v.reciprocal(inv[:, :, :], inv[:, :, :]))
            for h in range(H):
                cols = m.acc[:, :, h * F:(h + 1) * F]
                last = v.tensor_tensor(cols, cols, over(inv[:, :, h].unsqueeze(2), (P, W, F)), ALU.mult)
                if h < H - 1:
                    own(last)
            last.then_inc(heads.acc_ready, 1)
            dve.wait_ge(heads.out_ready, W)
            for w0, n, out in heads.banks():
                yb = y[:, w0:w0 + n, :]
                own(v.tensor_copy(yb, out))
                own(v.scalar_tensor_tensor(yb, yb, 0.2, yb, ALU.mult, ALU.max))
                own(v.tensor_tensor(m.x[:, w0:w0 + n, :], m.x[:, w0:w0 + n, :], yb, ALU.add))
            layer_norm(nc, own, s, m.x[:, :, :], m.h[:, :, :])
            own(v.tensor_copy(graph_rows[:, :, 0:F], m.h[:, :, :]))
            v.memset(graph_rows[:, :, F:F + 1], 1.0).then_inc(rows_ready, 1)

        @block.tensor
        def _(pe):
            for h in range(H):
                o, c = (h % 2) * F, h // 2
                last = nc.tensor.matmul(value_ps[o:o + F, c * F:(c + 1) * F], m.wt0[:, h * F:(h + 1) * F],
                                        m.merge[:, h, :], start=True, stop=True)
            last.then_inc(value_ready, 1)
            pe.wait_ge(value_copied, 1)
            heads.pe(pe, value)

        @block.scalar
        def _(act):
            act.wait_ge(value_ready, 1)
            nc.scalar.activation(value[:, :, :], value_ps[:, 0:4 * F].rearrange("p (c f) -> p c f", f=F),
                                 ACT.Copy).then_inc(value_copied, 1)
            heads.act(act)
            norm_root(nc, act, s, 1)

        @block.sync
        def _(sp):
            sp.wait_ge(rows_ready, 1)
            sp.dma_start(m.table[:, 0:F + 1].rearrange("(w p) c -> p w c", p=P), graph_rows[:, :, :]).then_inc(written, 16)
            sp.wait_ge(written, 16)


def finish_mean(nc, m, tag, weight, bias, kind):
    with ExitStack() as stack:
        s = Scope(nc, stack, tag, m.shared)
        norm_scratch(s)
        cat = s.sb("cat", [P, W, 2 * F])
        inv = s.sb("inv", [P, W])
        ps_t = [s.ps(f"ps_t{i}") for i in range(2)]
        ps_o = [s.ps(f"ps_o{i}") for i in range(4)]
        dense = Dense(nc, s, m, ps_t, ps_o, "dense")
        own_sem, rows_ready, written = s.sem("dve_step"), s.sem("rows_ready"), s.sem("written")
        block = stack.enter_context(nc.Block())

        @block.vector
        def _(dve):
            own, v = Own(dve, own_sem), nc.vector
            if kind == "hidden":
                own(v.tensor_copy(m.degree[:, :], m.acc[:, :, F]))
            own(v.tensor_scalar(inv[:, :], m.degree[:, :], 1.0, None, ALU.max))
            own(v.reciprocal(inv[:, :], inv[:, :]))
            own(v.tensor_tensor(cat[:, :, 0:F], m.acc[:, :, 0:F], over(inv[:, :].unsqueeze(2), (P, W, F)), ALU.mult))
            v.tensor_copy(cat[:, :, F:2 * F], m.h[:, :, :]).then_inc(dense.ready, 1)
            dve.wait_ge(dense.out_ready, 1)
            for w0, n, out in dense.banks():
                b = over(bias.unsqueeze(1), (P, n, F))
                if kind == "hidden":
                    own(v.tensor_tensor(m.h[:, w0:w0 + n, :], out, b, ALU.add))
                else:
                    own(v.tensor_tensor(cat[:, w0:w0 + n, 0:F], out, b, ALU.add))
                    own(v.tensor_tensor(m.x[:, w0:w0 + n, :], m.x[:, w0:w0 + n, :], cat[:, w0:w0 + n, 0:F], ALU.add))
            if kind == "hidden":
                own(v.tensor_scalar(m.h[:, :, :], m.h[:, :, :], 0.0, None, ALU.max))
            if kind == "last":
                layer_norm(nc, own, s, m.x[:, :, :], m.h[:, :, :])
            v.memset(inv[:, :], 0.0).then_inc(rows_ready, 1)

        @block.tensor
        def _(pe):
            dense.pe_turn(pe, cat, 2 * F)
            dense.pe_out(pe, 2 * F, weight)

        @block.scalar
        def _(act):
            dense.act(act, 2 * F)
            if kind == "last":
                norm_root(nc, act, s, 1)

        if kind != "edges":
            @block.sync
            def _(sp):
                sp.wait_ge(rows_ready, 1)
                sp.dma_start(m.table[:, 0:F].rearrange("(w p) c -> p w c", p=P), m.h[:, :, :]).then_inc(written, 16)
                sp.wait_ge(written, 16)


def tables3(nc, m):
    with ExitStack() as stack:
        s = Scope(nc, stack, "l3tab", m.shared)
        tables = Tables(nc, s, m)
        block = stack.enter_context(nc.Block())
        tables.write(block, m.x, m.wt3, m.at3, table_score=0)


def gather_rows3(nc, m):
    with ExitStack() as stack:
        s = Scope(nc, stack, "l3rows", m.shared)
        index = [s.sb(f"index{i}", [P, 8], I32) for i in range(2)]
        rows = [s.sb(f"rows{i}", [P, 8, R]) for i in range(2)]
        staged, kept, go = s.sem("staged"), s.sem("kept"), s.sem("go")
        gathered, spilled = s.pool_dma_sems("gathered", 2), s.sems("spilled", 2)
        block = stack.enter_context(nc.Block())
        spill = m.spill[:, :].rearrange("(p c) r -> p c r", p=P)

        @block.gpsimd
        def _(pool):
            def half(i, b):
                if not (isinstance(i, int) and i == 0):
                    pool.wait_ge(gathered[b], 128 * i)
                    pool.wait_ge(spilled[b], 16 * i)
                    pool.wait_ge(kept, 2 * i + b - 1)
                nc.gpsimd.tensor_copy(index[b][:, :], m.src_run[:, bass.ds(16 * i + 8 * b, 8)]).then_inc(staged, 1)
                pool.wait_ge(staged, 2 * i + b + 1)
                pool.sem_inc(go, 1)
                for t in range(8):
                    pool.indirect_dma_start(rows[b][:, t, :], None, m.table[:, :],
                                            bass.IndirectOffsetOnAxis(ap=index[b][:, t:t + 1], axis=0)
                                            ).then_inc(gathered[b], 16)
            half(0, 0)
            half(0, 1)
            with pool.Fori(1, C // 16, 1) as i:
                half(i, 0)
                half(i, 1)

        @block.sync
        def _(sp):
            with sp.Fori(0, C // 16, 1) as i:
                for b in range(2):
                    sp.wait_ge(gathered[b], 128 * (i + 1))
                    sp.dma_start(spill[:, bass.ds(16 * i + 8 * b, 8), :], rows[b][:, :, :]).then_inc(spilled[b], 16)
            for b in range(2):
                sp.wait_ge(spilled[b], 16 * (C // 16))

        @block.vector
        def _(dve):
            with dve.Fori(0, C // 16, 1) as i:
                for b in range(2):
                    dve.wait_ge(gathered[b], 128 * (i + 1))
                    nc.vector.tensor_copy(m.edge_score[:, bass.ds(16 * i + 8 * b, 8), :],
                                          rows[b][:, :, F:R]).then_inc(kept, 1)


def maxima3(nc, m):
    with ExitStack() as stack:
        s = Scope(nc, stack, "l3max", m.shared)
        key, neq, same0 = s.sb("key", [P, C]), s.sb("neq", [P, C]), s.sb("same0", [P, C])
        run = s.sb("run", [P, C, H])
        ends = s.sb("ends", [P, 4])
        edge_turn = s.sb("edge_turn", [4, 128])
        prev_last = s.sb("prev_last", [P, 1])
        cont, whole = s.sb("cont", [P, 1]), s.sb("whole", [P, 1])
        pack = s.sb("pack", [P, 4, H])
        turned = s.sb("turned", [H, 4, 128])
        carry = s.sb("carry", [H, 128])
        carry_in = s.sb("carry_in", [H, 128])
        carry_p = s.sb("carry_p", [P, H])
        last_f = s.sb("last_f", [P, W])
        cum = s.sb("cum", [P, W])
        last_i = s.sb("last_i", [P, W], I32)
        found = s.sb("found", [P, W, H])
        hole = s.sb("hole", [P, W])
        rest = s.sb("rest", [P, W, H])
        s.rest = rest[:, :, :]
        ps = s.ps("sums")
        ps2 = s.ps("before")
        ps3 = [s.ps(f"turn{i}") for i in range(4)]
        own_sem = s.sem("dve_step")
        to_pe, from_pe = s.sem("operands_ready"), s.sem("products_ready")
        run_ready, run_written, found_in, index_ready = s.sem("run_ready"), s.sem("run_written"), s.pool_dma_sems("found_in", 1)[0], s.sem("index_ready")
        block = stack.enter_context(nc.Block())

        @block.vector
        def _(dve):
            own, v = Own(dve, own_sem), nc.vector
            v.tensor_copy(key[:, :], m.dst_run[:, :]).then_inc(to_pe, 1)
            dve.wait_ge(from_pe, 1)
            own(v.tensor_tensor_scan(cum[:, :], m.ones[0:P, 0:W], ps[0:P, 0:W], 0.0, ALU.mult, ALU.add))
            own(v.tensor_tensor(cum[:, :], cum[:, :], ps[0:P, 0:W], ALU.subtract))
            own(v.tensor_tensor(last_f[:, :], cum[:, :], ps2[0:P, 0:W], ALU.add))
            own(v.tensor_scalar(last_f[:, :], last_f[:, :], -1.0, 0.0, ALU.add, ALU.max))
            v.tensor_copy(last_i[:, :], last_f[:, :]).then_inc(index_ready, 1)
            own(v.memset(neq[:, 0:1], -FAR))
            own(v.tensor_tensor(neq[:, 1:C], key[:, 1:C], key[:, 0:C - 1], ALU.not_equal))
            own(v.tensor_scalar(neq[:, 1:C], neq[:, 1:C], -FAR, None, ALU.mult))
            for h in range(H):
                own(v.tensor_tensor_scan(run[:, :, h], neq[:, :], m.edge_score[:, :, h], -FAR, ALU.add, ALU.max))
            own(v.tensor_copy(pack[:, 0, :], run[:, C - 1, :]))
            own(v.tensor_copy(pack[:, 1, :], over(key[:, 0:1], (P, H))))
            v.tensor_copy(pack[:, 2, :], over(key[:, C - 1:C], (P, H))).then_inc(to_pe, 1)
            dve.wait_ge(from_pe, 2)
            for i in range(3):
                own(v.tensor_copy(turned[:, i, 0:P], ps3[i][0:H, 0:P]))
            last, first, final = turned[:, 0, 0:P], turned[:, 1, 0:P], turned[:, 2, 0:P]
            gate = turned[:, 3, 0:P]
            own(v.memset(carry_in[:, :], -FAR))
            own(v.memset(gate, -FAR))
            own(v.tensor_tensor(turned[:, 3, 1:P], turned[:, 1, 1:P], turned[:, 2, 0:P - 1], ALU.not_equal))
            own(v.tensor_scalar(turned[:, 3, 1:P], turned[:, 3, 1:P], -FAR, None, ALU.mult))
            own(v.tensor_tensor(final, first, final, ALU.not_equal))
            own(v.scalar_tensor_tensor(final, final, -FAR, gate, ALU.mult, ALU.min))
            own(v.tensor_tensor_scan(carry[:, 0:P], final, last, -FAR, ALU.add, ALU.max))
            own(v.tensor_tensor(carry_in[:, 1:P], carry[:, 0:P - 1], turned[:, 3, 1:P], ALU.add))
            v.tensor_scalar(carry_in[:, 0:P], carry_in[:, 0:P], -FAR, None, ALU.max).then_inc(to_pe, 1)
            own(v.tensor_scalar(same0[:, :], key[:, :], key[:, 0:1], -FAR, ALU.not_equal, ALU.mult))
            dve.wait_ge(from_pe, 3)
            own(v.tensor_copy(carry_p[:, :], ps3[3][0:P, 0:H]))
            for h in range(H):
                last_op = v.scalar_tensor_tensor(run[:, :, h], same0[:, :], carry_p[:, h:h + 1], run[:, :, h],
                                                 ALU.add, ALU.max)
                if h < H - 1:
                    own(last_op)
            last_op.then_inc(run_ready, 1)
            own(v.tensor_scalar(hole[:, :], m.degree[:, :], 0.0, None, ALU.is_equal))
            dve.wait_ge(found_in, 16 * W)
            own(v.tensor_scalar(hole[:, :], hole[:, :], -FAR, None, ALU.mult))
            own(v.tensor_tensor(found[:, :, :], found[:, :, :], over(hole[:, :].unsqueeze(2), (P, W, H)), ALU.add))
            own(v.tensor_tensor(found[:, :, :], found[:, :, :], m.far[:, :, :], ALU.max))
            own(v.tensor_tensor(found[:, :, :], found[:, :, :], m.near[:, :, :], ALU.add))
            own(v.scalar_tensor_tensor(found[:, :, :], found[:, :, :], 0.2, found[:, :, :], ALU.mult, ALU.max))
            split3(nc, own, s, found[:, :, :], [m.near_parts[:, :, i, H:2 * H] for i in range(3)])
            own(v.tensor_tensor(rest[:, :, :], m.near[:, :, :], m.far[:, :, :], ALU.add))
            own(v.scalar_tensor_tensor(rest[:, :, :], rest[:, :, :], 0.2, rest[:, :, :], ALU.mult, ALU.max))
            own(v.tensor_tensor(m.loop_att[:, :, :], rest[:, :, :], found[:, :, :], ALU.subtract))

        @block.tensor
        def _(pe):
            pe.wait_ge(to_pe, 1)
            nc.tensor.matmul(ps[0:P, 0:W], m.ones[0:P, 0:P], m.degree[:, :], start=True, stop=True)
            nc.tensor.matmul(ps2[0:P, 0:W], m.upto[0:P, 0:P], m.degree[:, :], start=True, stop=True).then_inc(from_pe, 1)
            pe.wait_ge(to_pe, 2)
            for i in range(3):
                last = nc.tensor.transpose(ps3[i][0:H, 0:P], pack[:, i, :], m.ident[0:P, 0:P])
            last.then_inc(from_pe, 1)
            pe.wait_ge(to_pe, 3)
            nc.tensor.transpose(ps3[3][0:P, 0:H], carry_in[:, 0:P], m.ident[0:H, 0:H]).then_inc(from_pe, 1)

        @block.sync
        def _(sp):
            sp.wait_ge(run_ready, 1)
            sp.dma_start(m.running[:, :].rearrange("(p c) h -> p c h", p=P), run[:, :, :]).then_inc(run_written, 16)

        @block.gpsimd
        def _(pool):
            pool.wait_ge(index_ready, 1)
            pool.wait_ge(run_written, 16)
            for w in range(W):
                pool.indirect_dma_start(found[:, w, :], None, m.running[:, :],
                                        bass.IndirectOffsetOnAxis(ap=last_i[:, w:w + 1], axis=0)).then_inc(found_in, 16)
            pool.wait_ge(found_in, 16 * W)


def finish_layer3(nc, m, io, out):
    with ExitStack() as stack:
        s = Scope(nc, stack, "l3end", m.shared)
        norm_scratch(s)
        heads = Heads(nc, s, m)
        loop = s.sb("loop", [P, W, H])
        inv = s.sb("inv", [P, W, H])
        y = s.sb("y", [P, W, F])
        x1 = s.sb("x1", [P, W, F])
        hidden = s.sb("hidden", [2 * F, W * P])
        dense1 = Dense(nc, s, m, heads.ps_t, heads.ps_o, "ffn")
        own_sem, exp_ready, ff_ready, ff_psum = s.sem("dve_step"), s.sem("exp_ready"), s.sem("ff_ready"), s.sem("ff_psum")
        ff_out, result_ready, written = s.sem("ff_out"), s.sem("result_ready"), s.sem("written")
        block = stack.enter_context(nc.Block())
        bias_att, b2, g1, c1, g2, c2 = (m.rows[:, i * F:(i + 1) * F] for i in range(3, 9))
        chunks = (W + 3) // 4

        def rowwise(ap, n=W):
            return over(ap.unsqueeze(1), (P, n, F))

        @block.vector
        def _(dve):
            own, v = Own(dve, own_sem), nc.vector
            dve.wait_ge(exp_ready, 1)
            own(v.tensor_tensor(inv[:, :, :], m.acc[:, :, HF:HF + H], loop[:, :, :], ALU.add))
            own(v.tensor_scalar(inv[:, :, :], inv[:, :, :], 1e-16, None, ALU.add))
            own(v.reciprocal(inv[:, :, :], inv[:, :, :]))
            own(v.tensor_scalar(inv[:, :, :], inv[:, :, :], 1.0 / H, None, ALU.mult))
            for h in range(H):
                cols = m.acc[:, :, h * F:(h + 1) * F]
                own(v.tensor_tensor(y[:, :, :], m.h[:, :, :], over(loop[:, :, h].unsqueeze(2), (P, W, F)), ALU.mult))
                own(v.tensor_tensor(cols, cols, y[:, :, :], ALU.add))
                last = v.tensor_tensor(cols, cols, over(inv[:, :, h].unsqueeze(2), (P, W, F)), ALU.mult)
                if h < H - 1:
                    own(last)
            last.then_inc(heads.acc_ready, 1)
            dve.wait_ge(heads.out_ready, W)
            own(v.tensor_tensor(y[:, :, :], m.h[:, :, :], rowwise(bias_att), ALU.add))
            for w0, n, o in heads.banks():
                own(v.tensor_tensor(y[:, w0:w0 + n, :], y[:, w0:w0 + n, :], o, ALU.add))
            layer_norm(nc, own, s, y[:, :, :], x1[:, :, :], relu=False)
            own(v.tensor_tensor(x1[:, :, :], x1[:, :, :], rowwise(g1), ALU.mult))
            v.tensor_tensor(x1[:, :, :], x1[:, :, :], rowwise(c1), ALU.add).then_inc(dense1.ready, 1)
            dve.wait_ge(dense1.ready, 1)
            dve.wait_ge(ff_out, 1)
            own(v.tensor_tensor(y[:, :, :], x1[:, :, :], rowwise(b2), ALU.add))
            for w0, n, o in heads.banks():
                own(v.tensor_tensor(y[:, w0:w0 + n, :], y[:, w0:w0 + n, :], o, ALU.add))
            layer_norm(nc, own, s, y[:, :, :], x1[:, :, :], relu=False)
            own(v.tensor_tensor(x1[:, :, :], x1[:, :, :], rowwise(g2), ALU.mult))
            own(v.tensor_tensor(x1[:, :, :], x1[:, :, :], rowwise(c2), ALU.add))
            v.tensor_tensor(x1[:, :, :], x1[:, :, :], m.x[:, :, :], ALU.add).then_inc(result_ready, 1)

        @block.tensor
        def _(pe):
            heads.pe(pe, m.value3)
            dense1.pe_turn(pe, x1, F)
            pe.wait_ge(dense1.copied, chunks)
            for c in range(chunks):
                if c >= 2:
                    pe.wait_ge(ff_ready, c - 1)
                n = P * (min(4 * c + 4, W) - 4 * c)
                nc.tensor.matmul(heads.ps_t[c % 2][:, 0:n], m.ff1[:, :], dense1.turned_sb[0:F, 4 * c * P:4 * c * P + n],
                                 start=True, stop=True).then_inc(ff_psum, 1)
            pe.wait_ge(ff_ready, chunks)
            for w in range(W):
                last = nc.tensor.matmul(heads.ps_o[w // 8][0:P, (w % 8) * F:(w % 8 + 1) * F],
                                        hidden[:, w * P:(w + 1) * P], m.ff2[:, :], start=True, stop=True)
            last.then_inc(ff_out, 1)

        @block.scalar
        def _(act):
            nc.scalar.activation(loop[:, :, :], m.loop_att[:, :, :], ACT.Exp).then_inc(exp_ready, 1)
            heads.act(act)
            norm_root(nc, act, s, 1)
            dense1.act(act, F)
            for c in range(chunks):
                act.wait_ge(ff_psum, c + 1)
                n = P * (min(4 * c + 4, W) - 4 * c)
                nc.scalar.activation(hidden[:, 4 * c * P:4 * c * P + n], heads.ps_t[c % 2][:, 0:n], ACT.Relu,
                                     bias=m.ff1_b[:, 0:1]).then_inc(ff_ready, 1)
            norm_root(nc, act, s, 2)

        @block.sync
        def _(sp):
            sp.wait_ge(result_ready, 1)
            sp.dma_start(out.rearrange("(w p) f -> p w f", p=P), x1[:, :, :]).then_inc(written, 16)
            sp.wait_ge(written, 16)


class Memory:
    pass


LAYERS = 4


def program(nc, io, out):
    m = Memory()
    with ExitStack() as stack:
        def sb(name, shape, dt=F32):
            return stack.enter_context(nc.sbuf_tensor(name, shape, dt))

        m.x, m.h = sb("x", [P, W, F]), sb("h", [P, W, F])
        m.h_turned = sb("h_turned", [F, N])
        m.src_run, m.dst_run = sb("src_run", [P, C], I32), sb("dst_run", [P, C], I32)
        m.last_key = sb("last_key", [100, 2], I32)
        m.wt0, m.at0, m.merge = sb("wt0", [F, HF]), sb("at0", [F, 2 * H]), sb("merge", [F, H, F])
        m.wt3, m.at3, m.value3 = sb("wt3", [F, HF]), sb("at3", [F, 2 * H]), sb("value3", [2 * F, 4, F])
        m.sage1, m.sage2, m.edge_w = (sb(n, [2 * F, F]) for n in ("sage1", "sage2", "edge_w"))
        m.ff1, m.ff1_b, m.ff2 = sb("ff1", [F, 2 * F]), sb("ff1_b", [2 * F, 1]), sb("ff2", [2 * F, F])
        m.rows = sb("rows", [P, 9 * F])
        m.ident, m.ones, m.upto = (sb(n, [128, 128]) for n in ("ident", "ones", "upto"))
        m.node_iota, m.step_iota = sb("node_iota", [P, P]), sb("step_iota", [128, KV])
        m.code_iota = sb("code_iota", [P, CW], F16)
        m.group_iota, m.edge_iota = sb("group_iota", [100, 2]), sb("edge_iota", [100, 2])
        for name in ("by_dst", "by_src"):
            t = Memory()
            t.group_f, t.window_f, t.first_node = (sb(f"{name}_{n}", [128, K]) for n in ("group_f", "window_f", "first"))
            t.group, t.window = sb(f"{name}_group", [1, K], I32), sb(f"{name}_window", [1, K + 2 * PAD], I32)
            if name == "by_dst":
                m.by_dst = t
            else:
                m.by_src = t
        m.fine = Memory()
        m.fine.group_f, m.fine.window_f, m.fine.first, m.fine.last, m.fine.same = (
            sb(f"fine_{n}", [128, KV]) for n in ("group_f", "window_f", "first", "last", "same"))
        m.fine.group, m.fine.window = sb("fine_group", [1, KV], I32), sb("fine_window_i", [1, KV], I32)
        m.near, m.far = sb("near", [P, W, H]), sb("far", [P, W, H])
        m.near_parts = sb("near_parts", [P, W, 3, 2 * H], BF16)
        m.degree, m.loop_att = sb("degree", [P, W]), sb("loop_att", [P, W, H])
        m.src, m.dst = io["src"], io["dst"]
        m.records = nc.dram_tensor("records", (E, 2), I32, kind="Internal").ap()
        m.codes = nc.dram_tensor("codes", (E, 3), F32, kind="Internal").ap()
        m.counts = nc.dram_tensor("counts", (V, P, CW), F32, kind="Internal").ap()
        m.table = nc.dram_tensor("table", (N, R), F32, kind="Internal").ap()
        m.spill = nc.dram_tensor("spill", (E, R), F32, kind="Internal").ap()
        m.running = nc.dram_tensor("running", (E, H), F32, kind="Internal").ap()

        m.sems, m.shared = StepSems(nc, stack), SharedSems(nc, stack, 48)
        set_up(nc, m, io)
        with ExitStack() as early:
            m.place = early.enter_context(nc.sbuf_tensor("place", [P, C], I32))
            m.record = early.enter_context(nc.sbuf_tensor("record", [P, C, 2], I32))
            order_edges(nc, m)
            scatter_and_tables(nc, m)
        with ExitStack() as rest:
            m.acc = rest.enter_context(nc.sbuf_tensor("acc", [P, W, HF + H], F32))
            attend(nc, m, "l0", m.by_src, from_spill=False)
            finish_layer0(nc, m)
            if LAYERS >= 2:
                count_sum(nc, m, "l1a")
                finish_mean(nc, m, "l1a_end", m.sage1[:, :], m.rows[:, 0:F], "hidden")
                count_sum(nc, m, "l1b")
                finish_mean(nc, m, "l1b_end", m.sage2[:, :], m.rows[:, F:2 * F], "last")
            if LAYERS >= 3:
                gather_sum(nc, m, "l2", F, io["edge_attr"])
                finish_mean(nc, m, "l2_end", m.edge_w[:, :], m.rows[:, 2 * F:3 * F], "edges")
            if LAYERS >= 4:
                tables3(nc, m)
                with ExitStack() as scores:
                    m.edge_score = scores.enter_context(nc.sbuf_tensor("edge_score", [P, C, H], F32))
                    gather_rows3(nc, m)
                    maxima3(nc, m)
                attend(nc, m, "l3", m.by_dst, from_spill=True)
                finish_layer3(nc, m, io, out)
            else:
                with ExitStack() as st:
                    w = st.enter_context(nc.semaphore("dbg"))
                    block = st.enter_context(nc.Block())

                    @block.sync
                    def _(sp):
                        sp.dma_start(out.rearrange("(w p) f -> p w f", p=P), m.x[:, :, :]).then_inc(w, 16)
                        sp.wait_ge(w, 16)


def kernel(**inputs):
    import numpy as np
    import concourse.bacc as bacc
    from concourse.bass_utils import run_bass_kernel_spmd

    a = {k: np.asarray(v) for k, v in inputs.items()}
    a0, w0 = a["L0_gnn_a"], a["L0_gnn_W"]
    w3 = a["L3_gnn_W_att"]
    arrays = {
        "x": a["x"], "src": a["src"], "dst": a["dst"], "edge_attr": a["edge_attr_64"],
        "wt0": w0.transpose(2, 0, 1).reshape(F, HF),
        "at0": np.concatenate([a0[:, :F, 0].T, a0[:, F:, 0].T], axis=1),
        "merge": a["L0_gnn_merge_kernel"].reshape(H, F, F).transpose(1, 0, 2),
        "wt3": w3.reshape(F, H, F).transpose(2, 1, 0).reshape(F, HF),
        "at3": np.concatenate([a["L3_gnn_att_src"].T, a["L3_gnn_att_dst"].T], axis=1),
        "value3": w3.reshape(F, 4, 2, F).transpose(2, 0, 1, 3).reshape(2 * F, 4, F),
        "sage1": np.concatenate([a["L1_gnn_w1_l"], a["L1_gnn_w1_r"]]),
        "sage2": np.concatenate([a["L1_gnn_w2_l"], a["L1_gnn_w2_r"]]),
        "edge_w": np.concatenate([a["L2_gnn_W"].T[F:], a["L2_gnn_W"].T[:F]]),
        "ff1": a["L3_gnn_W1"], "ff1_b": a["L3_gnn_b1"].reshape(2 * F, 1), "ff2": a["L3_gnn_W2"],
        "rows": np.stack([a[n] for n in (
            "L1_gnn_b1", "L1_gnn_b2", "L2_gnn_b", "L3_gnn_bias_att", "L3_gnn_b2",
            "L3_gnn_ln1_g", "L3_gnn_ln1_b", "L3_gnn_ln2_g", "L3_gnn_ln2_b")]),
    }
    nc = bacc.Bacc("TRN2", target_bir_lowering=False, num_devices=1)
    io = {}
    for name, value in arrays.items():
        arrays[name] = np.ascontiguousarray(value)
        io[name] = nc.dram_tensor(name + "_in", value.shape, mybir.dt.from_np(value.dtype), kind="ExternalInput").ap()
    out = nc.dram_tensor("out", (N, F), F32, kind="ExternalOutput").ap()
    program(nc, io, out)
    r = run_bass_kernel_spmd(nc, [{k + "_in": v for k, v in arrays.items()}], core_ids=[0])
    return r.results[0]["out"]
```

```python
from contextlib import ExitStack

import concourse.bass as bass
from concourse import mybir
from concourse.bass import OrderedEngineSet

F32 = mybir.dt.float32
BF16 = mybir.dt.bfloat16
F16 = mybir.dt.float16
I32 = mybir.dt.int32
ALU = mybir.AluOpType
ACT = mybir.ActivationFunctionType
AX = mybir.AxisListType

N, E, F, H = 3125, 100000, 64, 8
P = 125
W = N // P
T = 4
SLOTS = 4
U = 8
G = E // (P * T)
K = G + W - 1
Q = K // U
HF = H * F
D = 25
V = N // D
KV = G + V - 1
UV = 12
CW = 26 * D
HALF = (HF + H) // 2
R = F + H
C = E // P
FAR = 1.0e30
PARTS = 4
QP = Q // PARTS
GP = QP * U
CP = T * GP
BLOCK = 5
AT_ONCE = 3
BATCH = 16
TRAIL = 3
PAD = U


def load_group(nc, steps, k):
    _, values = nc.values_load_multi_w_load_instructions(
        steps.group[0:1, bass.ds(k, 1)], engines=[mybir.EngineType.SP], min_val=0, max_val=G - 1,
        skip_runtime_bounds_check_because="order_edges counts the groups, from 0 to G - 1")
    return values[0]


class Own:

    def __init__(self, eng, sem):
        self.eng, self.sem, self.n = eng, sem, 0

    def __call__(self, instruction):
        self.n += 1
        instruction.then_inc(self.sem, 1)
        self.eng.wait_ge(self.sem, self.n)


def rounds(nc, eng, step, load=None, steps=K, u=U):
    last = steps // u - 1
    def one_round(q):
        if load:
            values = load(q)
            for j in range(u):
                step(q, j, values[j])
        else:
            for j in range(u):
                step(q, j)
    one_round(0)
    with nc.Fori(1, last, 1, engines=OrderedEngineSet([eng.engine]), hint_back_edge=True) as q:
        one_round(q)
    one_round(last)


def load_windows(nc, engine, steps, first):
    _, values = nc.values_load_multi_w_load_instructions(
        steps.window[0:1, bass.ds(first + PAD, U)], engines=[engine], min_val=0, max_val=W - 1,
        skip_runtime_bounds_check_because="order_edges counts the windows, from 0 to W - 1")
    return values


def early(q, j, n=SLOTS):
    return isinstance(q, int) and q == 0 and j < n


def uses(q, j):
    return q * (U // SLOTS) + j // SLOTS


def after(q, j, n=1, count=Q):
    if isinstance(q, int) and q == count - 1 and j + n >= U:
        return None
    return (q, j + n) if j + n < U else (q + 1, j + n - U)


def before(q, j):
    if early(q, j, 1):
        return None
    return (q, j - 1) if j else (q - 1, U - 1)


def over(ap, shape):
    return ap.to_broadcast(list(shape))


class SharedSems:

    def __init__(self, nc, stack, n):
        self.nc, self.used = nc, 0
        self.all = [stack.enter_context(nc.semaphore(f"shared{i}")) for i in range(n)]
        assert [x.num for x in self.all] == list(range(self.all[0].num, self.all[0].num + n))

    def reset(self):
        if self.used:
            first = self.all[0].num
            self.nc.all_engine_barrier(sems_to_clear=range(first, first + self.used))
        self.used = 0

    def take(self):
        self.used += 1
        return self.all[self.used - 1]


class Scope:

    def __init__(self, nc, stack, tag, shared=None):
        self.nc, self.stack, self.tag, self.shared = nc, stack, tag, shared
        if shared:
            shared.reset()

    def sb(self, name, shape, dt=F32):
        return self.stack.enter_context(self.nc.sbuf_tensor(f"{self.tag}_{name}", shape, dt))

    def ps(self, name, shape=(128, 512)):
        return self.stack.enter_context(self.nc.psum_tensor(f"{self.tag}_{name}", list(shape), F32))

    def sem(self, name):
        return self.shared.take()

    def sems(self, name, n):
        return [self.sem(f"{name}{i}") for i in range(n)]

    def pool_dma_sems(self, name, n):
        return [self.stack.enter_context(self.nc.semaphore(f"{self.tag}_{name}{i}")) for i in range(n)]


class StepSems:

    NAMES = ("rel_ready", "hot_ready", "turned", "turned_copied", "near_ready", "z_ready", "leaky_ready", "less_max",
             "score_ready", "att_ready", "msg_ready", "sums_ready", "acc_ready", "zeroed", "gather_go", "load_go")

    def __init__(self, nc, stack):
        self.nc, self.base, self.used = nc, 0, False
        self.gathered = [stack.enter_context(nc.semaphore(f"step_gathered{i}")) for i in range(4)]
        self.keys_in = [stack.enter_context(nc.semaphore(f"step_keys_in{i}")) for i in range(4)]
        self.streamed = [stack.enter_context(nc.semaphore(f"step_streamed{i}")) for i in range(4)]
        self.by_name = {n: stack.enter_context(nc.semaphore(f"step_{n}")) for n in self.NAMES}

    def begin(self, gathers):
        if self.used:
            numbers = sorted(s.num for s in (*self.keys_in, *self.streamed, *self.by_name.values()))
            assert numbers == list(range(numbers[0], numbers[-1] + 1))
            self.nc.all_engine_barrier(sems_to_clear=range(numbers[0], numbers[-1] + 1))
        self.used = True
        base = self.base
        if gathers:
            self.base += 16 * T * K // SLOTS
        return base



def norm_scratch(s):
    s.mean, s.var, s.root = s.sb("mean", [P, W]), s.sb("var", [P, W]), s.sb("root", [P, W])
    s.cen, s.sq = s.sb("cen", [P, W, F]), s.sb("sq", [P, W, F])
    s.var_ready, s.root_ready, s.norms = s.sem("var_ready"), s.sem("root_ready"), 0


def layer_norm(nc, own, s, x, y, relu=True):
    v = nc.vector
    own(v.tensor_reduce(s.mean[:, :], x, AX.X, ALU.add))
    own(v.tensor_scalar(s.mean[:, :], s.mean[:, :], 1.0 / F, None, ALU.mult))
    own(v.tensor_tensor(s.cen[:, :, :], x, over(s.mean[:, :].unsqueeze(2), (P, W, F)), ALU.subtract))
    own(v.tensor_tensor(s.sq[:, :, :], s.cen[:, :, :], s.cen[:, :, :], ALU.mult))
    own(v.tensor_reduce(s.var[:, :], s.sq[:, :, :], AX.X, ALU.add))
    v.tensor_scalar(s.var[:, :], s.var[:, :], 1.0 / F, 1e-5, ALU.mult, ALU.add).then_inc(s.var_ready, 1)
    s.norms += 1
    own.eng.wait_ge(s.root_ready, s.norms)
    own(v.reciprocal(s.root[:, :], s.root[:, :]))
    own(v.tensor_tensor(s.mean[:, :], s.root[:, :], s.root[:, :], ALU.mult))
    own(v.tensor_tensor(s.var[:, :], s.var[:, :], s.mean[:, :], ALU.mult))
    own(v.tensor_scalar(s.var[:, :], s.var[:, :], -0.5, 1.5, ALU.mult, ALU.add))
    own(v.tensor_tensor(s.var[:, :], s.var[:, :], s.root[:, :], ALU.mult))
    own(v.tensor_tensor(y, s.cen[:, :, :], over(s.var[:, :].unsqueeze(2), (P, W, F)), ALU.mult))
    if relu:
        own(v.tensor_scalar(y, y, 0.0, None, ALU.max))


def norm_root(nc, act, s, n):
    act.wait_ge(s.var_ready, n)
    nc.scalar.activation(s.root[:, :], s.var[:, :], ACT.Sqrt).then_inc(s.root_ready, 1)


def split3(nc, own, s, x, parts):
    v = nc.vector
    own(v.tensor_copy(parts[0], x))
    own(v.tensor_tensor(s.rest, x, parts[0], ALU.subtract))
    own(v.tensor_copy(parts[1], s.rest))
    own(v.tensor_tensor(s.rest, s.rest, parts[1], ALU.subtract))
    own(v.tensor_copy(parts[2], s.rest))



def set_up(nc, m, io):
    with ExitStack() as stack:
        s = Scope(nc, stack, "setup", m.shared)
        loaded, made, iota_made = s.sem("loaded"), s.sem("made"), s.sem("iota_made")
        ints = s.sb("ints", [P, P], I32)
        step_ints = s.sb("step_ints", [128, CW], I32)
        group_ints = s.sb("group_ints", [100, 2], I32)
        block = stack.enter_context(nc.Block())

        @block.sync
        def _(sp):
            loads = [
                (m.x[:, :, :], io["x"].rearrange("(w p) f -> p w f", p=P)),
                (m.src_run[:, :], io["src"].rearrange("(p c) -> p c", p=P)),
                (m.dst_run[:, :], io["dst"].rearrange("(p c) -> p c", p=P)),
                (m.last_key[:, :], io["dst"].rearrange("(j p e) -> p j e", p=100, e=P * T)[:, :, P * T - 1]),
                (m.wt0[:, :], io["wt0"]), (m.at0[:, :], io["at0"]), (m.merge[:, :, :], io["merge"]),
                (m.wt3[:, :], io["wt3"]), (m.at3[:, :], io["at3"]), (m.value3[:, :, :], io["value3"]),
                (m.sage1[:, :], io["sage1"]), (m.sage2[:, :], io["sage2"]), (m.edge_w[:, :], io["edge_w"]),
                (m.ff1[:, :], io["ff1"]), (m.ff1_b[:, :], io["ff1_b"]), (m.ff2[:, :], io["ff2"]),
                (m.rows[:, :], io["rows"].rearrange("a n -> (a n)").partition_broadcast(P)),
            ]
            for out, in_ in loads:
                sp.dma_start(out, in_, allow_slow_non_contiguous=in_.shape[0] == 100).then_inc(loaded, 16)
            sp.wait_ge(loaded, 16 * len(loads))

        @block.gpsimd
        def _(pool):
            own = Own(pool, made)
            g = nc.gpsimd
            own(g.memset(m.ident[:, :], 0.0))
            own(g.affine_select(out=m.ident[:, :], in_=m.ident[:, :], compare_op=ALU.not_equal, fill=1.0,
                                base=0, pattern=[[-1, 128]], channel_multiplier=1))
            own(g.memset(m.ones[:, :], 1.0))
            own(g.affine_select(out=m.upto[:, :], in_=m.ones[:, :], compare_op=ALU.is_ge, fill=0.0,
                                base=0, pattern=[[1, 128]], channel_multiplier=-1))
            own(g.iota(ints[:, :], pattern=[[1, P]], base=0, channel_multiplier=0))
            own(g.iota(step_ints[:, :], pattern=[[1, CW]], base=0, channel_multiplier=0))
            g.iota(group_ints[:, :], pattern=[[100, 2]], base=0, channel_multiplier=1).then_inc(iota_made, 1)

        @block.vector
        def _(dve):
            dve.wait_ge(iota_made, 1)
            nc.vector.tensor_copy(m.node_iota[:, :], ints[:, :])
            nc.vector.tensor_copy(m.step_iota[:, :], step_ints[:, 0:KV])
            nc.vector.tensor_copy(m.code_iota[:, :].rearrange("p (b d) -> p b d", d=D),
                                  step_ints[0:P, :].rearrange("p (d b) -> p b d", d=D))
            nc.vector.tensor_copy(m.group_iota[:, :], group_ints[:, :])
            nc.vector.tensor_scalar(m.edge_iota[:, :], group_ints[:, :], float(P * T), float(P * T - 1), ALU.mult, ALU.add)


def plan_steps(nc, own, s, m, steps=K):
    v = nc.vector
    own(v.tensor_tensor(s.finish[:, :], s.last_window[:, :], m.group_iota[:, :], ALU.add))
    for j in range(2):
        own(v.tensor_scalar(s.done[:, j, 0:steps], m.step_iota[0:100, 0:steps], s.finish[:, j:j + 1], None, ALU.is_gt))


def order_edges(nc, m):
    with ExitStack() as stack:
        s = Scope(nc, stack, "order", m.shared)
        s.finish = s.sb("finish", [100, 2])
        s.done = s.sb("done", [100, 2, KV])
        s.last_window = s.sb("last_window", [100, 2])
        flags = s.sb("flags", [100, 2, W - 1])
        bounds = s.sb("bounds", [128, W - 1])
        fine_flags = s.sb("fine_flags", [100, 2, V - 1])
        fine_bounds = s.sb("fine_bounds", [128, V - 1])
        last_key = s.sb("last_key", [100, 2])
        key = s.sb("key", [P, C])
        win = s.sb("win", [P, C])
        mask = s.sb("mask", [P, C])
        one = s.sb("one", [P, C])
        count = s.sb("count", [P, W, C])
        place = s.sb("place", [P, C])
        totals = s.sb("totals", [P, W])
        base = s.sb("base", [128, W])
        cum = s.sb("cum", [128, W])
        code = s.sb("code", [P, C, 2])
        spare = s.sb("spare", [1, KV])
        masked, base_ready, based, picks = (s.sem(n) for n in ("masked", "base_ready", "based", "picks"))
        coded, codes_written = s.sem("coded"), s.sem("codes_written")
        own_sem, to_pe, from_pe = s.sem("dve_step"), s.sem("operands_ready"), s.sem("sums_ready")
        ps = s.ps("sums")
        ps2 = s.ps("before")
        block = stack.enter_context(nc.Block())

        def finish_steps(dve, own, table, n):
            v = nc.vector
            dve.wait_ge(from_pe, n)
            own(v.tensor_scalar(table.group_f[:, :], ps[:, 0:K], float(G - 1), None, ALU.min))
            own(v.tensor_tensor(table.window_f[:, :], m.step_iota[:, 0:K], table.group_f[:, :], ALU.subtract))
            own(v.tensor_scalar(table.first_node[:, :], table.window_f[:, :], float(P), None, ALU.mult))
            own(v.tensor_copy(table.group[:, :], table.group_f[0:1, :]))
            own(v.memset(table.window[:, :], 0))
            own(v.tensor_copy(table.window[:, PAD:PAD + K], table.window_f[0:1, :]))

        def finish_fine(dve, own, n):
            v, t = nc.vector, m.fine
            dve.wait_ge(from_pe, n)
            own(v.tensor_scalar(t.group_f[:, :], ps[:, 0:KV], float(G - 1), None, ALU.min))
            own(v.tensor_tensor(t.window_f[:, :], m.step_iota[:, 0:KV], t.group_f[:, :], ALU.subtract))
            own(v.tensor_copy(t.group[:, :], t.group_f[0:1, :]))
            own(v.tensor_scalar(t.first[:, :], t.window_f[:, :], float(CW), None, ALU.mult))
            own(v.memset(t.same[:, 0:1], 0.0))
            own(v.tensor_tensor(t.same[:, 1:KV], t.window_f[:, 1:KV], t.window_f[:, 0:KV - 1], ALU.is_equal))
            for j in range(SLOTS):
                own(v.memset(spare[:, j:KV:SLOTS], float(V + j)))
            own(v.tensor_tensor(spare[:, :], spare[:, :], t.window_f[0:1, :], ALU.subtract))
            own(v.tensor_tensor(spare[:, 0:KV - 1], spare[:, 0:KV - 1], t.same[0:1, 1:KV], ALU.mult))
            own(v.memset(spare[:, KV - 1:KV], 0.0))
            own(v.tensor_tensor(spare[:, :], spare[:, :], t.window_f[0:1, :], ALU.add))
            own(v.memset(t.place[:, 0:TRAIL], 0))
            own(v.tensor_copy(t.place[:, TRAIL:TRAIL + KV], spare[:, :]))

        @block.vector
        def _(dve):
            own = Own(dve, own_sem)
            v = nc.vector
            own(v.tensor_scalar(bounds[:, :], m.step_iota[:, 1:W], float(P), None, ALU.mult))
            own(v.tensor_copy(last_key[:, :], m.last_key[:, :]))
            own(v.tensor_tensor(flags[:, :, :], over(last_key[:, :].unsqueeze(2), (100, 2, W - 1)),
                                over(bounds[0:100, :].unsqueeze(1), (100, 2, W - 1)), ALU.is_ge))
            own(v.tensor_reduce(s.last_window[:, :], flags[:, :, :], AX.X, ALU.add))
            plan_steps(nc, own, s, m)
            v.memset(one[:, :], 1.0).then_inc(to_pe, 1)
            finish_steps(dve, own, m.by_dst, 1)
            own(v.tensor_scalar(fine_bounds[:, :], m.step_iota[:, 1:V], float(D), None, ALU.mult))
            own(v.tensor_tensor(fine_flags[:, :, :], over(last_key[:, :].unsqueeze(2), (100, 2, V - 1)),
                                over(fine_bounds[0:100, :].unsqueeze(1), (100, 2, V - 1)), ALU.is_ge))
            own(v.tensor_reduce(s.last_window[:, :], fine_flags[:, :, :], AX.X, ALU.add))
            plan_steps(nc, own, s, m, KV)
            v.memset(one[:, :], 1.0).then_inc(to_pe, 1)
            finish_fine(dve, own, 2)

            own(v.tensor_copy(key[:, :], m.src_run[:, :]))
            own(v.tensor_scalar(mask[:, :], key[:, :], 1.0 / P, None, ALU.mult))
            own(v.tensor_copy(m.place[:, :], mask[:, :]))
            own(v.tensor_copy(win[:, :], m.place[:, :]))
            own(v.scalar_tensor_tensor(mask[:, :], win[:, :], -float(P), key[:, :], ALU.mult, ALU.add))
            own(v.scalar_tensor_tensor(win[:, :], mask[:, :], float(P), win[:, :], ALU.is_ge, ALU.add))
            own(v.scalar_tensor_tensor(win[:, :], mask[:, :], 0.0, win[:, :], ALU.is_ge, ALU.add))
            own(v.tensor_scalar(win[:, :], win[:, :], -1.0, None, ALU.add))
            own(v.scalar_tensor_tensor(code[:, :, 0], win[:, :], float(P), key[:, :], ALU.mult, ALU.subtract))
            own(v.tensor_copy(mask[:, :], m.dst_run[:, :]))
            v.scalar_tensor_tensor(code[:, :, 1], mask[:, :], float(CW // D), win[:, :], ALU.mult, ALU.add).then_inc(coded, 1)
            dve.wait_ge(coded, 1)
            masks = [mask, key]

            def in_window(w):
                v.tensor_scalar(masks[w % 2][:, :], win[:, :], float(w), None, ALU.is_equal).then_inc(masked, 1)
            in_window(0)
            for w in range(W):
                if w + 1 < W:
                    in_window(w + 1)
                dve.wait_ge(masked, w + 1)
                own(v.tensor_tensor_scan(count[:, w, :], one[:, :], masks[w % 2][:, :], 0.0, ALU.mult, ALU.add))
            v.tensor_copy(totals[:, :], count[:, :, C - 1]).then_inc(to_pe, 1)
            dve.wait_ge(from_pe, 3)
            own(v.tensor_tensor_scan(cum[0:P, :], one[:, 0:W], ps[0:P, 0:W], 0.0, ALU.mult, ALU.add))
            own(v.tensor_tensor(base[0:P, :], cum[0:P, :], ps[0:P, 0:W], ALU.subtract))
            own(v.tensor_tensor(base[0:P, :], base[0:P, :], ps2[0:P, 0:W], ALU.add))
            v.tensor_tensor(base[0:P, :], base[0:P, :], totals[:, :], ALU.subtract).then_inc(base_ready, 1)
            own(v.memset(place[:, :], -1.0))
            picked = [mask, key]

            def pick(w):
                dve.wait_ge(based, w + 1)
                v.scalar_tensor_tensor(picked[w % 2][:, :], win[:, :], float(w), count[:, w, :],
                                       ALU.is_equal, ALU.mult).then_inc(picks, 1)
            pick(0)
            for w in range(W):
                if w + 1 < W:
                    pick(w + 1)
                dve.wait_ge(picks, w + 1)
                own(v.tensor_tensor(place[:, :], place[:, :], picked[w % 2][:, :], ALU.add))
            own(v.tensor_copy(m.place[:, :], place[:, :]))
            own(v.tensor_copy(m.record[:, :, 0], m.src_run[:, :]))
            own(v.tensor_copy(m.record[:, :, 1], m.dst_run[:, :]))
            own(v.tensor_tensor(flags[:, :, :], over(m.edge_iota[:, :].unsqueeze(2), (100, 2, W - 1)),
                                over(cum[0:100, 0:W - 1].unsqueeze(1), (100, 2, W - 1)), ALU.is_ge))
            own(v.tensor_reduce(s.last_window[:, :], flags[:, :, :], AX.X, ALU.add))
            plan_steps(nc, own, s, m)
            v.memset(one[:, :], 1.0).then_inc(to_pe, 1)
            finish_steps(dve, own, m.by_src, 4)

        @block.tensor
        def _(pe):
            def add_up(n, steps=K):
                pe.wait_ge(to_pe, n)
                nc.tensor.matmul(ps[:, 0:steps], m.ones[0:100, :], s.done[:, 0, 0:steps], start=True, stop=False)
                nc.tensor.matmul(ps[:, 0:steps], m.ones[0:100, :], s.done[:, 1, 0:steps], start=False,
                                 stop=True).then_inc(from_pe, 1)
            add_up(1)
            add_up(2, KV)
            pe.wait_ge(to_pe, 3)
            nc.tensor.matmul(ps[0:P, 0:W], m.ones[0:P, 0:P], totals[:, :], start=True, stop=True)
            nc.tensor.matmul(ps2[0:P, 0:W], m.upto[0:P, 0:P], totals[:, :], start=True,
                             stop=True).then_inc(from_pe, 1)
            add_up(4)

        @block.scalar
        def _(act):
            act.wait_ge(base_ready, 1)
            for w in range(W):
                nc.scalar.activation(count[:, w, :], count[:, w, :], ACT.Identity, bias=base[0:P, w:w + 1]).then_inc(based, 1)

        @block.sync
        def _(sp):
            sp.wait_ge(coded, 1)
            sp.dma_start(m.codes[:, :].rearrange("(p c) a -> p c a", p=P), code[:, :, :]).then_inc(codes_written, 16)
            sp.wait_ge(codes_written, 16)


def scatter_and_tables(nc, m):
    with ExitStack() as stack:
        s = Scope(nc, stack, "l0tab", m.shared)
        slot_place = [s.sb(f"place{i}", [P, BATCH], I32) for i in range(2)]
        slot_record = [s.sb(f"record{i}", [P, BATCH, 2], I32) for i in range(2)]
        staged, sent, go = s.sem("staged"), s.pool_dma_sems("sent", 2), s.sem("go")
        tables = Tables(nc, s, m)
        count = Count(nc, s, m)
        block = stack.enter_context(nc.Block())

        @block.gpsimd
        def _(pool):
            def half(i, b):
                if not (isinstance(i, int) and i == 0):
                    pool.wait_ge(sent[b], 16 * BATCH * i)
                nc.gpsimd.tensor_copy(slot_place[b][:, :], m.place[:, bass.ds(BATCH * (2 * i + b), BATCH)])
                nc.gpsimd.tensor_copy(slot_record[b][:, :, :],
                                      m.record[:, bass.ds(BATCH * (2 * i + b), BATCH), :]).then_inc(staged, 1)
                pool.wait_ge(staged, 2 * i + b + 1)
                pool.sem_inc(go, 1)
                for t in range(BATCH):
                    pool.indirect_dma_start(
                        m.records[:, :], bass.IndirectOffsetOnAxis(ap=slot_place[b][:, t:t + 1], axis=0),
                        slot_record[b][:, t, :], None).then_inc(sent[b], 16)
            half(0, 0)
            half(0, 1)
            with pool.Fori(1, C // (2 * BATCH), 1) as i:
                half(i, 0)
                half(i, 1)
            for b in range(2):
                pool.wait_ge(sent[b], 16 * BATCH * (C // (2 * BATCH)))

        tables.write(block, m.x, m.wt0, m.at0, table_score=1, count=count)


class Count:

    def __init__(self, nc, s, m):
        self.nc, self.m = nc, m
        self.codes = [s.sb(f"codes{i}", [P, T, 2]) for i in range(SLOTS)]
        self.pair_hot = [s.sb(f"pair_hot{i}", [P, T, CW], BF16) for i in range(2)]
        self.src_hot = [s.sb(f"src_hot{i}", [P, T, P], BF16) for i in range(2)]
        self.off = [s.sb(f"off{i}", [P, T, P]) for i in range(2)]
        self.off_ready, self.src_hot_ready = s.sem("off_ready"), s.sem("src_hot_ready")
        self.sum = [s.sb(f"sum{i}", [P, 2, CW // 2]) for i in range(SLOTS)]
        self.ps = [s.ps(f"count_ps{i}", (128, 2, 512)) for i in range(2)]
        self.codes_in, self.sum_out = s.sems("codes_in", SLOTS), s.sems("sum_out", SLOTS)
        self.hot_ready = s.sem("hot_ready")
        self.count_ready, self.sum_ready, self.go = s.sem("count_ready"), s.sem("sum_ready"), s.sem("count_go")

    @staticmethod
    def uses(q, j):
        return q * (UV // SLOTS) + j // SLOTS

    def sp(self, sp):
        nc, m = self.nc, self.m

        def store(q, j, v):
            sp.wait_ge(self.sum_ready, UV * q + j + 1)
            sp.sem_inc(self.go, 1)
            sp.dma_start(m.counts[bass.ds(v, 1), :, :].rearrange("v i c -> i (v c)"),
                         self.sum[j % SLOTS][:, :, :].rearrange("p a c -> p (a c)")).then_inc(self.sum_out[j % SLOTS], 16)

        def step(q, j, values):
            k = UV * q + j
            g, place = values
            if not early(q, j):
                sp.wait_ge(self.hot_ready, k - 3)
                sp.sem_inc(self.go, 1)
                sp.wait_ge(self.off_ready, k - 3)
                sp.sem_inc(self.go, 1)
            sp.dma_start(self.codes[j % SLOTS][:, :, :],
                         m.codes[bass.ds(g * (P * T), P * T), :].rearrange("(p t) a -> p t a", t=T)
                         ).then_inc(self.codes_in[j % SLOTS], 16)
            if not early(q, j, TRAIL):
                pq, pj = (q, j - TRAIL) if j >= TRAIL else (q - 1, UV + j - TRAIL)
                store(pq, pj, place)

        def load(q):
            groups = self.values(m.fine.group, UV * q, G)
            return list(zip(groups, self.values(m.fine.place, UV * q, V + SLOTS)))
        rounds(nc, sp, step, load, steps=KV, u=UV)
        places = self.values(m.fine.place, KV, V + SLOTS, TRAIL)
        for j in range(UV - TRAIL, UV):
            store(KV // UV - 1, j, places[j - UV + TRAIL])
        for j in range(SLOTS):
            sp.wait_ge(self.sum_out[j], 16 * (KV // SLOTS))

    def values(self, table, k, n, count=UV):
        _, values = self.nc.values_load_multi_w_load_instructions(
            table[0:1, bass.ds(k, count)], engines=[mybir.EngineType.SP], min_val=0, max_val=n - 1,
            skip_runtime_bounds_check_because="order_edges counts groups and windows within their bounds")
        return values

    def dve(self, dve):
        nc, m, v = self.nc, self.m, self.nc.vector

        def add(q, j):
            k, b = UV * q + j, j % 2
            dve.wait_ge(self.count_ready, k + 1)
            if early(q, j, 1):
                v.tensor_copy(self.sum[0][:, :, :], self.ps[0][0:P, :, 0:CW // 2]).then_inc(self.sum_ready, 1)
                return
            dve.wait_ge(self.sum_ready, k)
            if not early(q, j):
                dve.wait_ge(self.sum_out[j % SLOTS], 16 * self.uses(q, j))
            v.scalar_tensor_tensor(self.sum[j % SLOTS][:, :, :], self.sum[(j - 1) % SLOTS][:, :, :],
                                   m.fine.same[0:P, bass.ds(k, 1)], self.ps[b][0:P, :, 0:CW // 2],
                                   ALU.mult, ALU.add).then_inc(self.sum_ready, 1)

        def step(q, j):
            k, b = UV * q + j, j % 2
            dve.wait_ge(self.codes_in[j % SLOTS], 16 * (self.uses(q, j) + 1))
            if not early(q, j, 2):
                dve.wait_ge(self.count_ready, k - 1)
            for t in range(T):
                last = v.tensor_scalar(self.pair_hot[b][:, t, :], m.code_iota[:, :], m.fine.first[0:P, bass.ds(k, 1)],
                                       self.codes[j % SLOTS][:, t, 1:2], ALU.add, ALU.is_equal)
            last.then_inc(self.hot_ready, 1)
            if not early(q, j, 1):
                add(*((q, j - 1) if j else (q - 1, UV - 1)))
        rounds(nc, dve, step, steps=KV, u=UV)
        add(KV // UV - 1, UV - 1)

    def act(self, act):
        nc, m = self.nc, self.m

        def step(q, j):
            k, b = UV * q + j, j % 2
            act.wait_ge(self.codes_in[j % SLOTS], 16 * (self.uses(q, j) + 1))
            for t in range(T):
                last = nc.scalar.activation(self.off[b][:, t, :], m.node_iota[:, :], ACT.Abs,
                                            bias=self.codes[j % SLOTS][:, t, 0:1])
            last.then_inc(self.off_ready, 1)
            if not early(q, j, 2):
                act.wait_ge(self.count_ready, k - 1)
            act.wait_ge(self.off_ready, k + 1)
            nc.scalar.activation(self.src_hot[b][:, :, :], self.off[b][:, :, :], ACT.Relu, scale=-1.0,
                                 bias=m.ones[0:P, 0:1]).then_inc(self.src_hot_ready, 1)
        rounds(nc, act, step, steps=KV, u=UV)

    def pe(self, pe):
        nc = self.nc

        def step(q, j):
            k, b = UV * q + j, j % 2
            pe.wait_ge(self.src_hot_ready, k + 1)
            pe.wait_ge(self.hot_ready, k + 1)
            if not early(q, j, 2):
                pe.wait_ge(self.sum_ready, k - 1)
            for t in range(T):
                for c in range(2):
                    last = nc.tensor.matmul(self.ps[b][0:P, c, 0:CW // 2], self.src_hot[b][:, t, :],
                                            self.pair_hot[b][:, t, c * (CW // 2):(c + 1) * (CW // 2)],
                                            start=(t == 0), stop=(t == T - 1))
            last.then_inc(self.count_ready, 1)
        rounds(nc, pe, step, steps=KV, u=UV)


class Tables:

    def __init__(self, nc, s, m):
        self.nc, self.s, self.m = nc, s, m
        norm_scratch(s)
        self.vec = s.sb("vec", [F, 2 * H])
        self.rest = s.sb("rest", [P, W, H])
        s.rest = self.rest[:, :, :]
        self.ps_t = [s.ps(f"turned{i}") for i in range(2)]
        self.ps_v, self.ps_s = s.ps("vec_ps"), s.ps("score_ps")
        self.own_sem = s.sem("dve_step")
        self.h_ready, self.turned, self.copied = s.sem("h_ready"), s.sem("turned"), s.sem("copied")
        self.vec_ready, self.vec_copied = s.sem("vec_ready"), s.sem("vec_copied")
        self.scores_ready, self.rows_ready = s.sem("scores_ready"), s.sem("rows_ready")
        self.written = s.sem("written")
        self.graph_rows = s.sb("graph_rows", [P, W, R])

    def write(self, block, x, wt, at, table_score, count=None):
        nc, m, s = self.nc, self.m, self.s
        near = 1 - table_score

        @block.vector
        def _(dve):
            own = Own(dve, self.own_sem)
            v = nc.vector
            layer_norm(nc, own, s, x[:, :, :], m.h[:, :, :])
            v.tensor_copy(self.graph_rows[:, :, 0:F], m.h[:, :, :]).then_inc(self.h_ready, 1)
            dve.wait_ge(self.vec_ready, 1)
            v.tensor_copy(self.vec[:, :], self.ps_v[0:F, 0:2 * H]).then_inc(self.vec_copied, 1)
            dve.wait_ge(self.scores_ready, 1)
            both = self.ps_s[0:P, 0:W * 2 * H].rearrange("p (w a h) -> p w a h", a=2, h=H)
            own(v.tensor_copy(m.near[:, :, :], both[:, :, near, :]))
            own(v.tensor_copy(m.far[:, :, :], both[:, :, table_score, :]))
            v.tensor_copy(self.graph_rows[:, :, F:R], m.far[:, :, :]).then_inc(self.rows_ready, 1)
            split3(nc, own, s, m.near[:, :, :], [m.near_parts[:, :, i, 0:H] for i in range(3)])
            if count:
                count.dve(dve)

        @block.tensor
        def _(pe):
            for a in range(2):
                for h in range(H):
                    c = a * H + h
                    last = nc.tensor.matmul(self.ps_v[0:F, c:c + 1], wt[:, h * F:(h + 1) * F],
                                            at[:, c:c + 1], start=True, stop=True)
            last.then_inc(self.vec_ready, 1)
            pe.wait_ge(self.h_ready, 1)
            for c in range((W + 3) // 4):
                if c >= 2:
                    pe.wait_ge(self.copied, c - 1)
                for w in range(4 * c, min(4 * c + 4, W)):
                    o = (w % 4) * P
                    last = nc.tensor.transpose(self.ps_t[c % 2][0:F, o:o + P], m.h[:, w, :], m.ident[0:P, 0:P])
                last.then_inc(self.turned, 1)
            pe.wait_ge(self.vec_copied, 1)
            pe.wait_ge(self.copied, (W + 3) // 4)
            for w in range(W):
                last = nc.tensor.matmul(self.ps_s[0:P, w * 2 * H:(w + 1) * 2 * H], m.h_turned[:, w * P:(w + 1) * P],
                                        self.vec[:, :], start=True, stop=True)
            last.then_inc(self.scores_ready, 1)
            if count:
                count.pe(pe)

        @block.scalar
        def _(act):
            norm_root(nc, act, s, 1)
            for c in range((W + 3) // 4):
                act.wait_ge(self.turned, c + 1)
                n = P * (min(4 * c + 4, W) - 4 * c)
                nc.scalar.activation(m.h_turned[:, 4 * c * P:4 * c * P + n], self.ps_t[c % 2][0:F, 0:n],
                                     ACT.Copy).then_inc(self.copied, 1)
            if count:
                count.act(act)

        @block.sync
        def _(sp):
            sp.wait_ge(self.rows_ready, 1)
            sp.dma_start(m.table[:, :].rearrange("(w p) c -> p w c", p=P),
                         self.graph_rows[:, :, :]).then_inc(self.written, 16)
            sp.wait_ge(self.written, 16)
            if count:
                count.sp(sp)


def attend(nc, m, tag, steps, from_spill, part=0):
    q0, count = (QP * part, QP) if from_spill else (0, Q)
    near_cols = 2 * H if from_spill else H
    with ExitStack() as stack:
        s = Scope(nc, stack, tag, m.shared)
        pairs = [s.sb(f"pairs{i}", [P, 2 * T], I32) for i in range(4)]
        rows = [s.sb(f"rows{i}", [P, T, R]) for i in range(4)]
        rel = [s.sb(f"rel{i}", [P, T]) for i in range(4)]
        hot = [s.sb(f"hot{i}", [P, T, P]) for i in range(4)]
        hot_turned = [s.sb(f"hot_turned{i}", [P, T * P], BF16) for i in range(2)]
        z = [s.sb(f"z{i}", [P, T, H]) for i in range(2)]
        score = [s.sb(f"score{i}", [P, T, H]) for i in range(2)]
        msg = [s.sb(f"msg{i}", [P, T, HF + H]) for i in range(2)]
        att = [x[:, :, HF:HF + H] for x in msg]
        turn_ps = [s.ps(f"turn_ps{i}") for i in range(2)]
        near_ps = [s.ps(f"near_ps{i}") for i in range(2)]
        sum_ps = [s.ps(f"sum_ps{i}", (128, 2, 512)) for i in range(2)]
        base = m.sems.begin(gathers=not from_spill)
        keys_in, rows_in = m.sems.keys_in, m.sems.streamed if from_spill else m.sems.gathered
        (rel_ready, hot_ready, turned, turned_copied, near_ready, z_ready, leaky_ready, less_max, score_ready,
         att_ready, msg_ready, sums_ready, acc_ready, zeroed, gather_go, load_go) = (m.sems.by_name[n] for n in m.sems.NAMES)
        if from_spill:
            base = 0
        gather_next = GatherRows(nc, s, m, part + 1) if from_spill and part + 1 < PARTS else None
        block = stack.enter_context(nc.Block())

        key_of = [(x[:, 0:T] if from_spill else x[:, 0:2 * T:2]) for x in pairs]
        rows_count = 16 if from_spill else 16 * T

        @block.sync
        def _(sp):
            def load(q, j):
                k = U * q + j
                g = load_group(nc, steps, U * (q + q0) + j)
                if not early(q, j):
                    sp.wait_ge(hot_ready, k - 3)
                    sp.sem_inc(load_go, 1)
                    if from_spill:
                        sp.wait_ge(msg_ready, k - 3)
                    else:
                        sp.wait_ge(rows_in[j % SLOTS], base + 16 * T * uses(q, j))
                    sp.sem_inc(load_go, 1)
                if from_spill:
                    sp.dma_start(pairs[j % SLOTS][:, 0:T],
                                 m.dst[bass.ds(g * (P * T), P * T)].rearrange("(p t) -> p t", t=T)).then_inc(keys_in[j % SLOTS], 16)
                    sp.dma_start(rows[j % SLOTS][:, :, :],
                                 m.spill[bass.ds(g * (P * T), P * T), :].rearrange("(p t) c -> p t c", t=T)
                                 ).then_inc(rows_in[j % SLOTS], 16)
                else:
                    sp.dma_start(pairs[j % SLOTS][:, :],
                                 m.records[bass.ds(g * (P * T), P * T), :].rearrange("(p t) c -> p (t c)", t=T)
                                 ).then_inc(keys_in[j % SLOTS], 16)
            if gather_next:
                gather_next.sp(sp)
            rounds(nc, sp, load, steps=U * count)

        @block.gpsimd
        def _(pool):
            if part == 0:
                nc.gpsimd.memset(m.acc[:, :, :], 0.0).then_inc(zeroed, 1)
            if gather_next:
                gather_next.pool(pool)
            if from_spill:
                return

            def gather(q, j):
                k = U * q + j
                pool.wait_ge(keys_in[j % SLOTS], 16 * (uses(q, j) + 1))
                if not early(q, j):
                    pool.wait_ge(msg_ready, k - 3)
                pool.sem_inc(gather_go, 1)
                for t in range(T):
                    pool.indirect_dma_start(
                        rows[j % SLOTS][:, t, :], None, m.table[:, :],
                        bass.IndirectOffsetOnAxis(ap=pairs[j % SLOTS][:, 2 * t + 1:2 * t + 2], axis=0)).then_inc(rows_in[j % SLOTS], 16)
            rounds(nc, pool, gather)

        @block.vector
        def _(dve):
            v = nc.vector

            def one_hot(q, j):
                k = U * q + j
                dve.wait_ge(keys_in[j % SLOTS], 16 * (uses(q, j) + 1))
                if not early(q, j):
                    dve.wait_ge(sums_ready, k - 3)
                v.tensor_scalar(rel[j % SLOTS][:, :], key_of[j % SLOTS], steps.first_node[0:P, bass.ds(k + U * q0, 1)], None,
                                ALU.subtract).then_inc(rel_ready, 1)
                dve.wait_ge(rel_ready, k + 1)
                v.tensor_tensor(hot[j % SLOTS][:, :, :], over(rel[j % SLOTS][:, :].unsqueeze(2), (P, T, P)),
                                over(m.node_iota[:, :].unsqueeze(1), (P, T, P)), ALU.is_equal).then_inc(hot_ready, 1)

            def scores(q, j):
                k, b = U * q + j, j % 2
                dve.wait_ge(near_ready, k + 1)
                dve.wait_ge(rows_in[j % SLOTS], base + rows_count * (uses(q, j) + 1))
                near = near_ps[b][0:P, 0:T * near_cols].rearrange("p (t c) -> p t c", t=T)
                v.tensor_tensor(z[b][:, :, :], near[:, :, 0:H], rows[j % SLOTS][:, :, F:R], ALU.add).then_inc(z_ready, 1)
                dve.wait_ge(z_ready, k + 1)
                v.scalar_tensor_tensor(z[b][:, :, :], z[b][:, :, :], 0.2, z[b][:, :, :], ALU.mult,
                                       ALU.max).then_inc(leaky_ready, 1)
                dve.wait_ge(leaky_ready, k + 1)
                if not early(q, j, 2):
                    dve.wait_ge(att_ready, k - 1)
                if from_spill:
                    v.tensor_tensor(z[b][:, :, :], z[b][:, :, :], near[:, :, H:2 * H], ALU.subtract).then_inc(less_max, 1)
                    dve.wait_ge(less_max, k + 1)
                    v.tensor_scalar(score[b][:, :, :], z[b][:, :, :], 0.0, None, ALU.min).then_inc(score_ready, 1)
                else:
                    v.tensor_scalar(score[b][:, :, :], z[b][:, :, :], -2.0, 2.0, ALU.max, ALU.min).then_inc(score_ready, 1)

            def messages(q, j):
                k, b = U * q + j, j % 2
                dve.wait_ge(att_ready, k + 1)
                if not early(q, j, 2):
                    dve.wait_ge(sums_ready, k - 1)
                v.tensor_tensor(msg[b][:, :, 0:HF].rearrange("p t (h f) -> p t h f", h=H), over(rows[j % SLOTS][:, :, 0:F].unsqueeze(2), (P, T, H, F)),
                                over(att[b].unsqueeze(3), (P, T, H, F)), ALU.mult).then_inc(msg_ready, 1)

            def accumulate(q, j, w):
                k, b = U * q + j, j % 2
                dve.wait_ge(sums_ready, k + 1)
                if not early(q, j, 1):
                    dve.wait_ge(acc_ready, k)
                here = m.acc[:, bass.ds(w, 1), :].rearrange("p a (c f) -> p (a c) f", c=2)
                v.tensor_tensor(here, here, sum_ps[b][0:P, :, 0:HALF], ALU.add).then_inc(acc_ready, 1)

            def step(q, j, window_before):
                if after(q, j, 2, count):
                    one_hot(*after(q, j, 2, count))
                messages(q, j)
                if after(q, j, 1, count):
                    scores(*after(q, j, 1, count))
                if before(q, j):
                    accumulate(*before(q, j), window_before)
            if part == 0:
                dve.wait_ge(zeroed, 1)
            one_hot(0, 0)
            one_hot(0, 1)
            scores(0, 0)
            rounds(nc, dve, step, lambda q: load_windows(nc, mybir.EngineType.DVE, steps, U * (q + q0) - 1), U * count)
            accumulate(count - 1, U - 1, load_windows(nc, mybir.EngineType.DVE, steps, U * (q0 + count) - 1)[0])

        @block.tensor
        def _(pe):
            def turn(q, j):
                k, b = U * q + j, j % 2
                pe.wait_ge(hot_ready, k + 1)
                if not early(q, j, 2):
                    pe.wait_ge(turned_copied, k - 1)
                for t in range(T):
                    last = nc.tensor.transpose(turn_ps[b][0:P, t * P:(t + 1) * P], hot[j % SLOTS][:, t, :], m.ident[0:P, 0:P])
                last.then_inc(turned, 1)

            def near(q, j, w):
                k, b = U * q + j, j % 2
                pe.wait_ge(turned_copied, k + 1)
                if not early(q, j, 2):
                    pe.wait_ge(score_ready, k - 1)
                for t in range(T):
                    for i in range(3):
                        last = nc.tensor.matmul(near_ps[b][0:P, t * near_cols:(t + 1) * near_cols],
                                                hot_turned[b][:, t * P:(t + 1) * P],
                                                m.near_parts[:, bass.ds(w, 1), i, 0:near_cols].rearrange("p a c -> p (a c)"),
                                                start=(i == 0), stop=(i == 2))
                last.then_inc(near_ready, 1)

            def sums(q, j):
                k, b = U * q + j, j % 2
                pe.wait_ge(msg_ready, k + 1)
                if not early(q, j, 2):
                    pe.wait_ge(acc_ready, k - 1)
                for c in range(2):
                    for t in range(T):
                        last = nc.tensor.matmul(sum_ps[b][0:P, c, 0:HALF], hot[j % SLOTS][:, t, :],
                                                msg[b][:, t, c * HALF:(c + 1) * HALF], start=(t == 0), stop=(t == T - 1))
                last.then_inc(sums_ready, 1)

            def step(q, j, window_behind):
                if after(q, j, 1, count):
                    near(*after(q, j, 1, count), window_behind)
                if after(q, j, 2, count):
                    turn(*after(q, j, 2, count))
                sums(q, j)
            turn(0, 0)
            near(0, 0, load_windows(nc, mybir.EngineType.PE, steps, U * q0)[0])
            turn(0, 1)
            rounds(nc, pe, step, lambda q: load_windows(nc, mybir.EngineType.PE, steps, U * (q + q0) + 1), U * count)

        @block.scalar
        def _(act):
            def copy(q, j):
                k, b = U * q + j, j % 2
                act.wait_ge(turned, k + 1)
                if not early(q, j, 2):
                    act.wait_ge(near_ready, k - 1)
                nc.scalar.activation(hot_turned[b][:, :], turn_ps[b][0:P, 0:T * P], ACT.Copy).then_inc(turned_copied, 1)

            def exponential(q, j):
                k, b = U * q + j, j % 2
                act.wait_ge(score_ready, k + 1)
                if not early(q, j, 2):
                    act.wait_ge(sums_ready, k - 1)
                nc.scalar.activation(att[b], score[b][:, :, :], ACT.Exp).then_inc(att_ready, 1)

            def step(q, j):
                if after(q, j, 1, count):
                    copy(*after(q, j, 1, count))
                exponential(q, j)
            copy(0, 0)
            rounds(nc, act, step, steps=U * count)


def gather_sum(nc, m, tag, cols, edge_attr=None):
    with ExitStack() as stack:
        s = Scope(nc, stack, tag, m.shared)
        keys = [s.sb(f"keys{i}", [P, T], I32) for i in range(4)]
        sources = [s.sb(f"sources{i}", [P, T], I32) for i in range(4)]
        rows = [s.sb(f"rows{i}", [P, T, R]) for i in range(4)]
        rel = [s.sb(f"rel{i}", [P, T]) for i in range(4)]
        hot = [s.sb(f"hot{i}", [P, T, P]) for i in range(4)]
        attr = [s.sb(f"attr{i}", [P, T, F]) for i in range(4)] if edge_attr is not None else None
        msg = [s.sb(f"msg{i}", [P, T, F]) for i in range(4)] if edge_attr is not None else rows
        sum_ps = [s.ps(f"sum_ps{i}") for i in range(2)]
        base = m.sems.begin(gathers=True)
        keys_in, rows_in = m.sems.keys_in, m.sems.gathered
        rel_ready, hot_ready, msg_ready, sums_ready, acc_ready, zeroed, gather_go, load_go = (
            m.sems.by_name[n] for n in ("rel_ready", "hot_ready", "msg_ready", "sums_ready", "acc_ready", "zeroed",
                                        "gather_go", "load_go"))
        steps = m.by_dst
        loads = 48 if edge_attr is not None else 32
        block = stack.enter_context(nc.Block())

        @block.sync
        def _(sp):
            def load(q, j):
                k = U * q + j
                g = load_group(nc, steps, k)
                if not early(q, j):
                    sp.wait_ge(hot_ready, k - 3)
                    sp.sem_inc(load_go, 1)
                    sp.wait_ge(rows_in[j % SLOTS], base + 16 * T * uses(q, j))
                    if edge_attr is not None:
                        sp.sem_inc(load_go, 1)
                        sp.wait_ge(msg_ready, k - 3)
                    sp.sem_inc(load_go, 1)
                here = bass.ds(g * (P * T), P * T)
                sp.dma_start(sources[j % SLOTS][:, :], m.src[here].rearrange("(p t) -> p t", t=T)).then_inc(keys_in[j % SLOTS], 16)
                sp.dma_start(keys[j % SLOTS][:, :], m.dst[here].rearrange("(p t) -> p t", t=T)).then_inc(keys_in[j % SLOTS], 16)
                if edge_attr is not None:
                    sp.dma_start(attr[j % SLOTS][:, :, :], edge_attr[here, :].rearrange("(p t) f -> p t f", t=T)
                                 ).then_inc(keys_in[j % SLOTS], 16)
            rounds(nc, sp, load)

        @block.gpsimd
        def _(pool):
            nc.gpsimd.memset(m.acc[:, :, 0:cols], 0.0).then_inc(zeroed, 1)

            def gather(q, j):
                k = U * q + j
                pool.wait_ge(keys_in[j % SLOTS], loads * (uses(q, j) + 1))
                if not early(q, j):
                    pool.wait_ge(sums_ready if edge_attr is None else msg_ready, k - 3)
                pool.sem_inc(gather_go, 1)
                for t in range(T):
                    pool.indirect_dma_start(rows[j % SLOTS][:, t, :], None, m.table[:, :],
                                            bass.IndirectOffsetOnAxis(ap=sources[j % SLOTS][:, t:t + 1], axis=0)
                                            ).then_inc(rows_in[j % SLOTS], 16)
            rounds(nc, pool, gather)

        @block.vector
        def _(dve):
            v = nc.vector

            def accumulate(q, j, w):
                k, b = U * q + j, j % 2
                dve.wait_ge(sums_ready, k + 1)
                if not early(q, j, 1):
                    dve.wait_ge(acc_ready, k)
                v.tensor_tensor(m.acc[:, bass.ds(w, 1), 0:cols], m.acc[:, bass.ds(w, 1), 0:cols],
                                sum_ps[b][0:P, 0:cols].unsqueeze(1), ALU.add).then_inc(acc_ready, 1)

            def step(q, j, window_before):
                k = U * q + j
                dve.wait_ge(keys_in[j % SLOTS], loads * (uses(q, j) + 1))
                if not early(q, j):
                    dve.wait_ge(sums_ready, k - 3)
                v.tensor_scalar(rel[j % SLOTS][:, :], keys[j % SLOTS][:, :], steps.first_node[0:P, bass.ds(k, 1)], None,
                                ALU.subtract).then_inc(rel_ready, 1)
                dve.wait_ge(rel_ready, k + 1)
                v.tensor_tensor(hot[j % SLOTS][:, :, :], over(rel[j % SLOTS][:, :].unsqueeze(2), (P, T, P)),
                                over(m.node_iota[:, :].unsqueeze(1), (P, T, P)), ALU.is_equal).then_inc(hot_ready, 1)
                if edge_attr is not None:
                    dve.wait_ge(rows_in[j % SLOTS], base + 16 * T * (uses(q, j) + 1))
                    v.tensor_tensor(msg[j % SLOTS][:, :, :], rows[j % SLOTS][:, :, 0:F], attr[j % SLOTS][:, :, :], ALU.mult).then_inc(msg_ready, 1)
                if before(q, j):
                    accumulate(*before(q, j), window_before)
            dve.wait_ge(zeroed, 1)
            rounds(nc, dve, step, lambda q: load_windows(nc, mybir.EngineType.DVE, steps, U * q - 1))
            accumulate(Q - 1, U - 1, load_windows(nc, mybir.EngineType.DVE, steps, K - 1)[0])

        @block.tensor
        def _(pe):
            def step(q, j):
                k, b = U * q + j, j % 2
                pe.wait_ge(hot_ready, k + 1)
                if edge_attr is not None:
                    pe.wait_ge(msg_ready, k + 1)
                else:
                    pe.wait_ge(rows_in[j % SLOTS], base + 16 * T * (uses(q, j) + 1))
                if not early(q, j, 2):
                    pe.wait_ge(acc_ready, k - 1)
                for t in range(T):
                    last = nc.tensor.matmul(sum_ps[b][0:P, 0:cols], hot[j % SLOTS][:, t, :], msg[j % SLOTS][:, t, 0:cols],
                                            start=(t == 0), stop=(t == T - 1))
                last.then_inc(sums_ready, 1)
            rounds(nc, pe, step)


def count_sum(nc, m, tag):
    chunks = [(w, min(AT_ONCE, W - w)) for w in range(0, W, AT_ONCE)]
    with ExitStack() as stack:
        s = Scope(nc, stack, tag, m.shared)
        h_one = s.sb("h_one", [P, W, F + 1])
        counts = [s.sb(f"counts{i}", [P, AT_ONCE * V // W, CW]) for i in range(2)]
        sums = [s.sb(f"sums{i}", [F + 1, AT_ONCE * P]) for i in range(2)]
        ps = [s.ps(f"ps{i}") for i in range(2)]
        turned_ps = [s.ps(f"turned_ps{i}") for i in range(2)]
        counts_in = s.sems("counts_in", 2)
        h_ready, sums_ready, sums_copied, turned, done = (
            s.sem(n) for n in ("h_ready", "sums_ready", "sums_copied", "turned", "done"))
        block = stack.enter_context(nc.Block())

        @block.sync
        def _(sp):
            for c, (w, n) in enumerate(chunks):
                if c >= 2:
                    sp.wait_ge(sums_ready, c - 1)
                sp.dma_start(counts[c % 2][:, 0:n * V // W, :], m.counts[w * (V // W):(w + n) * (V // W), :, :].rearrange(
                    "v i c -> i v c")).then_inc(counts_in[c % 2], 16)

        @block.vector
        def _(dve):
            nc.vector.memset(h_one[:, :, F:F + 1], 1.0)
            nc.vector.tensor_copy(h_one[:, :, 0:F], m.h[:, :, :]).then_inc(h_ready, 1)
            for c, (w, n) in enumerate(chunks):
                dve.wait_ge(turned, c + 1)
                nc.vector.tensor_copy(m.acc[:, w:w + n, 0:F + 1], turned_ps[c % 2][0:P, 0:n * (F + 1)].rearrange(
                    "p (w f) -> p w f", f=F + 1)).then_inc(done, 1)

        @block.scalar
        def _(act):
            for c, (w, n) in enumerate(chunks):
                act.wait_ge(sums_ready, c + 1)
                if c >= 2:
                    act.wait_ge(turned, c - 1)
                nc.scalar.activation(sums[c % 2][:, 0:n * P], ps[c % 2][0:F + 1, 0:n * P], ACT.Copy).then_inc(sums_copied, 1)

        @block.tensor
        def _(pe):
            def turn(c):
                w, n = chunks[c]
                pe.wait_ge(sums_copied, c + 1)
                if c >= 2:
                    pe.wait_ge(done, c - 1)
                for i in range(n):
                    last = nc.tensor.transpose(turned_ps[c % 2][0:P, i * (F + 1):(i + 1) * (F + 1)],
                                               sums[c % 2][:, i * P:(i + 1) * P], m.ident[0:F + 1, 0:F + 1])
                last.then_inc(turned, 1)
            pe.wait_ge(h_ready, 1)
            for c, (w, n) in enumerate(chunks):
                pe.wait_ge(counts_in[c % 2], 16 * (c // 2 + 1))
                if c >= 2:
                    pe.wait_ge(sums_copied, c - 1)
                for b in range(W):
                    last = nc.tensor.matmul(ps[c % 2][0:F + 1, 0:n * P], h_one[:, b, :],
                                            counts[c % 2][:, 0:n * V // W, b * D:(b + 1) * D],
                                            start=(b == 0), stop=(b == W - 1))
                last.then_inc(sums_ready, 1)
                if c:
                    turn(c - 1)
            turn(len(chunks) - 1)


def by_head(acc, w):
    return acc[:, w:w + BLOCK, 0:HF].rearrange("p w (h f) -> p w h f", h=H)


class Heads:

    def __init__(self, nc, s, m):
        self.nc, self.s, self.m = nc, s, m
        self.ps_t = [s.ps(f"heads_t{i}") for i in range(2)]
        self.ps_o = [s.ps(f"heads_o{i}") for i in range(4)]
        self.turned_sb = [s.sb(f"heads_sb{i}", [128, 4 * P]) for i in range(2)]
        self.acc_ready, self.turned = s.sem("heads_acc_ready"), s.sem("heads_turned")
        self.copied, self.out_ready = s.sem("heads_copied"), s.sem("heads_out")

    def pe(self, pe, value):
        nc, m = self.nc, self.m

        def turn(w):
            if w % BLOCK == 0:
                pe.wait_ge(self.acc_ready, w // BLOCK + 1)
            if w >= 2:
                pe.wait_ge(self.copied, w - 1)
            for c in range(4):
                last = nc.tensor.transpose(self.ps_t[w % 2][:, c * P:(c + 1) * P], m.acc[:, w, c * 128:(c + 1) * 128],
                                           m.ident[0:P, 0:P])
            last.then_inc(self.turned, 1)
        turn(0)
        for w in range(W):
            if w + 1 < W:
                turn(w + 1)
            pe.wait_ge(self.copied, w + 1)
            for c in range(4):
                last = nc.tensor.matmul(self.ps_o[w // 8][0:P, (w % 8) * F:(w % 8 + 1) * F],
                                        self.turned_sb[w % 2][:, c * P:(c + 1) * P], value[:, c, :],
                                        start=(c == 0), stop=(c == 3))
            last.then_inc(self.out_ready, 1)

    def act(self, act):
        for w in range(W):
            act.wait_ge(self.turned, w + 1)
            if w >= 2:
                act.wait_ge(self.out_ready, w - 1)
            self.nc.scalar.activation(self.turned_sb[w % 2][:, :], self.ps_t[w % 2][:, 0:4 * P],
                                      ACT.Copy).then_inc(self.copied, 1)

    def banks(self):
        for b in range(4):
            n = min(8, W - 8 * b)
            yield 8 * b, n, self.ps_o[b][0:P, 0:n * F].rearrange("p (w f) -> p w f", f=F)


class Dense:

    def __init__(self, nc, s, m, ps_t, ps_o, tag):
        self.nc, self.m, self.ps_t, self.ps_o = nc, m, ps_t, ps_o
        self.turned_sb = s.sb(f"{tag}_sb", [128, W * P])
        self.ready, self.turned = s.sem(f"{tag}_in_ready"), s.sem(f"{tag}_turned")
        self.copied, self.out_ready = s.sem(f"{tag}_copied"), s.sem(f"{tag}_out")
        self.chunks = (W + 3) // 4

    def pe_turn(self, pe, cat, width):
        pe.wait_ge(self.ready, 1)
        for c in range(self.chunks):
            if c >= 2:
                pe.wait_ge(self.copied, c - 1)
            for w in range(4 * c, min(4 * c + 4, W)):
                o = (w % 4) * P
                last = self.nc.tensor.transpose(self.ps_t[c % 2][0:width, o:o + P], cat[:, w, 0:width], self.m.ident[0:P, 0:P])
            last.then_inc(self.turned, 1)

    def pe_out(self, pe, width, weight):
        pe.wait_ge(self.copied, self.chunks)
        for w in range(W):
            last = self.nc.tensor.matmul(self.ps_o[w // 8][0:P, (w % 8) * F:(w % 8 + 1) * F],
                                         self.turned_sb[0:width, w * P:(w + 1) * P], weight, start=True, stop=True)
        last.then_inc(self.out_ready, 1)

    def act(self, act, width):
        for c in range(self.chunks):
            act.wait_ge(self.turned, c + 1)
            n = P * (min(4 * c + 4, W) - 4 * c)
            self.nc.scalar.activation(self.turned_sb[0:width, 4 * c * P:4 * c * P + n], self.ps_t[c % 2][0:width, 0:n],
                                      ACT.Copy).then_inc(self.copied, 1)

    def banks(self):
        for b in range(4):
            n = min(8, W - 8 * b)
            yield 8 * b, n, self.ps_o[b][0:P, 0:n * F].rearrange("p (w f) -> p w f", f=F)


def finish_layer0(nc, m):
    with ExitStack() as stack:
        s = Scope(nc, stack, "l0end", m.shared)
        norm_scratch(s)
        heads = Heads(nc, s, m)
        value = s.sb("value", [128, 4, F])
        inv = s.sb("inv", [P, W, H])
        y = s.sb("y", [P, W, F])
        graph_rows = s.sb("graph_rows", [P, W, F + 1])
        value_ps = s.ps("value_ps")
        own_sem, value_ready, value_copied = s.sem("dve_step"), s.sem("value_ready"), s.sem("value_copied")
        rows_ready, written = s.sem("rows_ready"), s.sem("written")
        block = stack.enter_context(nc.Block())

        @block.vector
        def _(dve):
            own, v = Own(dve, own_sem), nc.vector
            own(v.tensor_scalar(inv[:, :, :], m.acc[:, :, HF:HF + H], 1e-30, None, ALU.max))
            own(v.reciprocal(inv[:, :, :], inv[:, :, :]))
            for w in range(0, W, BLOCK):
                v.tensor_tensor(by_head(m.acc, w), by_head(m.acc, w), over(inv[:, w:w + BLOCK, :].unsqueeze(3), (P, BLOCK, H, F)),
                                ALU.mult).then_inc(heads.acc_ready, 1)
            dve.wait_ge(heads.out_ready, W)
            for w0, n, out in heads.banks():
                yb = y[:, w0:w0 + n, :]
                own(v.tensor_copy(yb, out))
                own(v.scalar_tensor_tensor(yb, yb, 0.2, yb, ALU.mult, ALU.max))
                own(v.tensor_tensor(m.x[:, w0:w0 + n, :], m.x[:, w0:w0 + n, :], yb, ALU.add))
            layer_norm(nc, own, s, m.x[:, :, :], m.h[:, :, :])
            own(v.tensor_copy(graph_rows[:, :, 0:F], m.h[:, :, :]))
            v.memset(graph_rows[:, :, F:F + 1], 1.0).then_inc(rows_ready, 1)

        @block.tensor
        def _(pe):
            for h in range(H):
                o, c = (h % 2) * F, h // 2
                last = nc.tensor.matmul(value_ps[o:o + F, c * F:(c + 1) * F], m.wt0[:, h * F:(h + 1) * F],
                                        m.merge[:, h, :], start=True, stop=True)
            last.then_inc(value_ready, 1)
            pe.wait_ge(value_copied, 1)
            heads.pe(pe, value)

        @block.scalar
        def _(act):
            act.wait_ge(value_ready, 1)
            nc.scalar.activation(value[:, :, :], value_ps[:, 0:4 * F].rearrange("p (c f) -> p c f", f=F),
                                 ACT.Copy).then_inc(value_copied, 1)
            heads.act(act)
            norm_root(nc, act, s, 1)

        @block.sync
        def _(sp):
            sp.wait_ge(rows_ready, 1)
            sp.dma_start(m.table[:, 0:F + 1].rearrange("(w p) c -> p w c", p=P), graph_rows[:, :, :]).then_inc(written, 16)
            sp.wait_ge(written, 16)


def finish_mean(nc, m, tag, weight, bias, kind):
    with ExitStack() as stack:
        s = Scope(nc, stack, tag, m.shared)
        norm_scratch(s)
        cat = s.sb("cat", [P, W, 2 * F])
        inv = s.sb("inv", [P, W])
        ps_t = [s.ps(f"ps_t{i}") for i in range(2)]
        ps_o = [s.ps(f"ps_o{i}") for i in range(4)]
        dense = Dense(nc, s, m, ps_t, ps_o, "dense")
        own_sem, rows_ready, written = s.sem("dve_step"), s.sem("rows_ready"), s.sem("written")
        block = stack.enter_context(nc.Block())

        @block.vector
        def _(dve):
            own, v = Own(dve, own_sem), nc.vector
            if kind == "hidden":
                own(v.tensor_copy(m.degree[:, :], m.acc[:, :, F]))
            own(v.tensor_scalar(inv[:, :], m.degree[:, :], 1.0, None, ALU.max))
            own(v.reciprocal(inv[:, :], inv[:, :]))
            own(v.tensor_tensor(cat[:, :, 0:F], m.acc[:, :, 0:F], over(inv[:, :].unsqueeze(2), (P, W, F)), ALU.mult))
            v.tensor_copy(cat[:, :, F:2 * F], m.h[:, :, :]).then_inc(dense.ready, 1)
            dve.wait_ge(dense.out_ready, 1)
            for w0, n, out in dense.banks():
                b = over(bias.unsqueeze(1), (P, n, F))
                if kind == "hidden":
                    own(v.tensor_tensor(m.h[:, w0:w0 + n, :], out, b, ALU.add))
                else:
                    own(v.tensor_tensor(cat[:, w0:w0 + n, 0:F], out, b, ALU.add))
                    own(v.tensor_tensor(m.x[:, w0:w0 + n, :], m.x[:, w0:w0 + n, :], cat[:, w0:w0 + n, 0:F], ALU.add))
            if kind == "hidden":
                own(v.tensor_scalar(m.h[:, :, :], m.h[:, :, :], 0.0, None, ALU.max))
            if kind == "last":
                layer_norm(nc, own, s, m.x[:, :, :], m.h[:, :, :])
            v.memset(inv[:, :], 0.0).then_inc(rows_ready, 1)

        @block.tensor
        def _(pe):
            dense.pe_turn(pe, cat, 2 * F)
            dense.pe_out(pe, 2 * F, weight)

        @block.scalar
        def _(act):
            dense.act(act, 2 * F)
            if kind == "last":
                norm_root(nc, act, s, 1)

        if kind != "edges":
            @block.sync
            def _(sp):
                sp.wait_ge(rows_ready, 1)
                sp.dma_start(m.table[:, 0:F].rearrange("(w p) c -> p w c", p=P), m.h[:, :, :]).then_inc(written, 16)
                sp.wait_ge(written, 16)


def tables3(nc, m):
    with ExitStack() as stack:
        s = Scope(nc, stack, "l3tab", m.shared)
        tables = Tables(nc, s, m)
        block = stack.enter_context(nc.Block())
        tables.write(block, m.x, m.wt3, m.at3, table_score=0)


def part_edges(part):
    return part * GP * P * T, T * (min(G, GP * (part + 1)) - GP * part)


class GatherRows:

    def __init__(self, nc, s, m, part):
        self.nc, self.m = nc, m
        self.first, self.columns = part_edges(part)
        self.index = [s.sb(f"next_index{i}", [P, BATCH], I32) for i in range(2)]
        self.rows = [s.sb(f"next_rows{i}", [P, BATCH, R]) for i in range(2)]
        self.staged, self.kept, self.go = s.sem("staged"), s.sem("kept"), s.sem("go")
        self.runs_in = s.sem("runs_in")
        self.before = sum(part_edges(i)[1] // (2 * BATCH) for i in range(part))

    def sp(self, sp):
        m, n = self.m, self.columns
        for run, source in ((m.src_part, m.src), (m.dst_part, m.dst)):
            sp.dma_start(run[:, 0:n], source[self.first:self.first + P * n].rearrange("(p c) -> p c", p=P)
                         ).then_inc(self.runs_in, 16)

    def pool(self, pool):
        nc, m, n = self.nc, self.m, self.columns
        spill = m.spill[self.first:self.first + P * n, :].rearrange("(p c) r -> p c r", p=P)

        def finish(i, b):
            pool.wait_ge(m.gathered[b], 16 * BATCH * (i + self.before + 1))
            nc.gpsimd.tensor_copy(m.edge_score[:, bass.ds(BATCH * (2 * i + b), BATCH), :],
                                  self.rows[b][:, :, F:R]).then_inc(self.kept, 1)
            pool.sem_inc(self.go, 1)
            pool.dma_start(spill[:, bass.ds(BATCH * (2 * i + b), BATCH), :], self.rows[b][:, :, :]
                           ).then_inc(m.spilled[b], 16)

        def batch(i, b):
            first = isinstance(i, int) and i == 0
            if not first:
                pool.wait_ge(m.spilled[b], 16 * (i + self.before))
                pool.wait_ge(self.kept, 2 * i + b - 1)
            nc.gpsimd.tensor_copy(self.index[b][:, :],
                                  m.src_part[:, bass.ds(BATCH * (2 * i + b), BATCH)]).then_inc(self.staged, 1)
            pool.wait_ge(self.staged, 2 * i + b + 1)
            pool.sem_inc(self.go, 1)
            for t in range(BATCH):
                if t == BATCH // 2:
                    if b:
                        finish(i, 0)
                    elif not first:
                        finish(i - 1, 1)
                pool.indirect_dma_start(self.rows[b][:, t, :], None, m.table[:, :],
                                        bass.IndirectOffsetOnAxis(ap=self.index[b][:, t:t + 1], axis=0)
                                        ).then_inc(m.gathered[b], 16)

        pool.wait_ge(self.runs_in, 32)
        for b in range(2):
            batch(0, b)
        with pool.Fori(1, n // (2 * BATCH), 1) as i:
            for b in range(2):
                batch(i, b)
        finish(n // (2 * BATCH) - 1, 1)
        for b in range(2):
            pool.wait_ge(m.spilled[b], 16 * (n // (2 * BATCH) + self.before))
        pool.wait_ge(self.kept, n // BATCH)


def gather_rows3(nc, m):
    with ExitStack() as stack:
        s = Scope(nc, stack, "l3rows", m.shared)
        gather = GatherRows(nc, s, m, 0)
        block = stack.enter_context(nc.Block())

        @block.sync
        def _(sp):
            gather.sp(sp)

        @block.gpsimd
        def _(pool):
            gather.pool(pool)


def maxima3(nc, m, part):
    first_edge, C = part_edges(part)
    with ExitStack() as stack:
        s = Scope(nc, stack, f"l3max{part}", m.shared)
        key, neq, same0 = s.sb("key", [P, C]), s.sb("neq", [P, C]), s.sb("same0", [P, C])
        run = s.sb("run", [P, C, H])
        ends = s.sb("ends", [P, 4])
        edge_turn = s.sb("edge_turn", [4, 128])
        prev_last = s.sb("prev_last", [P, 1])
        cont, whole = s.sb("cont", [P, 1]), s.sb("whole", [P, 1])
        pack = s.sb("pack", [P, 4, H])
        turned = s.sb("turned", [H, 4, 128])
        carry = s.sb("carry", [H, 128])
        carry_in = s.sb("carry_in", [H, 128])
        carry_p = s.sb("carry_p", [P, H])
        last_f, low = s.sb("last_f", [P, W]), s.sb("low", [P, W])
        factor = s.sb("factor", [P, W, H])
        drop_ready, factor_ready = s.sem("drop_ready"), s.sem("factor_ready")
        cum = s.sb("cum", [P, W])
        last_i = s.sb("last_i", [P, W], I32)
        found = s.sb("found", [P, W, H])
        hole = s.sb("hole", [P, W])
        rest = s.sb("rest", [P, W, H])
        s.rest = rest[:, :, :]
        ps = s.ps("sums")
        ps2 = s.ps("before")
        ps3 = [s.ps(f"turn{i}") for i in range(4)]
        own_sem = s.sem("dve_step")
        to_pe, from_pe = s.sem("operands_ready"), s.sem("products_ready")
        run_ready, run_written, found_in, index_ready = s.sem("run_ready"), s.sem("run_written"), m.found_in, s.sem("index_ready")
        block = stack.enter_context(nc.Block())

        @block.vector
        def _(dve):
            own, v = Own(dve, own_sem), nc.vector
            v.tensor_copy(key[:, :], m.dst_part[:, 0:C]).then_inc(to_pe, 1)
            dve.wait_ge(from_pe, 1)
            if part == 0:
                own(v.tensor_tensor_scan(cum[:, :], m.ones[0:P, 0:W], ps[0:P, 0:W], 0.0, ALU.mult, ALU.add))
                own(v.tensor_tensor(cum[:, :], cum[:, :], ps[0:P, 0:W], ALU.subtract))
                own(v.tensor_tensor(m.last_edge[:, :], cum[:, :], ps2[0:P, 0:W], ALU.add))
                own(v.tensor_scalar(m.last_edge[:, :], m.last_edge[:, :], -1.0, None, ALU.add))
                own(v.tensor_tensor(rest[:, :, :], m.near[:, :, :], m.far[:, :, :], ALU.add))
                own(v.scalar_tensor_tensor(m.maximum[:, :, :], rest[:, :, :], 0.2, rest[:, :, :], ALU.mult, ALU.max))
                own(v.tensor_copy(m.loop_att[:, :, :], m.maximum[:, :, :]))
            own(v.tensor_tensor(low[:, :], m.last_edge[:, :], m.degree[:, :], ALU.subtract))
            own(v.tensor_scalar(low[:, :], low[:, :], 1.0 - first_edge, 0.0, ALU.add, ALU.max))
            own(v.tensor_scalar(last_f[:, :], m.last_edge[:, :], float(-first_edge), float(P * C - 1), ALU.add, ALU.min))
            own(v.tensor_tensor(hole[:, :], low[:, :], last_f[:, :], ALU.is_gt))
            own(v.tensor_scalar(last_f[:, :], last_f[:, :], 0.0, None, ALU.max))
            v.tensor_copy(last_i[:, :], last_f[:, :]).then_inc(index_ready, 1)
            own(v.memset(neq[:, 0:1], -FAR))
            own(v.tensor_tensor(neq[:, 1:C], key[:, 1:C], key[:, 0:C - 1], ALU.not_equal))
            own(v.tensor_scalar(neq[:, 1:C], neq[:, 1:C], -FAR, None, ALU.mult))
            for h in range(H):
                own(v.tensor_tensor_scan(run[:, :, h], neq[:, :], m.edge_score[:, 0:C, h], -FAR, ALU.add, ALU.max))
            own(v.tensor_copy(pack[:, 0, :], run[:, C - 1, :]))
            own(v.tensor_copy(pack[:, 1, :], over(key[:, 0:1], (P, H))))
            v.tensor_copy(pack[:, 2, :], over(key[:, C - 1:C], (P, H))).then_inc(to_pe, 1)
            dve.wait_ge(from_pe, 2)
            for i in range(3):
                own(v.tensor_copy(turned[:, i, 0:P], ps3[i][0:H, 0:P]))
            last, first, final = turned[:, 0, 0:P], turned[:, 1, 0:P], turned[:, 2, 0:P]
            gate = turned[:, 3, 0:P]
            own(v.memset(carry_in[:, :], -FAR))
            own(v.memset(gate, -FAR))
            own(v.tensor_tensor(turned[:, 3, 1:P], turned[:, 1, 1:P], turned[:, 2, 0:P - 1], ALU.not_equal))
            own(v.tensor_scalar(turned[:, 3, 1:P], turned[:, 3, 1:P], -FAR, None, ALU.mult))
            own(v.tensor_tensor(final, first, final, ALU.not_equal))
            own(v.scalar_tensor_tensor(final, final, -FAR, gate, ALU.mult, ALU.min))
            own(v.tensor_tensor_scan(carry[:, 0:P], final, last, -FAR, ALU.add, ALU.max))
            own(v.tensor_tensor(carry_in[:, 1:P], carry[:, 0:P - 1], turned[:, 3, 1:P], ALU.add))
            v.tensor_scalar(carry_in[:, 0:P], carry_in[:, 0:P], -FAR, None, ALU.max).then_inc(to_pe, 1)
            own(v.tensor_scalar(same0[:, :], key[:, :], key[:, 0:1], -FAR, ALU.not_equal, ALU.mult))
            dve.wait_ge(from_pe, 3)
            own(v.tensor_copy(carry_p[:, :], ps3[3][0:P, 0:H]))
            for h in range(H):
                last_op = v.scalar_tensor_tensor(run[:, :, h], same0[:, :], carry_p[:, h:h + 1], run[:, :, h],
                                                 ALU.add, ALU.max)
                if h < H - 1:
                    own(last_op)
            last_op.then_inc(run_ready, 1)
            own(v.tensor_scalar(hole[:, :], hole[:, :], -FAR, None, ALU.mult))
            for i, w in enumerate(range(0, W, BLOCK)):
                here, old, drop = (x[:, w:w + BLOCK, :] for x in (found, m.maximum, factor))
                dve.wait_ge(found_in[i], 16 * BLOCK * (part + 1))
                own(v.tensor_tensor(here, here, over(hole[:, w:w + BLOCK].unsqueeze(2), (P, BLOCK, H)), ALU.add))
                own(v.tensor_tensor(here, here, m.near[:, w:w + BLOCK, :], ALU.add))
                own(v.scalar_tensor_tensor(here, here, 0.2, here, ALU.mult, ALU.max))
                own(v.tensor_tensor(here, here, old, ALU.max))
                v.tensor_tensor(drop, old, here, ALU.subtract).then_inc(drop_ready, 1)
                if part:
                    dve.wait_ge(factor_ready, i + 1)
                    v.tensor_tensor(by_head(m.acc, w), by_head(m.acc, w), over(drop.unsqueeze(3), (P, BLOCK, H, F)), ALU.mult)
                    sums = m.acc[:, w:w + BLOCK, HF:HF + H]
                    own(v.tensor_tensor(sums, sums, drop, ALU.mult))
            dve.wait_ge(drop_ready, W // BLOCK)
            own(v.tensor_copy(m.maximum[:, :, :], found[:, :, :]))
            split3(nc, own, s, found[:, :, :], [m.near_parts[:, :, i, H:2 * H] for i in range(3)])
            if part == PARTS - 1:
                own(v.tensor_tensor(m.loop_att[:, :, :], m.loop_att[:, :, :], m.maximum[:, :, :], ALU.subtract))

        if part:
            @block.scalar
            def _(act):
                for i in range(W // BLOCK):
                    act.wait_ge(drop_ready, i + 1)
                    drop = factor[:, i * BLOCK:(i + 1) * BLOCK, :]
                    nc.scalar.activation(drop, drop, ACT.Exp).then_inc(factor_ready, 1)

        @block.tensor
        def _(pe):
            pe.wait_ge(to_pe, 1)
            nc.tensor.matmul(ps[0:P, 0:W], m.ones[0:P, 0:P], m.degree[:, :], start=True, stop=True)
            nc.tensor.matmul(ps2[0:P, 0:W], m.upto[0:P, 0:P], m.degree[:, :], start=True, stop=True).then_inc(from_pe, 1)
            pe.wait_ge(to_pe, 2)
            for i in range(3):
                last = nc.tensor.transpose(ps3[i][0:H, 0:P], pack[:, i, :], m.ident[0:P, 0:P])
            last.then_inc(from_pe, 1)
            pe.wait_ge(to_pe, 3)
            nc.tensor.transpose(ps3[3][0:P, 0:H], carry_in[:, 0:P], m.ident[0:H, 0:H]).then_inc(from_pe, 1)

        @block.sync
        def _(sp):
            sp.wait_ge(run_ready, 1)
            sp.dma_start(m.running[0:P * C, :].rearrange("(p c) h -> p c h", p=P), run[:, :, :]).then_inc(run_written, 16)

        @block.gpsimd
        def _(pool):
            pool.wait_ge(index_ready, 1)
            pool.wait_ge(run_written, 16)
            for w in range(W):
                pool.indirect_dma_start(found[:, w, :], None, m.running[:, :],
                                        bass.IndirectOffsetOnAxis(ap=last_i[:, w:w + 1], axis=0)).then_inc(found_in[w // BLOCK], 16)
            for i in range(W // BLOCK):
                pool.wait_ge(found_in[i], 16 * BLOCK * (part + 1))


def finish_layer3(nc, m, io, out):
    with ExitStack() as stack:
        s = Scope(nc, stack, "l3end", m.shared)
        norm_scratch(s)
        heads = Heads(nc, s, m)
        loop = s.sb("loop", [P, W, H])
        share = s.sb("share", [P, BLOCK, HF])
        inv = s.sb("inv", [P, W, H])
        y = s.sb("y", [P, W, F])
        x1 = s.sb("x1", [P, W, F])
        hidden = s.sb("hidden", [2 * F, W * P])
        dense1 = Dense(nc, s, m, heads.ps_t, heads.ps_o, "ffn")
        own_sem, exp_ready, ff_ready, ff_psum = s.sem("dve_step"), s.sem("exp_ready"), s.sem("ff_ready"), s.sem("ff_psum")
        ff_out, result_ready, written = s.sem("ff_out"), s.sem("result_ready"), s.sem("written")
        block = stack.enter_context(nc.Block())
        bias_att, b2, g1, c1, g2, c2 = (m.rows[:, i * F:(i + 1) * F] for i in range(3, 9))
        chunks = (W + 3) // 4

        def rowwise(ap, n=W):
            return over(ap.unsqueeze(1), (P, n, F))

        @block.vector
        def _(dve):
            own, v = Own(dve, own_sem), nc.vector
            dve.wait_ge(exp_ready, 1)
            own(v.tensor_tensor(inv[:, :, :], m.acc[:, :, HF:HF + H], loop[:, :, :], ALU.add))
            own(v.tensor_scalar(inv[:, :, :], inv[:, :, :], 1e-16, None, ALU.add))
            own(v.reciprocal(inv[:, :, :], inv[:, :, :]))
            own(v.tensor_scalar(inv[:, :, :], inv[:, :, :], 1.0 / H, None, ALU.mult))
            for w in range(0, W, BLOCK):
                here, shape = by_head(m.acc, w), (P, BLOCK, H, F)
                own(v.tensor_tensor(by_head(share, 0), over(m.h[:, w:w + BLOCK, :].unsqueeze(2), shape),
                                    over(loop[:, w:w + BLOCK, :].unsqueeze(3), shape), ALU.mult))
                own(v.tensor_tensor(here, here, by_head(share, 0), ALU.add))
                v.tensor_tensor(here, here, over(inv[:, w:w + BLOCK, :].unsqueeze(3), shape), ALU.mult).then_inc(heads.acc_ready, 1)
            dve.wait_ge(heads.out_ready, W)
            own(v.tensor_tensor(y[:, :, :], m.h[:, :, :], rowwise(bias_att), ALU.add))
            for w0, n, o in heads.banks():
                own(v.tensor_tensor(y[:, w0:w0 + n, :], y[:, w0:w0 + n, :], o, ALU.add))
            layer_norm(nc, own, s, y[:, :, :], x1[:, :, :], relu=False)
            own(v.tensor_tensor(x1[:, :, :], x1[:, :, :], rowwise(g1), ALU.mult))
            v.tensor_tensor(x1[:, :, :], x1[:, :, :], rowwise(c1), ALU.add).then_inc(dense1.ready, 1)
            dve.wait_ge(dense1.ready, 1)
            dve.wait_ge(ff_out, 1)
            own(v.tensor_tensor(y[:, :, :], x1[:, :, :], rowwise(b2), ALU.add))
            for w0, n, o in heads.banks():
                own(v.tensor_tensor(y[:, w0:w0 + n, :], y[:, w0:w0 + n, :], o, ALU.add))
            layer_norm(nc, own, s, y[:, :, :], x1[:, :, :], relu=False)
            own(v.tensor_tensor(x1[:, :, :], x1[:, :, :], rowwise(g2), ALU.mult))
            own(v.tensor_tensor(x1[:, :, :], x1[:, :, :], rowwise(c2), ALU.add))
            v.tensor_tensor(x1[:, :, :], x1[:, :, :], m.x[:, :, :], ALU.add).then_inc(result_ready, 1)

        @block.tensor
        def _(pe):
            heads.pe(pe, m.value3)
            dense1.pe_turn(pe, x1, F)
            pe.wait_ge(dense1.copied, chunks)
            for c in range(chunks):
                if c >= 2:
                    pe.wait_ge(ff_ready, c - 1)
                n = P * (min(4 * c + 4, W) - 4 * c)
                nc.tensor.matmul(heads.ps_t[c % 2][:, 0:n], m.ff1[:, :], dense1.turned_sb[0:F, 4 * c * P:4 * c * P + n],
                                 start=True, stop=True).then_inc(ff_psum, 1)
            pe.wait_ge(ff_ready, chunks)
            for w in range(W):
                last = nc.tensor.matmul(heads.ps_o[w // 8][0:P, (w % 8) * F:(w % 8 + 1) * F],
                                        hidden[:, w * P:(w + 1) * P], m.ff2[:, :], start=True, stop=True)
            last.then_inc(ff_out, 1)

        @block.scalar
        def _(act):
            nc.scalar.activation(loop[:, :, :], m.loop_att[:, :, :], ACT.Exp).then_inc(exp_ready, 1)
            heads.act(act)
            norm_root(nc, act, s, 1)
            dense1.act(act, F)
            for c in range(chunks):
                act.wait_ge(ff_psum, c + 1)
                n = P * (min(4 * c + 4, W) - 4 * c)
                nc.scalar.activation(hidden[:, 4 * c * P:4 * c * P + n], heads.ps_t[c % 2][:, 0:n], ACT.Relu,
                                     bias=m.ff1_b[:, 0:1]).then_inc(ff_ready, 1)
            norm_root(nc, act, s, 2)

        @block.sync
        def _(sp):
            sp.wait_ge(result_ready, 1)
            sp.dma_start(out.rearrange("(w p) f -> p w f", p=P), x1[:, :, :]).then_inc(written, 16)
            sp.wait_ge(written, 16)


class Memory:
    pass


def program(nc, io, out):
    m = Memory()
    with ExitStack() as stack:
        def sb(name, shape, dt=F32):
            return stack.enter_context(nc.sbuf_tensor(name, shape, dt))

        m.x, m.h = sb("x", [P, W, F]), sb("h", [P, W, F])
        m.h_turned = sb("h_turned", [F, N])
        m.src_run, m.dst_run = sb("src_run", [P, C], I32), sb("dst_run", [P, C], I32)
        m.last_key = sb("last_key", [100, 2], I32)
        m.wt0, m.at0, m.merge = sb("wt0", [F, HF]), sb("at0", [F, 2 * H]), sb("merge", [F, H, F])
        m.wt3, m.at3, m.value3 = sb("wt3", [F, HF]), sb("at3", [F, 2 * H]), sb("value3", [2 * F, 4, F])
        m.sage1, m.sage2, m.edge_w = (sb(n, [2 * F, F]) for n in ("sage1", "sage2", "edge_w"))
        m.ff1, m.ff1_b, m.ff2 = sb("ff1", [F, 2 * F]), sb("ff1_b", [2 * F, 1]), sb("ff2", [2 * F, F])
        m.rows = sb("rows", [P, 9 * F])
        m.ident, m.ones, m.upto = (sb(n, [128, 128]) for n in ("ident", "ones", "upto"))
        m.node_iota, m.step_iota = sb("node_iota", [P, P]), sb("step_iota", [128, KV])
        m.code_iota = sb("code_iota", [P, CW], F16)
        m.group_iota, m.edge_iota = sb("group_iota", [100, 2]), sb("edge_iota", [100, 2])
        for name in ("by_dst", "by_src"):
            t = Memory()
            t.group_f, t.window_f, t.first_node = (sb(f"{name}_{n}", [128, K]) for n in ("group_f", "window_f", "first"))
            t.group, t.window = sb(f"{name}_group", [1, K], I32), sb(f"{name}_window", [1, K + 2 * PAD], I32)
            if name == "by_dst":
                m.by_dst = t
            else:
                m.by_src = t
        m.fine = Memory()
        m.fine.group_f, m.fine.window_f, m.fine.first, m.fine.same = (
            sb(f"fine_{n}", [128, KV]) for n in ("group_f", "window_f", "first", "same"))
        m.fine.group, m.fine.place = sb("fine_group", [1, KV], I32), sb("fine_place", [1, KV + TRAIL], I32)
        m.near, m.far = sb("near", [P, W, H]), sb("far", [P, W, H])
        m.near_parts = sb("near_parts", [P, W, 3, 2 * H], BF16)
        m.degree, m.loop_att = sb("degree", [P, W]), sb("loop_att", [P, W, H])
        m.src, m.dst = io["src"], io["dst"]
        m.records = nc.dram_tensor("records", (E, 2), I32, kind="Internal").ap()
        m.codes = nc.dram_tensor("codes", (E, 2), F32, kind="Internal").ap()
        m.counts = nc.dram_tensor("counts", (V + SLOTS, P, CW), F32, kind="Internal").ap()
        m.table = nc.dram_tensor("table", (N, R), F32, kind="Internal").ap()
        m.spill = nc.dram_tensor("spill", (E, R), F32, kind="Internal").ap()
        m.running = nc.dram_tensor("running", (P * CP, H), F32, kind="Internal").ap()

        m.sems, m.shared = StepSems(nc, stack), SharedSems(nc, stack, 48)
        set_up(nc, m, io)
        with ExitStack() as early:
            m.place = early.enter_context(nc.sbuf_tensor("place", [P, C], I32))
            m.record = early.enter_context(nc.sbuf_tensor("record", [P, C, 2], I32))
            order_edges(nc, m)
            scatter_and_tables(nc, m)
        with ExitStack() as rest:
            m.acc = rest.enter_context(nc.sbuf_tensor("acc", [P, W, HF + H], F32))
            attend(nc, m, "l0", m.by_src, from_spill=False)
            finish_layer0(nc, m)
            count_sum(nc, m, "l1a")
            finish_mean(nc, m, "l1a_end", m.sage1[:, :], m.rows[:, 0:F], "hidden")
            count_sum(nc, m, "l1b")
            finish_mean(nc, m, "l1b_end", m.sage2[:, :], m.rows[:, F:2 * F], "last")
            gather_sum(nc, m, "l2", F, io["edge_attr"])
            finish_mean(nc, m, "l2_end", m.edge_w[:, :], m.rows[:, 2 * F:3 * F], "edges")
            tables3(nc, m)
            with ExitStack() as scores:
                def part_sb(name, shape, dt=F32):
                    return scores.enter_context(nc.sbuf_tensor(name, shape, dt))
                m.edge_score = part_sb("edge_score", [P, CP, H])
                m.src_part, m.dst_part = part_sb("src_part", [P, CP], I32), part_sb("dst_part", [P, CP], I32)
                m.last_edge, m.maximum = part_sb("last_edge", [P, W]), part_sb("maximum", [P, W, H])
                m.gathered = [scores.enter_context(nc.semaphore(f"l3_gathered{i}")) for i in range(2)]
                m.spilled = [scores.enter_context(nc.semaphore(f"l3_spilled{i}")) for i in range(2)]
                m.found_in = [scores.enter_context(nc.semaphore(f"l3_found_in{i}")) for i in range(W // BLOCK)]
                gather_rows3(nc, m)
                for part in range(PARTS):
                    maxima3(nc, m, part)
                    attend(nc, m, f"l3_{part}", m.by_dst, from_spill=True, part=part)
            finish_layer3(nc, m, io, out)


def kernel(**inputs):
    import numpy as np
    import concourse.bacc as bacc
    from concourse.bass_utils import run_bass_kernel_spmd

    a = {k: np.asarray(v) for k, v in inputs.items()}
    a0, w0 = a["L0_gnn_a"], a["L0_gnn_W"]
    w3 = a["L3_gnn_W_att"]
    arrays = {
        "x": a["x"], "src": a["src"], "dst": a["dst"], "edge_attr": a["edge_attr_64"],
        "wt0": w0.transpose(2, 0, 1).reshape(F, HF),
        "at0": np.concatenate([a0[:, :F, 0].T, a0[:, F:, 0].T], axis=1),
        "merge": a["L0_gnn_merge_kernel"].reshape(H, F, F).transpose(1, 0, 2),
        "wt3": w3.reshape(F, H, F).transpose(2, 1, 0).reshape(F, HF),
        "at3": np.concatenate([a["L3_gnn_att_src"].T, a["L3_gnn_att_dst"].T], axis=1),
        "value3": w3.reshape(F, 4, 2, F).transpose(2, 0, 1, 3).reshape(2 * F, 4, F),
        "sage1": np.concatenate([a["L1_gnn_w1_l"], a["L1_gnn_w1_r"]]),
        "sage2": np.concatenate([a["L1_gnn_w2_l"], a["L1_gnn_w2_r"]]),
        "edge_w": np.concatenate([a["L2_gnn_W"].T[F:], a["L2_gnn_W"].T[:F]]),
        "ff1": a["L3_gnn_W1"], "ff1_b": a["L3_gnn_b1"].reshape(2 * F, 1), "ff2": a["L3_gnn_W2"],
        "rows": np.stack([a[n] for n in (
            "L1_gnn_b1", "L1_gnn_b2", "L2_gnn_b", "L3_gnn_bias_att", "L3_gnn_b2",
            "L3_gnn_ln1_g", "L3_gnn_ln1_b", "L3_gnn_ln2_g", "L3_gnn_ln2_b")]),
    }
    nc = bacc.Bacc("TRN2", target_bir_lowering=False, num_devices=1)
    io = {}
    for name, value in arrays.items():
        arrays[name] = np.ascontiguousarray(value)
        io[name] = nc.dram_tensor(name + "_in", value.shape, mybir.dt.from_np(value.dtype), kind="ExternalInput").ap()
    out = nc.dram_tensor("out", (N, F), F32, kind="ExternalOutput").ap()
    program(nc, io, out)
    r = run_bass_kernel_spmd(nc, [{k + "_in": v for k, v in arrays.items()}], core_ids=[0])
    return r.results[0]["out"]
```
